# Optimizing a Trainium2 kernel written in Bass

```python
import numpy as np
import jax
import jax.numpy as jnp

def _softmax(x, axis=-1):
    return jax.nn.softmax(x, axis=axis)

def _gelu(x):
    return jax.nn.gelu(x, approximate=True)

def _silu(x):
    return jax.nn.silu(x)

def _sigmoid(x):
    return jax.nn.sigmoid(x)

def _layernorm(x, axis=-1, eps=1e-05):
    m = jnp.mean(x, axis=axis, keepdims=True)
    v = jnp.var(x, axis=axis, keepdims=True)
    return (x - m) / jnp.sqrt(v + eps)

def _scatter_add(tgt, idx, src, axis=0):
    return tgt.at[idx].add(src)

def _segment_sum(src, seg, n):
    return jax.ops.segment_sum(src, seg, n)
kernel_name = 'mk_hybrid_d1_jaxref_r8_d46229'

def setup_inputs(seed: int=0):
    np.random.seed(seed)
    _w = jnp.asarray

    def _L0_attn_a_setup():
        import jax, jax.numpy as jnp
        import numpy as np
        D = 128
        H = 16
        HD = 64
        AHD = H * HD
        B = 4
        S = 128
        EPS = 1e-05
        SMAX = float(D) ** 0.5

        def _ln(x, s, b):
            mu = jnp.mean(x, axis=-1, keepdims=True)
            var = jnp.mean(jnp.square(x - mu), axis=-1, keepdims=True)
            return (x - mu) * jax.lax.rsqrt(var + EPS) * s + b

        def _forward(x, lnq_s, lnq_b, Wq, bq, lnk_s, lnk_b, Wk, bk, lnv_s, lnv_b, Wv, bv, Wo, bo, lnm_s, lnm_b, W1, b1, W2, b2):
            Bq, Sq, _ = x.shape
            q = (_ln(x, lnq_s, lnq_b) @ Wq + bq).reshape(Bq, Sq, H, HD).transpose(0, 2, 1, 3)
            k = (_ln(x, lnk_s, lnk_b) @ Wk + bk).reshape(Bq, Sq, H, HD).transpose(0, 2, 1, 3)
            v = (_ln(x, lnv_s, lnv_b) @ Wv + bv).reshape(Bq, Sq, H, HD).transpose(0, 2, 1, 3)
            scores = jnp.einsum('bhqd,bhkd->bhqk', q, k) / SMAX
            mask = jnp.triu(jnp.full((Sq, Sq), -999.0, dtype=scores.dtype), k=Sq - 1)
            p = jax.nn.softmax(scores + mask, axis=-1)
            att = jnp.einsum('bhqk,bhkd->bhqd', p, v).transpose(0, 2, 1, 3).reshape(Bq, Sq, AHD)
            h = att @ Wo + bo + x
            y = _ln(h, lnm_s, lnm_b)
            m = jax.nn.gelu(y @ W1 + b1) @ W2 + b2
            return m + h
        key = jax.random.key(seed)
        ks = jax.random.split(key, 7)

        def lin(k, fan_in, fan_out):
            lim = 1.0 / np.sqrt(fan_in)
            kw, kb = jax.random.split(k)
            W = jax.random.uniform(kw, (fan_in, fan_out), minval=-lim, maxval=lim, dtype=jnp.float32)
            b = jax.random.uniform(kb, (fan_out,), minval=-lim, maxval=lim, dtype=jnp.float32)
            return (W, b)
        Wq, bq = lin(ks[0], D, AHD)
        Wk, bk = lin(ks[1], D, AHD)
        Wv, bv = lin(ks[2], D, AHD)
        Wo, bo = lin(ks[3], AHD, D)
        W1, b1 = lin(ks[4], D, 2 * D)
        W2, b2 = lin(ks[5], 2 * D, D)
        x = jax.random.normal(ks[6], (B, S, D), dtype=jnp.float32)
        ones = jnp.ones((D,), jnp.float32)
        zeros = jnp.zeros((D,), jnp.float32)
        return {'x': x, 'lnq_s': ones, 'lnq_b': zeros, 'Wq': Wq, 'bq': bq, 'lnk_s': ones, 'lnk_b': zeros, 'Wk': Wk, 'bk': bk, 'lnv_s': ones, 'lnv_b': zeros, 'Wv': Wv, 'bv': bv, 'Wo': Wo, 'bo': bo, 'lnm_s': ones, 'lnm_b': zeros, 'W1': W1, 'b1': b1, 'W2': W2, 'b2': b2}
    _L0_attn_a_in = _L0_attn_a_setup()

    def _L0_attn_b_setup():
        import jax, jax.numpy as jnp
        import numpy as np
        B, T, D = (4, 256, 128)
        H, Dh = (16, 64)
        key = jax.random.key(seed)
        ks = jax.random.split(key, 5)
        std_qkv = float(np.sqrt(2.0 / (Dh * D)))
        std_o = float(np.sqrt(2.0 / (D * Dh)))
        return {'x': jax.random.normal(ks[0], (B, T, D), dtype=jnp.float32), 'W_Q': jax.random.normal(ks[1], (H, Dh, D), dtype=jnp.float32) * std_qkv, 'b_Q': jnp.zeros((H, Dh), dtype=jnp.float32), 'W_K': jax.random.normal(ks[2], (H, Dh, D), dtype=jnp.float32) * std_qkv, 'b_K': jnp.zeros((H, Dh), dtype=jnp.float32), 'W_V': jax.random.normal(ks[3], (H, Dh, D), dtype=jnp.float32) * std_qkv, 'b_V': jnp.zeros((H, Dh), dtype=jnp.float32), 'W_O': jax.random.normal(ks[4], (H, D, Dh), dtype=jnp.float32) * std_o, 'b_O': jnp.zeros((D,), dtype=jnp.float32)}
    _L0_attn_b_in = _L0_attn_b_setup()

    def _L0_ffn_setup():
        import jax, jax.numpy as jnp
        import numpy as np
        B, S, DIM = (4, 256, 128)
        E, K, HID = (8, 2, 512)
        key = jax.random.key(seed)
        ks = jax.random.split(key, 8)
        init = lambda k, sh: jax.random.normal(k, sh, jnp.float32) * 0.02
        return {'x': jax.random.normal(ks[0], (B, S, DIM), jnp.float32), 'gate_w': init(ks[1], (DIM, E)), 'gate_b': jnp.zeros((E,), jnp.float32), 'w1': init(ks[2], (E, DIM, HID)), 'b1': jnp.zeros((E, HID), jnp.float32), 'w2': init(ks[3], (E, HID, DIM)), 'b2': jnp.zeros((E, DIM), jnp.float32), 'ws1': init(ks[4], (DIM, HID)), 'bs1': jnp.zeros((HID,), jnp.float32), 'ws2': init(ks[5], (HID, DIM)), 'bs2': jnp.zeros((DIM,), jnp.float32)}
    _L0_ffn_in = _L0_ffn_setup()
    _d = {'L0_attn_a_x': _L0_attn_a_in['x'], 'L0_attn_a_lnq_s': _L0_attn_a_in['lnq_s'], 'L0_attn_a_lnq_b': _L0_attn_a_in['lnq_b'], 'L0_attn_a_Wq': _L0_attn_a_in['Wq'], 'L0_attn_a_bq': _L0_attn_a_in['bq'], 'L0_attn_a_lnk_s': _L0_attn_a_in['lnk_s'], 'L0_attn_a_lnk_b': _L0_attn_a_in['lnk_b'], 'L0_attn_a_Wk': _L0_attn_a_in['Wk'], 'L0_attn_a_bk': _L0_attn_a_in['bk'], 'L0_attn_a_lnv_s': _L0_attn_a_in['lnv_s'], 'L0_attn_a_lnv_b': _L0_attn_a_in['lnv_b'], 'L0_attn_a_Wv': _L0_attn_a_in['Wv'], 'L0_attn_a_bv': _L0_attn_a_in['bv'], 'L0_attn_a_Wo': _L0_attn_a_in['Wo'], 'L0_attn_a_bo': _L0_attn_a_in['bo'], 'L0_attn_a_lnm_s': _L0_attn_a_in['lnm_s'], 'L0_attn_a_lnm_b': _L0_attn_a_in['lnm_b'], 'L0_attn_a_W1': _L0_attn_a_in['W1'], 'L0_attn_a_b1': _L0_attn_a_in['b1'], 'L0_attn_a_W2': _L0_attn_a_in['W2'], 'L0_attn_a_b2': _L0_attn_a_in['b2'], 'L0_attn_b_W_Q': _L0_attn_b_in['W_Q'], 'L0_attn_b_b_Q': _L0_attn_b_in['b_Q'], 'L0_attn_b_W_K': _L0_attn_b_in['W_K'], 'L0_attn_b_b_K': _L0_attn_b_in['b_K'], 'L0_attn_b_W_V': _L0_attn_b_in['W_V'], 'L0_attn_b_b_V': _L0_attn_b_in['b_V'], 'L0_attn_b_W_O': _L0_attn_b_in['W_O'], 'L0_attn_b_b_O': _L0_attn_b_in['b_O'], 'L0_ffn_gate_w': _L0_ffn_in['gate_w'], 'L0_ffn_gate_b': _L0_ffn_in['gate_b'], 'L0_ffn_w1': _L0_ffn_in['w1'], 'L0_ffn_b1': _L0_ffn_in['b1'], 'L0_ffn_w2': _L0_ffn_in['w2'], 'L0_ffn_b2': _L0_ffn_in['b2'], 'L0_ffn_ws1': _L0_ffn_in['ws1'], 'L0_ffn_bs1': _L0_ffn_in['bs1'], 'L0_ffn_ws2': _L0_ffn_in['ws2'], 'L0_ffn_bs2': _L0_ffn_in['bs2']}
    _x0 = _d['L0_attn_a_x']
    _d['L0_attn_a_x'] = jax.random.normal(jax.random.fold_in(jax.random.key(seed), 1), (2, 1024, 128), dtype=_x0.dtype)
    del _x0
    return _d

def reference(L0_attn_a_x, L0_attn_a_lnq_s, L0_attn_a_lnq_b, L0_attn_a_Wq, L0_attn_a_bq, L0_attn_a_lnk_s, L0_attn_a_lnk_b, L0_attn_a_Wk, L0_attn_a_bk, L0_attn_a_lnv_s, L0_attn_a_lnv_b, L0_attn_a_Wv, L0_attn_a_bv, L0_attn_a_Wo, L0_attn_a_bo, L0_attn_a_lnm_s, L0_attn_a_lnm_b, L0_attn_a_W1, L0_attn_a_b1, L0_attn_a_W2, L0_attn_a_b2, L0_attn_b_W_Q, L0_attn_b_b_Q, L0_attn_b_W_K, L0_attn_b_b_K, L0_attn_b_W_V, L0_attn_b_b_V, L0_attn_b_W_O, L0_attn_b_b_O, L0_ffn_gate_w, L0_ffn_gate_b, L0_ffn_w1, L0_ffn_b1, L0_ffn_w2, L0_ffn_b2, L0_ffn_ws1, L0_ffn_bs1, L0_ffn_ws2, L0_ffn_bs2):

    def _L0_attn_a_ref(x, lnq_s, lnq_b, Wq, bq, lnk_s, lnk_b, Wk, bk, lnv_s, lnv_b, Wv, bv, Wo, bo, lnm_s, lnm_b, W1, b1, W2, b2):
        import jax, jax.numpy as jnp
        import numpy as np
        D = 128
        H = 16
        HD = 64
        AHD = H * HD
        B = 4
        S = 128
        EPS = 1e-05
        SMAX = float(D) ** 0.5

        def _ln(x, s, b):
            mu = jnp.mean(x, axis=-1, keepdims=True)
            var = jnp.mean(jnp.square(x - mu), axis=-1, keepdims=True)
            return (x - mu) * jax.lax.rsqrt(var + EPS) * s + b

        def _forward(x, lnq_s, lnq_b, Wq, bq, lnk_s, lnk_b, Wk, bk, lnv_s, lnv_b, Wv, bv, Wo, bo, lnm_s, lnm_b, W1, b1, W2, b2):
            Bq, Sq, _ = x.shape
            q = (_ln(x, lnq_s, lnq_b) @ Wq + bq).reshape(Bq, Sq, H, HD).transpose(0, 2, 1, 3)
            k = (_ln(x, lnk_s, lnk_b) @ Wk + bk).reshape(Bq, Sq, H, HD).transpose(0, 2, 1, 3)
            v = (_ln(x, lnv_s, lnv_b) @ Wv + bv).reshape(Bq, Sq, H, HD).transpose(0, 2, 1, 3)
            scores = jnp.einsum('bhqd,bhkd->bhqk', q, k) / SMAX
            mask = jnp.triu(jnp.full((Sq, Sq), -999.0, dtype=scores.dtype), k=Sq - 1)
            p = jax.nn.softmax(scores + mask, axis=-1)
            att = jnp.einsum('bhqk,bhkd->bhqd', p, v).transpose(0, 2, 1, 3).reshape(Bq, Sq, AHD)
            h = att @ Wo + bo + x
            y = _ln(h, lnm_s, lnm_b)
            m = jax.nn.gelu(y @ W1 + b1) @ W2 + b2
            return m + h
        return _forward(x, lnq_s, lnq_b, Wq, bq, lnk_s, lnk_b, Wk, bk, lnv_s, lnv_b, Wv, bv, Wo, bo, lnm_s, lnm_b, W1, b1, W2, b2)

    def _L0_attn_b_ref(x, W_Q, b_Q, W_K, b_K, W_V, b_V, W_O, b_O):
        import jax, jax.numpy as jnp
        import numpy as np
        B, T, D = (4, 256, 128)
        H, Dh = (16, 64)
        Q = jnp.einsum('btd,hkd->bthk', x, W_Q) + b_Q
        K = jnp.einsum('btd,hkd->bthk', x, W_K) + b_K
        V = jnp.einsum('btd,hkd->bthk', x, W_V) + b_V
        d_head = W_Q.shape[1]
        scores = jnp.einsum('bqhk,bshk->bhqs', Q, K) / jnp.sqrt(jnp.asarray(d_head, x.dtype))
        attn = jax.nn.softmax(scores, axis=-1)
        out_h = jnp.einsum('bhqs,bshk->bqhk', attn, V)
        return jnp.einsum('bqhk,hdk->bqd', out_h, W_O) + b_O

    def _L0_ffn_ref(x, gate_w, gate_b, w1, b1, w2, b2, ws1, bs1, ws2, bs2):
        import jax, jax.numpy as jnp
        import numpy as np
        B, S, DIM = (4, 256, 128)
        E, K, HID = (8, 2, 512)
        orig_shape = x.shape
        xf = x.reshape(-1, DIM)
        logits = xf @ gate_w + gate_b
        top_w, top_i = jax.lax.top_k(logits, K)
        gw = jax.nn.softmax(top_w, axis=-1).astype(xf.dtype)
        combine = (gw[:, :, None] * jax.nn.one_hot(top_i, E, dtype=xf.dtype)).sum(axis=1)
        out = jnp.zeros_like(xf)
        for e in range(E):
            h = jax.nn.gelu(xf @ w1[e] + b1[e], approximate=False)
            out = out + combine[:, e:e + 1] * (h @ w2[e] + b2[e])
        shared = jax.nn.gelu(xf @ ws1 + bs1, approximate=False) @ ws2 + bs2
        return (out + shared).reshape(orig_shape)
    x = L0_attn_a_x
    x = x + _L0_attn_a_ref(_layernorm(x, axis=-1), L0_attn_a_lnq_s, L0_attn_a_lnq_b, L0_attn_a_Wq, L0_attn_a_bq, L0_attn_a_lnk_s, L0_attn_a_lnk_b, L0_attn_a_Wk, L0_attn_a_bk, L0_attn_a_lnv_s, L0_attn_a_lnv_b, L0_attn_a_Wv, L0_attn_a_bv, L0_attn_a_Wo, L0_attn_a_bo, L0_attn_a_lnm_s, L0_attn_a_lnm_b, L0_attn_a_W1, L0_attn_a_b1, L0_attn_a_W2, L0_attn_a_b2)
    x = x + _L0_ffn_ref(_layernorm(x, axis=-1), L0_ffn_gate_w, L0_ffn_gate_b, L0_ffn_w1, L0_ffn_b1, L0_ffn_w2, L0_ffn_b2, L0_ffn_ws1, L0_ffn_bs1, L0_ffn_ws2, L0_ffn_bs2)
    x = x + _L0_attn_b_ref(_layernorm(x, axis=-1), L0_attn_b_W_Q, L0_attn_b_b_Q, L0_attn_b_W_K, L0_attn_b_b_K, L0_attn_b_W_V, L0_attn_b_b_V, L0_attn_b_W_O, L0_attn_b_b_O)
    x = x + _L0_ffn_ref(_layernorm(x, axis=-1), L0_ffn_gate_w, L0_ffn_gate_b, L0_ffn_w1, L0_ffn_b1, L0_ffn_w2, L0_ffn_b2, L0_ffn_ws1, L0_ffn_bs1, L0_ffn_ws2, L0_ffn_bs2)
    return x

_drawn_inputs = setup_inputs


def setup_inputs(seed=0):
    import zlib

    import numpy as np

    out = dict(_drawn_inputs(seed))
    spreads = {'L0_attn_a_lnq_s': (1.0, 0.6),
     'L0_attn_a_lnq_b': (0.0, 0.8),
     'L0_attn_a_lnk_s': (1.0, 0.6),
     'L0_attn_a_lnk_b': (0.0, 0.8),
     'L0_attn_a_lnv_s': (1.0, 0.6),
     'L0_attn_a_lnv_b': (0.0, 0.498),
     'L0_attn_a_lnm_s': (1.0, 0.6),
     'L0_attn_a_lnm_b': (0.0, 0.646),
     'L0_attn_b_b_Q': (0.0, 0.8),
     'L0_attn_b_b_K': (0.0, 0.8),
     'L0_attn_b_b_V': (0.0, 0.299),
     'L0_attn_b_b_O': (0.0, 0.1),
     'L0_ffn_gate_b': (0.0, 0.1),
     'L0_ffn_b1': (0.0, 0.477),
     'L0_ffn_b2': (0.0, 0.1),
     'L0_ffn_bs1': (0.0, 0.361),
     'L0_ffn_bs2': (0.0, 0.1)}
    factors = {'L0_attn_a_Wq': 8.0,
     'L0_attn_a_bq': 8.0,
     'L0_attn_a_Wk': 8.0,
     'L0_attn_a_bk': 8.0,
     'L0_attn_a_Wv': 3.158,
     'L0_attn_a_bv': 3.048,
     'L0_attn_a_bo': 5.11,
     'L0_attn_a_b1': 5.677,
     'L0_attn_a_b2': 2.918,
     'L0_attn_b_W_Q': 8.0,
     'L0_attn_b_W_K': 8.0,
     'L0_attn_b_W_V': 8.0}
    for name, (base, spread) in spreads.items():
        noise = np.random.default_rng([zlib.crc32(name.encode()), seed]).standard_normal(out[name].shape)
        drawn = base * np.exp(spread * noise) if base else spread * noise
        out[name] = jnp.asarray(drawn.astype(out[name].dtype))
    for name, factor in factors.items():
        out[name] = (out[name] * factor).astype(out[name].dtype)
    return out
```

```python
from contextlib import ExitStack

import concourse.bass as bass
from concourse import mybir

F32 = mybir.dt.float32
F16 = mybir.dt.float16
U32 = mybir.dt.uint32
ALU = mybir.AluOpType
ACT = mybir.ActivationFunctionType
AX = mybir.AxisListType

P = 128
B, S, D = 2, 1024, 128
TOK = B * S
NT = TOK // P
NG = TOK // 512
H, HD = 16, 64
PAIRS = H // 2
NIT = PAIRS * B
KT = S // P
NC = S // 512
U = NC * KT
E, HID = 8, 512
NE = E + 1
HT = HID // P
WS = 64.0
EPS = 1e-5
MASK = -999.0
SCALE_A = float(D) ** -0.5
SCALE_B = float(HD) ** -0.5
QB, KB, KA, QA = range(4)
QH, KL, KH, QL = range(4)

M_AT = {4: 1, 5: 1, 6: 1, 7: 2, 8: 1, 9: 2, 10: 1, 11: 1, 12: 2, 13: 1, 14: 2, 15: 1}
NM = KT * 2


def extras(u, first, last):
    out = []
    if u == 0 and not last:
        out.append(("Q", 0))
    if u == 1 and not last:
        out.append(("K", 0))
    if u == 2:
        if not first:
            out.append(("L", 1))
        if not last:
            out.append(("V", 0))
    if u == 3:
        out.append(("T", 1))
    if u == 5 and not first:
        out.append(("Y", 1))
    if u == 10:
        out.append(("L", 0))
    if u == 13:
        out.append(("Y", 0))
    if not last:
        done = sum(n for v, n in M_AT.items() if v < u)
        out += [("M", done + i) for i in range(M_AT.get(u, 0))]
        if u == 12:
            out.append(("T", 0))
    return out


PROLOGUE = [("Q", 0), ("K", 0), ("V", 0)] + [("M", i) for i in range(12)] + [("T", 0)] + [("M", i) for i in range(12, NM)]


def ring_of(first, last):
    return [x for u in range(U) for x in extras(u, first, last) if x[0] != "L"]


PRO = len(PROLOGUE)
R0 = len(ring_of(True, False))
R1 = len(ring_of(False, False))


def at(n, value):
    return isinstance(n, int) and n == value


def ring_base(n, first):
    return PRO if first else n * R1 + (PRO + R0 - R1)


def build(nc, t, out):
    with ExitStack() as ctx:
        def sb(name, shape, dt):
            return ctx.enter_context(nc.sbuf_tensor(name, shape, dt))

        def sem(name):
            return ctx.enter_context(nc.semaphore(name))

        ps = ctx.enter_context(nc.psum_tensor("ps", [P, 8, 512], F32))

        x = sb("x", [P, NT, D], F32)
        xn = sb("xn", [P, NT, D], F32)
        xs = [sb(f"xs{v}", [P, 2, TOK], F16) for v in range(3)]
        xT32 = xs[1][:].rearrange("p a n -> p (a n)").bitcast(F32)
        wh = sb("wh", [P, 3, H * HD], F16)
        wl = sb("wl", [P, 3, H * HD], F16)
        wo = sb("wo", [P, PAIRS, D], F32)
        bqk = sb("bqk", [P, 2, PAIRS], F32)
        bv = sb("bv", [P, H * HD], F32)
        bo = sb("bo", [P, D], F32)
        w1h = sb("w1h", [P, NE, HID], F16)
        w1l = sb("w1l", [P, NE, HID], F16)
        w2h = sb("w2h", [P, NE, HT * D], F16)
        w2l = sb("w2l", [P, NE, HT * D], F16)
        stage = sb("stage", [P, 3, 2 * HID], F32)
        fb1 = sb("fb1", [P, NE, HT], F32)
        fb2 = sb("fb2", [NE, D], F32)
        gw = sb("gw", [P, E], F32)
        gb = sb("gb", [1, E], F32)
        ln_sb = sb("ln_sb", [P, 4, 2], F32)
        mw1 = sb("mw1", [P, 2 * D], F32)
        mw2 = sb("mw2", [P, 2, D], F32)
        mb1 = sb("mb1", [P, 2], F32)
        mb2 = sb("mb2", [P, D], F32)
        ident = sb("ident", [P, P], F32)
        ident16 = sb("ident16", [P, P], F16)
        ones = sb("ones", [P, P], F32)
        mrows = sb("mrows", [1, 2, P], F32)
        iota = sb("iota", [P, E], F32)
        pair = sb("pair", [P, 4, S], F16)
        heads = [sb(f"heads{b}", [P, 2, 4, S], F16) for b in range(2)]
        vb = [sb(f"vb{b}", [P, KT, P], F32) for b in range(2)]
        pt = sb("pt", [P, 4, 2, 512], F32)
        acc = sb("acc", [P, NC, 2, 512], F32)
        f = sb("f", [P, 2, S], F32)
        ou = sb("ou", [P, NC, 512], F32)
        rec = sb("rec", [P, 512], F32)
        att = sb("att", [P, NC, 512], F32)
        mxp = sb("mxp", [P, KT, 2, 2], F32)
        mtmp = sb("mtmp", [P, NC, 4, 2], F32)
        mneg = sb("mneg", [P, NC, 2, 4], F16)
        mrow = sb("mrow", [8, NC, P], F16)
        spare = sb("spare", [P, 4], F32)
        now_b1 = sb("now_b1", [P, HT], F32)
        st = sb("st", [P, NT, 6], F32)
        mv = sb("mv", [P, NT, 2], F32)
        var = sb("var", [P, NT], F32)
        std = sb("std", [P, NT], F32)
        rstd = sb("rstd", [P, NT], F32)
        ix8 = sb("ix8", [P, NT, 8], U32)
        ixf = sb("ixf", [P, NT, 2], F32)
        gd = sb("gd", [P, NT], F32)
        ge = sb("ge", [P, NT], F32)
        gden = sb("gden", [P, NT], F32)
        g1 = sb("g1", [P, NT], F32)
        g2 = sb("g2", [P, NT], F32)

        att_flat = att[:].rearrange("p c n -> p (c n)")

        def gate_buffer(at, *shape):
            size = shape[0] * shape[1] * (shape[2] if len(shape) > 2 else 1)
            names = "abc"[:len(shape)]
            return att_flat[:, at:at + size].rearrange(f"p ({' '.join(names)}) -> p {' '.join(names)}",
                                                       **dict(zip(names, shape)))

        lg = gate_buffer(0, NT, E)
        mx8 = gate_buffer(NT * E, NT, 8)
        eq = gate_buffer(2 * NT * E, 2, NT, E)
        comb = gate_buffer(4 * NT * E, NE, NT)
        combs = gate_buffer(4 * NT * E + NE * NT, NE, NT)
        pt_flat = pt[:].rearrange("p a b n -> p (a b n)")
        tmp_tok = pt_flat[:, 0:NT * D].rearrange("p (t d) -> p t d", t=NT)
        combT = pt_flat[0:NE, 0:TOK]
        h1T = pt_flat.rearrange("p (i n) -> p i n", i=2)
        h32 = pt_flat.rearrange("p (r n) -> p r n", r=8)
        hsplit = [heads[b][:].rearrange("p a b n -> p (a b n)")[:, 0:2 * HT * 512]
                  .rearrange("p (s i n) -> p s i n", s=2, i=HT) for b in range(2)]

        loads = {}

        def load_sem(name):
            loads[name] = sem("ld_" + name)
            return loads[name]

        for name in ("x", "const", "ln", "wa", "woa", "mlp", "ffn", "gate", "wb", "wob"):
            load_sem(name)
        staged = [sem(f"staged{i}") for i in range(3)]
        w_hi = sem("w_hi")
        w_64 = sem("w_64")
        w_lo = sem("w_lo")
        stored = sem("stored")
        const_ready = sem("const_ready")
        rows_ready = sem("rows_ready")

        class Norm:
            STATS, AGGR, EPSD, RECIP = NT, 2 * NT, 2 * NT + 1, 2 * NT + 2
            DONE = 3 * NT + 2

            def __init__(self, name, src, dst, before):
                self.src, self.dst, self.before = src, dst, before
                self.v = sem(name + "_norm_dve")
                self.a = sem(name + "_norm_sqrt")

            def tile_done(self, i):
                return self.RECIP + 1 + i

            def dve(self, e):
                for s, v in self.before:
                    e.wait_ge(s, v)
                for i in range(NT):
                    nc.vector.bn_stats(st[:, i, :], self.src[:, i, :]).then_inc(self.v, 1)
                e.wait_ge(self.v, self.STATS)
                for i in range(NT):
                    nc.vector.bn_aggr(mv[:, i, :], st[:, i, :]).then_inc(self.v, 1)
                e.wait_ge(self.v, self.AGGR)
                nc.vector.tensor_scalar(var[:], mv[:, :, 1], EPS, None, ALU.add).then_inc(self.v, 1)
                e.wait_ge(self.a, 1)
                nc.vector.reciprocal(rstd[:], std[:]).then_inc(self.v, 1)
                e.wait_ge(self.v, self.RECIP)
                for i in range(NT):
                    nc.vector.tensor_scalar(self.dst[:, i, :], self.src[:, i, :], mv[:, i, 0:1], rstd[:, i:i + 1],
                                            ALU.subtract, ALU.mult).then_inc(self.v, 1)

            def act(self, e):
                e.wait_ge(self.v, self.EPSD)
                nc.scalar.activation(std[:], var[:], ACT.Sqrt).then_inc(self.a, 1)

        class Turn:

            def __init__(self, name, norm, variants):
                self.norm, self.variants = norm, variants
                self.n = len(variants)
                self.full = sem(name + "_turned")
                self.f32 = sem(name + "_affine")
                self.hi = sem(name + "_high")
                self.lo = sem(name + "_low")
                self.split = any(v[3] is not None for v in variants)

            def done(self):
                return (self.lo, NG * self.n) if self.split else (self.f32, NG * self.n)

            def out32(self, g, v):
                if self.variants[v][2] is not None:
                    return self.variants[v][2][:, 512 * g:512 * g + 512]
                q = (g * self.n + v) % 4
                return f[:, q // 2, 512 * (q % 2):512 * (q % 2) + 512]

            def pe(self, e):
                for g in range(NG):
                    for i in range(4):
                        e.wait_ge(self.norm.v, self.norm.tile_done(4 * g + i))
                        last = nc.tensor.transpose(ps[:, g, P * i:P * i + P], self.norm.dst[:, 4 * g + i, :], ident[:])
                    last.then_inc(self.full, 1)

            def act(self, e):
                for g in range(NG):
                    e.wait_ge(self.full, g + 1)
                    for v, (scale, offset, out32, split) in enumerate(self.variants):
                        q = g * self.n + v
                        if out32 is None and q >= 4:
                            e.wait_ge(self.lo, q - 3)
                        nc.scalar.activation(self.out32(g, v), ps[:, g, :], ACT.Identity,
                                             bias=offset, scale=scale).then_inc(self.f32, 1)

            def dve(self, e):
                if not self.split:
                    return
                for g in range(NG):
                    for v, (_, _, _, split) in enumerate(self.variants):
                        q = g * self.n + v
                        hi, lo = (split[:, k, 512 * g:512 * g + 512] for k in range(2))
                        e.wait_ge(self.f32, q + 1)
                        nc.vector.tensor_copy(hi, self.out32(g, v)).then_inc(self.hi, 1)
                        e.wait_ge(self.hi, q + 1)
                        nc.vector.tensor_tensor(lo, self.out32(g, v), hi, ALU.subtract).then_inc(self.lo, 1)

        class Attention:

            def __init__(self, name, scale, masked, xq, xk, xv, y, turn, w_sem, wo_sem):
                self.scale, self.masked, self.x3, self.y, self.turn = scale, masked, (xq, xk, xv), y, turn
                self.w_sem, self.wo_sem = w_sem, wo_sem

                def s(what):
                    return sem(f"{name}_{what}")

                self.wsplit_hi = s("w_high")
                self.wsplit_lo = s("w_low")
                self.y_init = s("y_init")
                self.ring_full = s("ring_full")
                self.f_ready = s("f_ready")
                self.hi_ready = s("hi_ready")
                self.lo_ready = s("lo_ready")
                self.v_ready = s("v_ready")
                self.max_ready = s("max_ready")
                self.mtmp_ready = s("mtmp_ready")
                self.mneg_ready = s("mneg_ready")
                self.mrow_ready = s("mrow_ready")
                self.assembled = s("assembled")
                self.max_rows = [s(f"max_rows{c}") for c in range(NC)]
                self.scores = s("scores")
                self.probs = s("probs")
                self.pv = s("pv")
                self.summed = s("summed")
                self.o_copied = s("o_copied")
                self.sums = s("sums")
                self.rec_ready = s("rec_ready")
                self.att_ready = s("att_ready")
                self.y_added = s("y_added")

            def freed(self, use, n):
                kind, i = use
                if kind == "Q" or kind == "K":
                    return self.f_ready, 2 * (n + 1) + (1 if kind == "Q" else 2)
                if kind == "V":
                    return self.v_ready, n + 2
                if kind == "M":
                    return self.max_ready, NM * (n + 1) + i + 1
                if kind == "T":
                    return self.mrow_ready, (2 * (n + 1) + 1 if i == 0 else 2 * n + 2)
                if kind == "Y":
                    return self.y_added, (2 * n + 1 if i == 0 else 2 * n)
                raise ValueError(kind)

            def slot(self, number, parity):
                k = 2 * ((number + parity) % 2)
                return ps[:, k:k + 2, :]

            def pe(self, e):
                e.wait_ge(self.turn.done()[0], self.turn.done()[1])
                e.wait_ge(self.wsplit_lo, 3)
                uses = PROLOGUE
                for k, use in enumerate(uses):
                    if k >= 2:
                        e.wait_ge(*self.freed(uses[k - 2], -1))
                    self.pe_use(e, use, -1, 0, 1, k)
                self.pe_iteration(e, 0, 0, 0, True, False)
                with e.Fori(0, NIT // 2 - 1) as j:
                    self.pe_iteration(e, 2 * j + 1, j, 1, False, False)
                    self.pe_iteration(e, 2 * j + 2, j + 1, 0, False, False)
                self.pe_iteration(e, NIT - 1, PAIRS - 1, 1, False, True)
                self.pe_pv(e, NIT - 1, 1, U - 1)
                self.pe_sums(e, NIT, 1)
                self.pe_y(e, NIT, 1, ps[:, 0:2, :], PAIRS - 1)

            def pe_iteration(self, e, n, p, b, first, last):
                uses = ring_of(first, last)
                before = PROLOGUE if first else ring_of(at(n, 1), False)
                chain = [(x, n - 1 if not first else -1) for x in before[-2:]] + [(x, n) for x in uses]
                k = 0
                for u in range(U):
                    c, kt = divmod(u, KT)
                    if u == 0:
                        e.wait_ge(self.assembled, 96 * (n + 1))
                        e.wait_ge(self.max_rows[0], 32 * (n + 1))
                    if kt == 0 and c == 1:
                        e.wait_ge(self.max_rows[1], 32 * (n + 1))
                    for h in range(2):
                        if not (first and u == 0):
                            e.wait_ge(self.probs, 2 * U * n + 2 * u + h - 1)
                        self.pe_scores(e, b, h, c, kt)
                    for use in extras(u, first, last):
                        if use[0] == "L":
                            self.pe_sums(e, n, use[1])
                            continue
                        e.wait_ge(*self.freed(*chain[k]))
                        self.pe_use(e, use, n, p, b, k)
                        k += 1
                    if u > 0:
                        self.pe_pv(e, n, b, u - 1)
                    elif not first:
                        self.pe_pv(e, n - 1, 1 - b, U - 1)

            def pe_use(self, e, use, n, p, b, k):
                kind, i = use
                slot = self.ring_slot(n, b, k)
                p1, b1 = p + b if not at(n, -1) else 0, 1 - b
                if kind in "QK":
                    self.pe_qk(e, "QK".index(kind), p1, b1, slot)
                elif kind == "V":
                    self.pe_v(e, p1, b1, slot)
                elif kind == "M":
                    e.wait_ge(self.hi_ready, 2 * (n + 1) + 2)
                    self.pe_m(i, slot)
                elif kind == "T":
                    e.wait_ge(self.mneg_ready, 2 * (n + 1) + 1 if i == 0 else 2 * n + 2)
                    nc.tensor.transpose(slot[0:8, 0, 0:64].bitcast(F16),
                                        mneg[:, i].rearrange("p h t -> p (h t)"), ident16[:]).then_inc(self.ring_full, 1)
                elif kind == "Y":
                    self.pe_y(e, n, i, slot, p if i == 0 else p + b - 1)

            def ring_slot(self, n, b, k):
                if at(n, -1):
                    return self.slot(k, 0)
                if at(n, 0):
                    return self.slot(PRO + k, 0)
                return self.slot(PRO + R0 - R1 + k, b * R1)

            def pe_qk(self, e, which, p, b, slot):
                hi, lo = (w[:, which, bass.ds(p * P, P)] for w in (wh, wl))
                xt = self.x3[which]
                for c in range(NC):
                    cols = slice(b * S + 512 * c, b * S + 512 * c + 512)
                    nc.tensor.matmul(slot[:, c, :], hi, xt[:, 0, cols], start=True, stop=False)
                    nc.tensor.matmul(slot[:, c, :], hi, xt[:, 1, cols], start=False, stop=False)
                    last = nc.tensor.matmul(slot[:, c, :], lo, xt[:, 0, cols], start=False, stop=True)
                last.then_inc(self.ring_full, 1)

            def pe_v(self, e, p, b, slot):
                hi, lo = (w[:, 2, bass.ds(p * P, P)] for w in (wh, wl))
                for i in range(KT):
                    cols = slice(b * S + P * i, b * S + P * i + P)
                    o = slot[:, i // 4, P * (i % 4):P * (i % 4) + P]
                    nc.tensor.matmul(o, self.x3[2][:, 0, cols], hi, start=True, stop=False)
                    nc.tensor.matmul(o, self.x3[2][:, 0, cols], lo, start=False, stop=False)
                    last = nc.tensor.matmul(o, self.x3[2][:, 1, cols], hi, start=False, stop=True)
                last.then_inc(self.ring_full, 1)

            def pe_m(self, item, slot):
                i, half = divmod(item, 2)
                masked = self.masked and i == 0 and half == 1
                for h in range(2):
                    r = slice(HD * h, HD * h + HD)
                    last = nc.tensor.matmul(slot[:, h, :], pair[r, QH, P * i:P * i + P], pair[r, KH, 512 * half:512 * half + 512],
                                            start=True, stop=True)
                if masked:
                    for h in range(2):
                        last = nc.tensor.matmul(slot[:, h, 511:512], mrows[0:1, 0, :], ones[0:1, 0:1], start=False, stop=True,
                                                skip_group_check=True)
                last.then_inc(self.ring_full, 1)

            def pe_scores(self, e, b, h, c, kt):
                hb = heads[b]
                keys, queries = slice(P * kt, P * kt + P), slice(512 * c, 512 * c + 512)
                o = ps[:, 4 + h, :]
                masked = self.masked and c == 0 and kt == KT - 1
                nc.tensor.matmul(o, hb[:, h, KA, keys], hb[:, h, QA, queries], start=True, stop=False)
                last = nc.tensor.matmul(o, hb[0:HD + 1, h, KB, keys], hb[0:HD + 1, h, QB, queries],
                                        start=False, stop=True)
                if masked:
                    last = nc.tensor.matmul(o[:, 0:1], mrows[0:1, 1, :], ones[0:1, 0:1], start=False, stop=True,
                                            skip_group_check=True)
                last.then_inc(self.scores, 1)

            def pe_pv(self, e, n, b, u):
                c, kt = divmod(u, KT)
                e.wait_ge(self.probs, 2 * U * n + 2 * u + 2)
                if u == 0:
                    e.wait_ge(self.v_ready, n + 1)
                if kt == 0 and not (at(n, 0) and c == 0):
                    e.wait_ge(self.o_copied, 2 * n + c)
                for h in range(2):
                    last = nc.tensor.matmul(ps[HD * h:HD * h + HD, 6, :], vb[b][:, kt, HD * h:HD * h + HD], pt[:, u % 4, h, :],
                                            start=(kt == 0), stop=(kt == KT - 1), skip_group_check=True)
                last.then_inc(self.pv, 1)

            def pe_sums(self, e, n, i):
                chunk = 2 * n if i == 0 else 2 * n - 1
                e.wait_ge(self.summed, 7 * chunk + 7)
                if not (at(n, 0) and i == 0):
                    e.wait_ge(self.rec_ready, chunk)
                for h in range(2):
                    last = nc.tensor.matmul(ps[HD * h:HD * h + HD, 7, :], ones[:, 0:HD], acc[:, i, h, :],
                                            start=True, stop=True, skip_group_check=True)
                last.then_inc(self.sums, 1)

            def pe_y(self, e, n, i, slot, p):
                e.wait_ge(self.att_ready, 2 * n + 1 if i == 0 else 2 * n)
                for k in range(4):
                    last = nc.tensor.matmul(slot[:, 0, P * k:P * k + P], att[:, i, P * k:P * k + P],
                                            wo[:, p, :] if isinstance(p, int) else wo[:, bass.ds(p, 1), :].rearrange("p a n -> p (a n)"),
                                            start=True, stop=True)
                last.then_inc(self.ring_full, 1)

            def act_prologue(self, e):
                for k, use in enumerate(PROLOGUE):
                    self.act_use(e, use, -1, 0, 1, k, k)

            def act(self, e):
                self.act_iteration(e, 0, 0, 0, True, False)
                with e.Fori(0, NIT // 2 - 1) as j:
                    self.act_iteration(e, 2 * j + 1, j, 1, False, False)
                    self.act_iteration(e, 2 * j + 2, j + 1, 0, False, False)
                self.act_iteration(e, NIT - 1, PAIRS - 1, 1, False, True)
                self.act_copy_o(e, NIT - 1, 1)

            def act_iteration(self, e, n, p, b, first, last):
                k, base = 0, ring_base(n, first)
                for u in range(U):
                    self.act_exp(e, n, u, first)
                    for use in extras(u, first, last):
                        if use[0] != "L":
                            self.act_use(e, use, n, p, b, k, base + k)
                            k += 1
                    if u == 0 and not first:
                        self.act_copy_o(e, n - 1, 1)
                    if u == KT:
                        self.act_copy_o(e, n, 0)

            def act_exp(self, e, n, u, first):
                if not (first and u < 4):
                    e.wait_ge(self.pv, U * n + u - 3)
                    if u >= 4:
                        c, kt = divmod(u - 4, KT)
                        e.wait_ge(self.summed, 14 * n + 7 * c + max(kt, 1))
                    else:
                        e.wait_ge(self.summed, 14 * n - 14 + 7 + U // 2 - 4 + u)
                for h in range(2):
                    e.wait_ge(self.scores, 2 * U * n + 2 * u + h + 1)
                    nc.scalar.activation(pt[:, u % 4, h, :], ps[:, 4 + h, :], ACT.Exp,
                                         scale=self.scale).then_inc(self.probs, 1)

            def act_use(self, e, use, n, p, b, k, number):
                kind, _ = use
                if kind not in "QK":
                    return
                slot = self.ring_slot(n, b, k)
                which = "QK".index(kind)
                p1 = p + b if not at(n, -1) else 0
                e.wait_ge(self.ring_full, number + 1)
                if not at(n, -1):
                    e.wait_ge(self.lo_ready, 2 * n + which + 1)
                if not isinstance(p1, int):
                    nc.scalar.copy(spare[:, 1 + which:2 + which], spare[:, 0:1])
                offset = bqk[:, which, p1:p1 + 1] if isinstance(p1, int) else bqk[:, which, bass.ds(p1, 1)]
                nc.scalar.activation(f[:, which, :].rearrange("p (a n) -> p a n", a=2), slot, ACT.Identity,
                                     bias=offset, scale=1.0 / WS).then_inc(self.f_ready, 1)

            def act_copy_o(self, e, n, c):
                e.wait_ge(self.pv, U * n + KT * c + KT)
                if c == 1:
                    e.wait_ge(self.att_ready, 2 * n + 1)
                elif not at(n, 0):
                    e.wait_ge(self.att_ready, 2 * n - 1)
                nc.scalar.activation(ou[:, c, :], ps[:, 6, :], ACT.Copy).then_inc(self.o_copied, 1)

            def dve_weights(self, e):
                e.wait_ge(self.w_sem, 16 * 5)
                for i in range(3):
                    raw = self.raw_weights(i)
                    nc.vector.tensor_scalar(wh[:, i, :], raw, WS, None, ALU.mult).then_inc(self.wsplit_hi, 1)
                    e.wait_ge(self.wsplit_hi, i + 1)
                    nc.vector.scalar_tensor_tensor(out=wl[:, i, :], in0=raw, scalar=WS, in1=wh[:, i, :],
                                                   op0=ALU.mult, op1=ALU.subtract).then_inc(self.wsplit_lo, 1)

            def dve(self, e):
                e.wait_ge(self.wo_sem, 32)
                e.wait_ge(self.turn.norm.v, Norm.DONE)
                y = self.y
                nc.vector.tensor_tensor(y[:], y[:], bo[:].rearrange("p (a n) -> p a n", a=1).broadcast_to([P, NT, D]),
                                        ALU.add).then_inc(self.y_init, 1)
                for k, use in enumerate(PROLOGUE):
                    self.dve_use(e, use, -1, 0, 1, k, k)
                self.dve_iteration(e, 0, 0, 0, True, False)
                with e.Fori(0, NIT // 2 - 1) as j:
                    self.dve_iteration(e, 2 * j + 1, j, 1, False, False)
                    self.dve_iteration(e, 2 * j + 2, j + 1, 0, False, False)
                self.dve_iteration(e, NIT - 1, PAIRS - 1, 1, False, True)
                self.dve_normalise(e, NIT, 1)
                self.dve_add_y(e, NIT, 1, 1, ps[:, 0:2, :], NIT * R1 + (PRO + R0 - R1) - self.ahead + 1)

            ahead = R1 - len(ring_of(False, True))

            def raw_weights(self, i):
                return (f[:, 0, :], f[:, 1, :], acc[:, 0].rearrange("p h n -> p (h n)"))[i]

            def dve_iteration(self, e, n, p, b, first, last):
                k, base = 0, ring_base(n, first)
                for u in range(U):
                    for use in extras(u, first, last):
                        if use[0] == "L":
                            self.dve_normalise(e, n, use[1])
                            continue
                        self.dve_use(e, use, n, p, b, k, base + k)
                        k += 1

            def dve_use(self, e, use, n, p, b, k, number):
                kind, i = use
                slot = self.ring_slot(n, b, k)
                if kind in "QK":
                    which = "QK".index(kind)
                    done = 2 * (n + 1) + which + 1
                    hi, lo = (pair[:, s, :] for s in ((QH, QL), (KH, KL))[which])
                    e.wait_ge(self.f_ready, done)
                    if not at(n, -1):
                        e.wait_ge(self.assembled, 96 * (n + 1))
                    nc.vector.tensor_copy(hi, f[:, which, :]).then_inc(self.hi_ready, 1)
                    e.wait_ge(self.hi_ready, done)
                    nc.vector.tensor_tensor(lo, f[:, which, :], hi, ALU.subtract).then_inc(self.lo_ready, 1)
                    return
                e.wait_ge(self.ring_full, number + 1)
                if kind == "V":
                    b1, p1 = 1 - b, (p + b if not at(n, -1) else 0)
                    if not at(n, -1) and not at(n, 0):
                        e.wait_ge(self.pv, U * n)
                    offset = bv[:, p1 * P:p1 * P + P] if isinstance(p1, int) else bv[:, bass.ds(p1 * P, P)]
                    nc.vector.scalar_tensor_tensor(
                        out=vb[b1][:], in0=slot.rearrange("p a (t n) -> p (a t) n", n=P), scalar=1.0 / WS,
                        in1=offset.rearrange("p (a n) -> p a n", a=1).broadcast_to([P, KT, P]),
                        op0=ALU.mult, op1=ALU.add).then_inc(self.v_ready, 1)
                elif kind == "M":
                    t_, half = divmod(i, 2)
                    nc.vector.tensor_reduce(mxp[:, t_, :, half], slot, AX.X, ALU.max).then_inc(self.max_ready, 1)
                    if t_ % 4 == 3 and half == 1:
                        c = t_ // 4
                        e.wait_ge(self.max_ready, NM * (n + 1) + i + 1)
                        nc.vector.tensor_tensor(mtmp[:, c], mxp[:, 4 * c:4 * c + 4, :, 0], mxp[:, 4 * c:4 * c + 4, :, 1],
                                                ALU.max).then_inc(self.mtmp_ready, 1)
                        e.wait_ge(self.mtmp_ready, 2 * (n + 1) + c + 1)
                        nc.vector.tensor_scalar(mneg[:, c].rearrange("p h t -> p t h"), mtmp[:, c], -1.0, None,
                                                ALU.mult).then_inc(self.mneg_ready, 1)
                elif kind == "T":
                    m = n + 1 if i == 0 else n
                    if not (at(m, 0)):
                        e.wait_ge(self.max_rows[i], 32 * m)
                    nc.vector.tensor_copy(mrow[:, i, :], slot[0:8, 0, 0:64].bitcast(F16)).then_inc(self.mrow_ready, 1)
                elif kind == "Y":
                    self.dve_add_y(e, n, i, b if i == 0 else 1 - b, slot, None)

            def dve_normalise(self, e, n, i):
                chunk = 2 * n if i == 0 else 2 * n - 1
                e.wait_ge(self.sums, chunk + 1)
                if not (at(n, 0) and i == 0):
                    e.wait_ge(self.att_ready, chunk)
                nc.vector.reciprocal(rec[:], ps[:, 7, :]).then_inc(self.rec_ready, 1)
                e.wait_ge(self.rec_ready, chunk + 1)
                e.wait_ge(self.o_copied, chunk + 1)
                nc.vector.tensor_tensor(att[:, i, :], ou[:, i, :], rec[:], ALU.mult).then_inc(self.att_ready, 1)

            def dve_add_y(self, e, n, i, b, slot, full):
                if full is not None:
                    e.wait_ge(self.ring_full, full)
                done = 2 * n if i == 0 else 2 * n - 1
                if at(n, 0) and i == 0:
                    e.wait_ge(self.y_init, 1)
                else:
                    e.wait_ge(self.y_added, done)
                first = b * KT + 4 * i
                ys = self.y[:, first:first + 4, :]
                nc.vector.tensor_tensor(ys, ys, slot[:, 0, :].rearrange("p (t n) -> p t n", t=4), ALU.add)\
                    .then_inc(self.y_added, 1)

            Y_DONE = 2 * NIT

            def pool(self, e):
                self.pool_iteration(e, 0)
                with e.Fori(1, NIT) as n:
                    self.pool_iteration(e, n)

            def pool_iteration(self, e, n):
                for c in range(NC):
                    if at(n, 0):
                        e.wait_ge(self.wsplit_lo, 3)
                    else:
                        e.wait_ge(self.sums, 2 * (n - 1) + c + 1)
                    for kt in range(1, KT):
                        u = KT * c + kt
                        e.wait_ge(self.probs, 2 * U * n + 2 * u + 2)
                        one = pt[:, (u - 1) % 4] if kt == 1 else acc[:, c]
                        if kt > 1:
                            e.wait_ge(self.summed, 14 * n + 7 * c + kt - 1)
                        nc.gpsimd.tensor_tensor(acc[:, c], one, pt[:, u % 4], ALU.add).then_inc(self.summed, 1)

            def sp(self, e):
                self.sp_assemble(e, 0, 0)
                self.sp_rows(e, 0, 0, 0)
                self.sp_rows(e, 0, 0, 1)
                self.sp_assemble(e, 1, 1)
                self.sp_rows(e, 1, 1, 0)
                self.sp_rows(e, 1, 1, 1)
                with e.Fori(1, NIT // 2) as j:
                    for b in range(B):
                        m = 2 * j + b
                        self.sp_assemble(e, m, b)
                        self.sp_rows(e, m, b, 0)
                        self.sp_rows(e, m, b, 1)

            def sp_assemble(self, e, m, b):
                e.wait_ge(self.lo_ready, 2 * m + 2)
                for h in range(2):
                    r = slice(HD * h, HD * h + HD)
                    for dst, src in ((heads[b][0:HD, h, QB:KA + 1, :], pair[r, QH:KH + 1, :]),
                                     (heads[b][HD:P, h, KA:QA + 1, :], pair[r, KH:QL + 1, :]),
                                     (heads[b][0:HD, h, QA, :], pair[r, QH, :])):
                        e.dma_start(dst, src).then_inc(self.assembled, 16)

            def sp_rows(self, e, m, b, c):
                e.wait_ge(self.mrow_ready, 2 * m + c + 1)
                for h in range(2):
                    e.dma_start(heads[b][HD:HD + 1, h, QB, 512 * c:512 * c + 512],
                                mrow[4 * h:4 * h + 4, c, :]).then_inc(self.max_rows[c], 16)

        class Mlp:

            def __init__(self, turn):
                self.turn = turn
                self.up = sem("mlp_up")
                self.gelu = sem("mlp_gelu")
                self.down = sem("mlp_down")
                self.x_ready = sem("mlp_x_ready")

            def pe(self, e):
                e.wait_ge(loads["mlp"], 16 * 4)
                for g in range(NG):
                    e.wait_ge(self.turn.f32, g + 1)
                    for i in range(2):
                        k = 2 * g + i
                        if k >= 4:
                            e.wait_ge(self.gelu, k - 3)
                        elif k == 0:
                            e.wait_ge(self.turn.f32, NG)
                        nc.tensor.matmul(ps[:, k % 4, :], mw1[:, P * i:P * i + P], xT32[:, 512 * g:512 * g + 512],
                                         start=True, stop=True).then_inc(self.up, 1)
                for g in range(NG):
                    e.wait_ge(self.gelu, 2 * g + 2)
                    for k in range(4):
                        for i in range(2):
                            last = nc.tensor.matmul(ps[:, 4 + g, P * k:P * k + P], h1T[:, i, 512 * g + P * k:512 * g + P * k + P],
                                                    mw2[:, i, :], start=(i == 0), stop=(i == 1))
                    last.then_inc(self.down, 1)

            def act(self, e):
                for g in range(NG):
                    for i in range(2):
                        k = 2 * g + i
                        e.wait_ge(self.up, k + 1)
                        nc.scalar.activation(h1T[:, i, 512 * g:512 * g + 512], ps[:, k % 4, :], ACT.Gelu_apprx_tanh,
                                             bias=mb1[:, i:i + 1]).then_inc(self.gelu, 1)

            def dve(self, e):
                e.wait_ge(loads["mlp"], 16 * 4)
                nc.vector.tensor_tensor(x[:], x[:], xn[:], ALU.add).then_inc(self.x_ready, 1)
                e.wait_ge(self.x_ready, 1)
                nc.vector.tensor_tensor(x[:], x[:], mb2[:].rearrange("p (a n) -> p a n", a=1).broadcast_to([P, NT, D]),
                                        ALU.add).then_inc(self.x_ready, 1)
                e.wait_ge(self.x_ready, 2)
                for g in range(NG):
                    e.wait_ge(self.down, g + 1)
                    xg = x[:, 4 * g:4 * g + 4, :]
                    nc.vector.tensor_tensor(xg, xg, ps[:, 4 + g, :].rearrange("p (t n) -> p t n", t=4), ALU.add)\
                        .then_inc(self.x_ready, 1)

            X_DONE = 2 + NG

        class Moe:

            def __init__(self, name, turn):
                self.turn = turn

                def s(what):
                    return sem(f"{name}_{what}")

                self.logits = s("logits")
                self.gate = s("gate_dve")
                self.gexp = s("gate_exp")
                self.b1_ready = s("b1_ready")
                self.up = s("up")
                self.gelu = s("gelu")
                self.hi = s("high")
                self.lo = s("low")
                self.down = s("down")
                self.combined = s("combined")
                self.ct = s("combine_turned")
                self.ct_sb = s("combine_copied")
                self.bias = s("bias")
                self.x_ready = s("x_ready")

            NK = NE * NG
            G_LG, G_MAX = 1, 1 + NT
            G_IDX = 1 + 2 * NT
            G_D = G_IDX + 2
            G_END = G_D + 10

            def pe(self, e):
                done = self.turn.done()
                e.wait_ge(done[0], done[1])
                e.wait_ge(loads["gate"], 16 * 2)
                e.wait_ge(w_lo, NE)
                for i in range(NT):
                    o = ps[:, 6, E * i:E * i + E]
                    nc.tensor.matmul(o, xT32[:, P * i:P * i + P], gw[:], start=True, stop=False)
                    last = nc.tensor.matmul(o, ones[0:1, :], gb[:], start=False, stop=True)
                last.then_inc(self.logits, 1)
                self.pe_up(e, 0, 0, True)
                self.pe_expert(e, 0)
                with e.Fori(1, NE - 1) as ex:
                    self.pe_expert(e, ex)
                for c in range(NG):
                    if c < 3:
                        self.pe_up(e, NE - 1, c + 1, False)
                    self.pe_down(e, NE - 1, c)
                for g in range(NG):
                    for k in range(4):
                        last = nc.tensor.matmul(ps[0:NE, g, P * k:P * k + P], comb[:, :, 4 * g + k], ident[:], start=True, stop=True)
                    last.then_inc(self.ct, 1)
                for g in range(NG):
                    e.wait_ge(self.ct_sb, g + 1)
                    if g < 2:
                        e.wait_ge(self.combined, 4 * (self.NK - 1 + g))
                    for k in range(4):
                        c0 = 512 * g + P * k
                        last = nc.tensor.matmul(ps[:, 4 + g, P * k:P * k + P], combT[:, c0:c0 + P], fb2[:],
                                                start=True, stop=True)
                    last.then_inc(self.bias, 1)

            def pe_expert(self, e, ex):
                for c in range(NG):
                    self.pe_up(e, ex if c < NG - 1 else ex + 1, (c + 1) % NG, False)
                    self.pe_down(e, ex, c)

            def pe_up(self, e, ex, c, start):
                for i in range(HT):
                    if not start:
                        e.wait_ge(self.gelu, 16 * ex + 4 * c + i - 3)
                    if isinstance(ex, int):
                        hi, lo = (w[:, ex, P * i:P * i + P] for w in (w1h, w1l))
                    else:
                        hi, lo = (w[:].rearrange("p e n -> p (e n)")[:, bass.ds(ex * HID + P * i, P)] for w in (w1h, w1l))
                    cols = slice(512 * c, 512 * c + 512)
                    nc.tensor.matmul(ps[:, i, :], hi, xs[0][:, 0, cols], start=True, stop=False)
                    nc.tensor.matmul(ps[:, i, :], hi, xs[0][:, 1, cols], start=False, stop=False)
                    nc.tensor.matmul(ps[:, i, :], lo, xs[0][:, 0, cols], start=False, stop=True).then_inc(self.up, 1)

            def pe_down(self, e, ex, c):
                k = 4 * ex + c
                if not (at(ex, 0) and c < 2):
                    e.wait_ge(self.combined, 4 * k - 4)
                e.wait_ge(self.lo, 4 * k + 4)
                hs = hsplit[c % 2]
                for i in range(4):
                    o = ps[:, 4 + c % 2, P * i:P * i + P]
                    cols = slice(P * i, P * i + P)
                    for q in range(HT):
                        if isinstance(ex, int):
                            hi, lo = (w[:, ex, P * q:P * q + P] for w in (w2h, w2l))
                        else:
                            hi, lo = (w[:].rearrange("p e n -> p (e n)")[:, bass.ds(ex * HID + P * q, P)] for w in (w2h, w2l))
                        nc.tensor.matmul(o, hs[:, 0, q, cols], hi, start=(q == 0), stop=False)
                        nc.tensor.matmul(o, hs[:, 0, q, cols], lo, start=False, stop=False)
                        last = nc.tensor.matmul(o, hs[:, 1, q, cols], hi, start=False, stop=(q == HT - 1))
                last.then_inc(self.down, 1)

            def act(self, e):
                e.wait_ge(self.gate, self.G_D)
                nc.scalar.activation(ge[:], gd[:], ACT.Exp).then_inc(self.gexp, 1)
                self.act_expert(e, 0)
                with e.Fori(1, NE) as ex:
                    self.act_expert(e, ex)
                for g in range(NG):
                    e.wait_ge(self.ct, g + 1)
                    nc.scalar.activation(combT[:, 512 * g:512 * g + 512], ps[0:NE, g, :], ACT.Copy).then_inc(self.ct_sb, 1)

            def act_expert(self, e, ex):
                if at(ex, 0):
                    nc.scalar.copy(now_b1[:], fb1[:, 0, :]).then_inc(self.b1_ready, 1)
                else:
                    e.wait_ge(self.gelu, 16 * ex)
                    nc.scalar.copy(spare[:, 3:4], spare[:, 0:1])
                    nc.scalar.copy(now_b1[:], fb1[:].rearrange("p e n -> p (e n)")[:, bass.ds(ex * HT, HT)])\
                        .then_inc(self.b1_ready, 1)
                e.wait_ge(self.b1_ready, ex + 1)
                for c in range(NG):
                    for i in range(HT):
                        k = 4 * c + i
                        if not (at(ex, 0) and k < 8):
                            e.wait_ge(self.lo, 16 * ex + k - 7)
                        e.wait_ge(self.up, 16 * ex + k + 1)
                        offset = now_b1[:, i:i + 1]
                        nc.scalar.activation(h32[:, k % 8, :], ps[:, i, :], ACT.Gelu, bias=offset, scale=1.0 / WS)\
                            .then_inc(self.gelu, 1)

            def dve(self, e):
                self.dve_gate(e)
                self.dve_split(e, 0, 0, True)
                self.dve_expert(e, 0)
                with e.Fori(1, NE - 1) as ex:
                    self.dve_expert(e, ex)
                for c in range(NG):
                    if c < 3:
                        self.dve_split(e, NE - 1, c + 1, False)
                    self.dve_combine(e, NE - 1, c)
                e.wait_ge(self.combined, 4 * self.NK)
                for g in range(NG):
                    e.wait_ge(self.bias, g + 1)
                    xg = x[:, 4 * g:4 * g + 4, :]
                    nc.vector.tensor_tensor(xg, xg, ps[:, 4 + g, :].rearrange("p (t n) -> p t n", t=4), ALU.add)\
                        .then_inc(self.x_ready, 1)

            X_DONE = NG

            def dve_gate(self, e):
                g = self.gate
                e.wait_ge(self.logits, 1)
                nc.vector.tensor_copy(lg[:], ps[:, 6, 0:NT * E].rearrange("p (t e) -> p t e", t=NT)).then_inc(g, 1)
                e.wait_ge(g, self.G_LG)
                for i in range(NT):
                    nc.vector.max(mx8[:, i, :], lg[:, i, :]).then_inc(g, 1)
                e.wait_ge(g, self.G_MAX)
                for i in range(NT):
                    nc.vector.max_index(ix8[:, i, :], mx8[:, i, :], lg[:, i, :]).then_inc(g, 1)
                e.wait_ge(g, self.G_IDX)
                nc.vector.tensor_copy(ixf[:], ix8[:, :, 0:2]).then_inc(g, 1)
                nc.vector.tensor_tensor(gd[:], mx8[:, :, 1], mx8[:, :, 0], ALU.subtract).then_inc(g, 1)
                e.wait_ge(self.gexp, 1)
                n = self.G_D
                nc.vector.tensor_scalar(gden[:], ge[:], 1.0, None, ALU.add).then_inc(g, 1)
                e.wait_ge(g, n + 1)
                nc.vector.reciprocal(g1[:], gden[:]).then_inc(g, 1)
                e.wait_ge(g, n + 2)
                nc.vector.tensor_tensor(g2[:], ge[:], g1[:], ALU.mult).then_inc(g, 1)
                e.wait_ge(g, n + 3)
                io = iota[:].rearrange("p (a e) -> p a e", a=1).broadcast_to([P, NT, E])
                for k in range(2):
                    nc.vector.tensor_tensor(eq[:, k], io, ixf[:, :, k:k + 1].broadcast_to([P, NT, E]), ALU.is_equal).then_inc(g, 1)
                e.wait_ge(g, n + 5)
                for k, w in enumerate((g1, g2)):
                    nc.vector.tensor_tensor(eq[:, k], eq[:, k], w[:].rearrange("p (t a) -> p t a", a=1).broadcast_to([P, NT, E]),
                                            ALU.mult).then_inc(g, 1)
                e.wait_ge(g, n + 7)
                nc.vector.tensor_tensor(comb[:, 0:E, :].rearrange("p e t -> p t e"), eq[:, 0], eq[:, 1], ALU.add).then_inc(g, 1)
                nc.vector.memset(comb[:, E, :], 1.0).then_inc(g, 1)
                e.wait_ge(g, n + 9)
                nc.vector.tensor_scalar(combs[:], comb[:], 1.0 / WS, None, ALU.mult).then_inc(g, 1)
                e.wait_ge(g, self.G_END)

            def dve_expert(self, e, ex):
                for c in range(NG):
                    self.dve_split(e, ex if c < NG - 1 else ex + 1, (c + 1) % NG, False)
                    self.dve_combine(e, ex, c)

            def dve_split(self, e, ex, c, start):
                hs = hsplit[c % 2]
                if not (start or (at(ex, 0) and c < 2)):
                    e.wait_ge(self.down, 4 * ex + c - 1)
                for i in range(HT):
                    n = 16 * ex + 4 * c + i + 1
                    src = h32[:, (4 * c + i) % 8, :]
                    e.wait_ge(self.gelu, n)
                    nc.vector.tensor_copy(hs[:, 0, i, :], src).then_inc(self.hi, 1)
                    e.wait_ge(self.hi, n)
                    nc.vector.tensor_tensor(hs[:, 1, i, :], src, hs[:, 0, i, :], ALU.subtract).then_inc(self.lo, 1)

            def dve_combine(self, e, ex, c):
                k = 4 * ex + c
                e.wait_ge(self.down, k + 1)
                if not (at(ex, 0)):
                    e.wait_ge(self.combined, 4 * (k - 3))
                for i in range(4):
                    tile = 4 * c + i
                    w = combs[:, ex, tile:tile + 1] if isinstance(ex, int) else \
                        combs[:].rearrange("p e t -> p (e t)")[:, bass.ds(ex * NT + tile, 1)]
                    nc.vector.scalar_tensor_tensor(out=x[:, tile, :], in0=ps[:, 4 + c % 2, P * i:P * i + P], scalar=w,
                                                   in1=x[:, tile, :], op0=ALU.mult, op1=ALU.add).then_inc(self.combined, 1)

        one_zero = (1.0, 0.0)
        norm_a1 = Norm("a1", x, xn, [(loads["x"], 16)])
        norm_a2 = Norm("a2", xn, tmp_tok, [(norm_a1.v, Norm.DONE)])
        turn_a = Turn("a", norm_a2, [(ln_sb[:, v, 0:1], ln_sb[:, v, 1:2], None, xs[v]) for v in range(3)])
        attn_a = Attention("attn_a", SCALE_A, True, xs[0], xs[1], xs[2], xn, turn_a, loads["wa"], loads["woa"])
        norm_m = Norm("m", xn, tmp_tok, [(attn_a.y_added, Attention.Y_DONE)])
        turn_m = Turn("m", norm_m, [(ln_sb[:, 3, 0:1], ln_sb[:, 3, 1:2], xT32, None)])
        mlp = Mlp(turn_m)
        norm_f1 = Norm("f1", x, xn, [(mlp.x_ready, Mlp.X_DONE)])
        turn_f1 = Turn("f1", norm_f1, [(1.0, 0.0, xT32, xs[0])])
        moe1 = Moe("moe1", turn_f1)
        norm_b = Norm("b", x, xn, [(moe1.x_ready, Moe.X_DONE)])
        turn_b = Turn("b", norm_b, [(1.0, 0.0, xT32, xs[0])])
        attn_b = Attention("attn_b", SCALE_B, False, xs[0], xs[0], xs[0], x, turn_b, loads["wb"], loads["wob"])
        norm_f2 = Norm("f2", x, xn, [(attn_b.y_added, Attention.Y_DONE)])
        turn_f2 = Turn("f2", norm_f2, [(1.0, 0.0, xT32, xs[0])])
        moe2 = Moe("moe2", turn_f2)

        def load_attention(e, k, w_sem, wo_sem):
            for i in range(3):
                e.dma_start(attn_a.raw_weights(i), t[f"w{k}"][i]).then_inc(w_sem, 16)
            e.dma_start(bqk[:], t[f"bqk{k}"]).then_inc(w_sem, 16)
            e.dma_start(bv[:], t[f"bv{k}"].partition_broadcast(P)).then_inc(w_sem, 16)
            e.dma_start(wo[:], t[f"wo{k}"].rearrange("(a r) n -> r a n", r=P)).then_inc(wo_sem, 16)
            e.dma_start(bo[:], t[f"bo{k}"].partition_broadcast(P)).then_inc(wo_sem, 16)

        block = ctx.enter_context(nc.Block())

        @block.sync
        def _(sp):
            sp.dma_start(x[:], t["x"].rearrange("b (t p) d -> p (b t) d", p=P)).then_inc(loads["x"], 16)
            for dst, name in ((ident, "ident"), (ident16, "ident16"), (mrows, "mrows"), (iota, "iota"), (ln_sb, "ln_sb")):
                sp.dma_start(dst[:], t[name]).then_inc(loads["const"], 16)
            load_attention(sp, "a", loads["wa"], loads["woa"])
            for ex in range(NE):
                if ex >= 3:
                    sp.wait_ge(w_lo, ex - 2)
                w1, w2 = (t["fw1"][ex], t["fw2"][ex]) if ex < E else (t["fws1"], t["fws2"])
                sp.dma_start(stage[:, ex % 3, 0:HID], w1).then_inc(staged[ex % 3], 16)
                sp.dma_start(stage[:, ex % 3, HID:2 * HID].rearrange("p (i n) -> p i n", i=HT),
                             w2.rearrange("(i p) n -> p i n", p=P)).then_inc(staged[ex % 3], 16)
            sp.dma_start(gw[:], t["gw"]).then_inc(loads["gate"], 16)
            sp.dma_start(gb[:], t["gb"]).then_inc(loads["gate"], 16)
            sp.dma_start(fb1[:], t["fb1"]).then_inc(loads["ffn"], 16)
            sp.dma_start(fb2[:], t["fb2"]).then_inc(loads["ffn"], 16)
            sp.dma_start(mw1[:], t["mw1"]).then_inc(loads["mlp"], 16)
            sp.dma_start(mw2[:], t["mw2"].rearrange("(i p) n -> p i n", p=P)).then_inc(loads["mlp"], 16)
            sp.dma_start(mb1[:], t["mb1"]).then_inc(loads["mlp"], 16)
            sp.dma_start(mb2[:], t["mb2"].partition_broadcast(P)).then_inc(loads["mlp"], 16)
            attn_a.sp(sp)
            sp.wait_ge(attn_a.y_added, Attention.Y_DONE)
            load_attention(sp, "b", loads["wb"], loads["wob"])
            attn_b.sp(sp)
            for g in range(NG):
                sp.wait_ge(moe2.x_ready, g + 1)
                sp.dma_start(out.rearrange("b (t p) d -> p (b t) d", p=P)[:, 4 * g:4 * g + 4, :],
                             x[:, 4 * g:4 * g + 4, :]).then_inc(stored, 16)
            sp.wait_ge(stored, 16 * NG)

        @block.gpsimd
        def _(pool):
            nc.gpsimd.memset(ones[:], 1.0).then_inc(const_ready, 1)
            pool.wait_ge(const_ready, 1)
            nc.gpsimd.memset(spare[:], 0.0).then_inc(const_ready, 1)
            pool.wait_ge(const_ready, 2)
            for b in range(B):
                nc.gpsimd.memset(heads[b][HD:HD + 1, :, KB, :], 1.0).then_inc(rows_ready, 1)
                pool.wait_ge(rows_ready, b + 1)
            for ex in range(NE):
                pool.wait_ge(w_64, ex + 1)
                nc.gpsimd.tensor_tensor(w1l[:, ex, :], stage[:, ex % 3, 0:HID], w1h[:, ex, :], ALU.subtract)
                nc.gpsimd.tensor_tensor(w2l[:, ex, :], stage[:, ex % 3, HID:2 * HID], w2h[:, ex, :], ALU.subtract).then_inc(w_lo, 1)
            attn_a.pool(pool)
            pool.wait_ge(moe1.down, Moe.NK)
            for b in range(B):
                nc.gpsimd.memset(heads[b][HD:HD + 1, :, KB, :], 1.0).then_inc(rows_ready, 1)
                pool.wait_ge(rows_ready, B + b + 1)
            attn_b.pool(pool)

        @block.scalar
        def _(act):
            norm_a1.act(act)
            norm_a2.act(act)
            act.wait_ge(loads["const"], 16 * 5)
            act.wait_ge(attn_a.wsplit_lo, 3)
            turn_a.act(act)
            attn_a.act_prologue(act)
            for ex in range(NE):
                act.wait_ge(staged[ex % 3], 32 * (ex // 3 + 1))
                nc.scalar.activation(w1h[:, ex, :], stage[:, ex % 3, 0:HID], ACT.Copy, scale=WS)
                nc.scalar.activation(w2h[:, ex, :], stage[:, ex % 3, HID:2 * HID], ACT.Copy, scale=WS).then_inc(w_hi, 1)
                act.wait_ge(w_hi, ex + 1)
                nc.scalar.activation(stage[:, ex % 3, :], stage[:, ex % 3, :], ACT.Copy, scale=WS).then_inc(w_64, 1)
            attn_a.act(act)
            norm_m.act(act)
            turn_m.act(act)
            mlp.act(act)
            norm_f1.act(act)
            turn_f1.act(act)
            act.wait_ge(loads["ffn"], 16 * 2)
            moe1.act(act)
            norm_b.act(act)
            turn_b.act(act)
            attn_b.act_prologue(act)
            attn_b.act(act)
            norm_f2.act(act)
            turn_f2.act(act)
            moe2.act(act)

        @block.vector
        def _(dve):
            norm_a1.dve(dve)
            norm_a2.dve(dve)
            attn_a.dve_weights(dve)
            turn_a.dve(dve)
            attn_a.dve(dve)
            norm_m.dve(dve)
            mlp.dve(dve)
            norm_f1.dve(dve)
            turn_f1.dve(dve)
            moe1.dve(dve)
            norm_b.dve(dve)
            attn_b.dve_weights(dve)
            turn_b.dve(dve)
            attn_b.dve(dve)
            norm_f2.dve(dve)
            turn_f2.dve(dve)
            moe2.dve(dve)

        @block.tensor
        def _(pe):
            pe.wait_ge(loads["const"], 16 * 5)
            pe.wait_ge(const_ready, 2)
            turn_a.pe(pe)
            pe.wait_ge(rows_ready, 2)
            attn_a.pe(pe)
            turn_m.pe(pe)
            mlp.pe(pe)
            turn_f1.pe(pe)
            pe.wait_ge(loads["ffn"], 16 * 2)
            moe1.pe(pe)
            turn_b.pe(pe)
            pe.wait_ge(rows_ready, 4)
            attn_b.pe(pe)
            turn_f2.pe(pe)
            moe2.pe(pe)


def kernel(**inputs):
    import numpy as np
    import concourse.bacc as _bacc
    from concourse import mybir as _mybir
    from concourse.bass_utils import run_bass_kernel_spmd as _run

    a = {k.removeprefix("L0_"): np.asarray(v) for k, v in inputs.items()}

    def cols(v, *shape):
        return np.ascontiguousarray(np.moveaxis(v.reshape(*shape, 128), -1, 0))

    last, first = np.zeros(128, np.float32), np.zeros(128, np.float32)
    first[0] = last[127] = MASK * float(D) ** 0.5
    arrays = {
        "x": a["attn_a_x"],
        "ident": np.eye(128, dtype=np.float32), "ident16": np.eye(128, dtype=np.float16),
        "mrows": np.stack([first, last])[None], "iota": np.tile(np.arange(E, dtype=np.float32), (128, 1)),
        "ln_sb": np.stack([np.stack([a[f"attn_a_ln{k}_{p}"] for p in "sb"], -1) for k in "qkvm"], 1),
        "wa": np.stack([a[f"attn_a_W{k}"] for k in "qkv"]),
        "bqka": np.stack([cols(a[f"attn_a_b{k}"], 8) for k in "qk"], 1),
        "bva": a["attn_a_bv"], "woa": a["attn_a_Wo"], "boa": a["attn_a_bo"],
        "wb": np.stack([a[f"attn_b_W_{k}"].transpose(2, 0, 1).reshape(128, 1024) for k in "QKV"]),
        "bqkb": np.stack([cols(a[f"attn_b_b_{k}"], 8) for k in "QK"], 1),
        "bvb": a["attn_b_b_V"].reshape(-1), "wob": a["attn_b_W_O"].transpose(0, 2, 1).reshape(1024, 128),
        "bob": a["attn_b_b_O"],
        "mw1": a["attn_a_W1"], "mw2": a["attn_a_W2"], "mb1": cols(a["attn_a_b1"], 2), "mb2": a["attn_a_b2"],
        "gw": a["ffn_gate_w"], "gb": a["ffn_gate_b"][None],
        "fw1": a["ffn_w1"], "fws1": a["ffn_ws1"], "fw2": a["ffn_w2"], "fws2": a["ffn_ws2"],
        "fb1": np.concatenate([cols(a["ffn_b1"], 8, 4), cols(a["ffn_bs1"], 1, 4)], 1),
        "fb2": np.concatenate([a["ffn_b2"], a["ffn_bs2"][None]]),
    }
    nc = _bacc.Bacc("TRN2", target_bir_lowering=False, num_devices=1)
    feeds, aps = {}, {}
    for name, v in arrays.items():
        v = np.ascontiguousarray(v)
        feeds[f"in_{name}"] = v
        aps[name] = nc.dram_tensor(f"in_{name}", v.shape, _mybir.dt.from_np(v.dtype), kind="ExternalInput").ap()
    out = nc.dram_tensor("out_0", (B, S, D), _mybir.dt.float32, kind="ExternalOutput").ap()
    build(nc, aps, out)
    r = _run(nc, [feeds], core_ids=[0])
    return r.results[0]["out_0"]
```

```python
from contextlib import ExitStack

import concourse.bass as bass
from concourse import mybir

F32 = mybir.dt.float32
F16 = mybir.dt.float16
U32 = mybir.dt.uint32
ALU = mybir.AluOpType
ACT = mybir.ActivationFunctionType
AX = mybir.AxisListType

P = 128
B, S, D = 2, 1024, 128
TOK = B * S
NT = TOK // P
NG = TOK // 512
H, HD = 16, 64
PAIRS = H // 2
NIT = PAIRS * B
KT = S // P
NC = S // 512
U = NC * KT
E, HID = 8, 512
NE = E + 1
HT = HID // P
WS = 64.0
EPS = 1e-5
MASK = -999.0
SCALE_A = float(D) ** -0.5
SCALE_B = float(HD) ** -0.5
QB, KB, KA, QA = range(4)
QH, KL, KH, QL = range(4)

NM = KT * 2

M_STEPS = {3: 1, 4: 1, 5: 1, 6: 2, 7: 1, 8: 2, 9: 1, 10: 1, 11: 1, 12: 1, 13: 1, 14: 2, 15: 1}
M_STEPS_FIRST = {7: 1, 8: 2, 9: 2, 10: 2, 11: 2, 12: 2, 13: 2, 14: 2, 15: 1}


def extras(u, first, last):
    out = []
    lead = 4 if first else 0
    if first and u < 4:
        out += [("N", NM // 2 + 2 * u), ("N", NM // 2 + 2 * u + 1)]
    if not last:
        if u == lead:
            out.append(("Q", 0))
        if u == lead + 1:
            out.append(("K", 0))
        if u == lead + 2:
            out.append(("V", 0))
    if not first:
        if u == 2:
            out.append(("L", 1))
        if u == 7:
            out.append(("Y", 1))
    if u == (5 if first else 3):
        out.append(("T", 1))
    if u == 10:
        out.append(("L", 0))
    if not last:
        steps = M_STEPS_FIRST if first else M_STEPS
        done = sum(n for v, n in steps.items() if v < u)
        out += [("M", done + i) for i in range(steps.get(u, 0))]
        if u == (13 if first else 10):
            out.append(("T", 0))
    if 2 <= u < 6 and not first:
        out.append(("R", 4 + u - 2))
    if 10 <= u < 14:
        out.append(("R", u - 10))
    if u == U - 1:
        out.append(("Y", 0))
    return out


PROLOGUE = [("Q", 0), ("K", 0), ("V", 0)] + [("M", i) for i in range(NM // 2)] + [("T", 0)]


def ring_of(first, last):
    return [x for u in range(U) for x in extras(u, first, last) if x[0] not in "LR"]


PRO = len(PROLOGUE)
R0 = len(ring_of(True, False))
R1 = len(ring_of(False, False))


def at(n, value):
    return isinstance(n, int) and n == value


def ring_base(n, first):
    return PRO if first else n * R1 + (PRO + R0 - R1)


def build(nc, t, out):
    with ExitStack() as ctx:
        def sb(name, shape, dt):
            return ctx.enter_context(nc.sbuf_tensor(name, shape, dt))

        def sem(name):
            return ctx.enter_context(nc.semaphore(name))

        ps = ctx.enter_context(nc.psum_tensor("ps", [P, 8, 512], F32))

        x = sb("x", [P, NT, D], F32)
        xn = sb("xn", [P, NT, D], F32)
        xs = [sb(f"xs{v}", [P, 2, TOK], F16) for v in range(3)]
        xT32 = xs[1][:].rearrange("p a n -> p (a n)").bitcast(F32)
        wh = sb("wh", [P, 3, H * HD], F16)
        wl = sb("wl", [P, 3, H * HD], F16)
        wo = sb("wo", [P, PAIRS, D], F32)
        bqk = sb("bqk", [P, 2, PAIRS], F32)
        bv = sb("bv", [P, H * HD], F32)
        bo = sb("bo", [P, D], F32)
        w1h = sb("w1h", [P, NE, HID], F16)
        w1l = sb("w1l", [P, NE, HID], F16)
        w2h = sb("w2h", [P, NE, HT * D], F16)
        w2l = sb("w2l", [P, NE, HT * D], F16)
        stage = sb("stage", [P, 3, 2 * HID], F32)
        fb1 = sb("fb1", [P, NE, HT], F32)
        fb2s = sb("fb2s", [2, NE * D], F16)
        gw = sb("gw", [P, E], F32)
        gwh = sb("gwh", [P, E], F16)
        gwl = sb("gwl", [P, E], F16)
        gb = sb("gb", [P, E], F32)
        ln_sb = sb("ln_sb", [P, 4, 2], F32)
        mw1 = sb("mw1", [P, 2 * D], F32)
        mw2 = sb("mw2", [P, 2, D], F32)
        mb1 = sb("mb1", [P, 2], F32)
        mb2 = sb("mb2", [P, D], F32)
        ident = sb("ident", [P, P], F32)
        ident16 = sb("ident16", [P, P], F16)
        ones = sb("ones", [P, P], F32)
        ones16 = sb("ones16", [2, P], F16)
        mrows = sb("mrows", [1, 2, P], F32)
        iota = sb("iota", [P, E], F32)
        pair = sb("pair", [P, 4, S], F16)
        heads = [sb(f"heads{b}", [P, 2, 4, S], F16) for b in range(2)]
        vb = [sb(f"vb{b}", [P, KT, P], F32) for b in range(2)]
        pt = sb("pt", [P, 4, 2, 512], F32)
        acc = sb("acc", [P, NC, 2, 512], F32)
        f = sb("f", [P, 2, S], F32)
        ou = sb("ou", [P, NC, 512], F32)
        att = sb("att", [P, NC, 512], F32)
        mxp = sb("mxp", [P, KT, 2, 2], F32)
        mtmp = sb("mtmp", [P, NC, 4, 2], F32)
        mneg = sb("mneg", [P, NC, 2, 4], F16)
        mrow = sb("mrow", [8, NC, P], F16)
        spare = sb("spare", [P, 4], F32)
        now_b1 = sb("now_b1", [P, HT], F32)
        st = sb("st", [P, NT, 6], F32)
        mv = sb("mv", [P, NT, 2], F32)
        var = sb("var", [P, NT], F32)
        std = sb("std", [P, NT], F32)
        rstd = sb("rstd", [P, NT], F32)
        var2 = sb("var2", [P, NT], F32)
        std2 = sb("std2", [P, NT], F32)
        rstd2 = sb("rstd2", [P, NT], F32)
        ix8 = sb("ix8", [P, NT, 8], U32)
        ixf = sb("ixf", [P, NT, 2], F32)
        gd = sb("gd", [P, NT], F32)
        ge = sb("ge", [P, NT], F32)
        gden = sb("gden", [P, NT], F32)
        g1 = sb("g1", [P, NT], F32)
        g2 = sb("g2", [P, NT], F32)

        fb2 = f[0:2].rearrange("p a n -> p (a n)")[:, 0:NE * D]
        fb2h = pair[0:2].rearrange("p a n -> p (a n)")[:, 0:NE * D]
        att_flat = att[:].rearrange("p c n -> p (c n)")

        def gate_buffer(at, *shape):
            size = shape[0] * shape[1] * (shape[2] if len(shape) > 2 else 1)
            names = "abc"[:len(shape)]
            return att_flat[:, at:at + size].rearrange(f"p ({' '.join(names)}) -> p {' '.join(names)}",
                                                       **dict(zip(names, shape)))

        lg = gate_buffer(0, NT, E)
        mx8 = gate_buffer(NT * E, NT, 8)
        eq = gate_buffer(2 * NT * E, 2, NT, E)
        comb = gate_buffer(4 * NT * E, NE, NT)
        combs = gate_buffer(4 * NT * E + NE * NT, NE, NT)
        pt_flat = pt[:].rearrange("p a b n -> p (a b n)")
        tmp_tok = pt_flat[:, 0:NT * D].rearrange("p (t d) -> p t d", t=NT)
        tmp_m = xs[2][:].rearrange("p a n -> p (a n)").bitcast(F32).rearrange("p (t d) -> p t d", t=NT)
        h1T = heads[0][:].rearrange("p a b n -> p (a b n)").bitcast(F32).rearrange("p (i n) -> p i n", i=2)
        h32 = pt_flat.rearrange("p (r n) -> p r n", r=8)
        hsplit = [heads[b][:].rearrange("p a b n -> p (a b n)")[:, 0:2 * HT * 512]
                  .rearrange("p (s i n) -> p s i n", s=2, i=HT) for b in range(2)]

        loads = {}

        def load_sem(name):
            loads[name] = sem("ld_" + name)
            return loads[name]

        for name in ("x0", "x1", "x2", "x3", "const", "ln", "wa", "woa", "mlp", "ffn", "gate", "wb", "wob"):
            load_sem(name)
        staged = [sem(f"staged{i}") for i in range(3)]
        w_hi = sem("w_hi")
        w_lo = sem("w_lo")
        small_hi = sem("small_high")
        small_lo = sem("small_low")
        stored = sem("stored")
        const_ready = sem("const_ready")
        rows_ready = sem("rows_ready")

        class Norm:
            STEPS = 14

            def __init__(self, name, src, dst, before, twice=None):
                self.src, self.dst, self.before, self.twice = src, dst, before, twice
                self.stats = sem(name + "_norm_stats")
                self.root = sem(name + "_norm_root")
                self.done = sem(name + "_norm_done")
                if twice is not None:
                    self.var2 = sem(name + "_norm_var2")
                    self.root2 = sem(name + "_norm_root2")
                    self.done2 = sem(name + "_norm_done2")

            def out(self):
                return self.dst if self.twice is None else self.twice

            def tile_done(self, i):
                return (self.done if self.twice is None else self.done2), 5 * (i // 4) + i % 4 + 2

            def dve_stats(self, e, g):
                e.wait_ge(*self.before[g])
                for i in range(4 * g, 4 * g + 4):
                    nc.vector.bn_stats(st[:, i, :], self.src[:, i, :]).then_inc(self.stats, 1)
                e.wait_ge(self.stats, 9 * g + 4)
                for i in range(4 * g, 4 * g + 4):
                    nc.vector.bn_aggr(mv[:, i, :], st[:, i, :]).then_inc(self.stats, 1)
                e.wait_ge(self.stats, 9 * g + 8)
                r = slice(4 * g, 4 * g + 4)
                nc.vector.tensor_scalar(var[:, r], mv[:, r, 1], EPS, None, ALU.add).then_inc(self.stats, 1)

            def act_root(self, e, g):
                e.wait_ge(self.stats, 9 * g + 9)
                nc.scalar.activation(std[:, 4 * g:4 * g + 4], var[:, 4 * g:4 * g + 4], ACT.Sqrt).then_inc(self.root, 1)

            def dve_norm(self, e, g):
                e.wait_ge(self.root, g + 1)
                nc.vector.reciprocal(rstd[:, 4 * g:4 * g + 4], std[:, 4 * g:4 * g + 4]).then_inc(self.done, 1)
                e.wait_ge(self.done, 5 * g + 1)
                for i in range(4 * g, 4 * g + 4):
                    nc.vector.tensor_scalar(self.dst[:, i, :], self.src[:, i, :], mv[:, i, 0:1], rstd[:, i:i + 1],
                                            ALU.subtract, ALU.mult).then_inc(self.done, 1)

            def dve_stats2(self, e, g):
                r = slice(4 * g, 4 * g + 4)
                nc.vector.tensor_tensor(var2[:, r], mv[:, r, 1], rstd[:, r], ALU.mult).then_inc(self.var2, 1)
                e.wait_ge(self.var2, 3 * g + 1)
                nc.vector.tensor_tensor(var2[:, r], var2[:, r], rstd[:, r], ALU.mult).then_inc(self.var2, 1)
                e.wait_ge(self.var2, 3 * g + 2)
                nc.vector.tensor_scalar(var2[:, r], var2[:, r], EPS, None, ALU.add).then_inc(self.var2, 1)

            def act_root2(self, e, g):
                e.wait_ge(self.var2, 3 * g + 3)
                nc.scalar.activation(std2[:, 4 * g:4 * g + 4], var2[:, 4 * g:4 * g + 4], ACT.Sqrt).then_inc(self.root2, 1)

            def dve_norm2(self, e, g):
                e.wait_ge(self.root2, g + 1)
                nc.vector.reciprocal(rstd2[:, 4 * g:4 * g + 4], std2[:, 4 * g:4 * g + 4]).then_inc(self.done2, 1)
                e.wait_ge(self.done2, 5 * g + 1)
                e.wait_ge(self.done, 5 * g + 5)
                for i in range(4 * g, 4 * g + 4):
                    nc.vector.tensor_scalar(self.twice[:, i, :], self.dst[:, i, :], rstd2[:, i:i + 1], None,
                                            ALU.mult).then_inc(self.done2, 1)

        class Turn:

            def __init__(self, name, norm, variants, banks, free=None):
                self.norm, self.variants, self.banks = norm, variants, banks
                self.free = free or {}
                self.n = len(variants)
                self.full = sem(name + "_turned")
                self.hi = sem(name + "_high")
                self.f32 = sem(name + "_affine")
                self.lo = sem(name + "_low")
                self.split = any(v[3] is not None for v in variants)

            def ready(self, g):
                return (self.lo if self.split else self.f32), (g + 1) * self.n

            def out32(self, g, v):
                if self.variants[v][2] is not None:
                    return self.variants[v][2][:, 512 * g:512 * g + 512]
                q = (g * self.n + v) % 4
                return f[:, q // 2, 512 * (q % 2):512 * (q % 2) + 512]

            def pe(self, e, g):
                if g in self.free:
                    e.wait_ge(*self.free[g])
                if g >= 2 and self.banks[g] == self.banks[g - 2]:
                    e.wait_ge(self.f32, (g - 1) * self.n)
                for i in range(4):
                    e.wait_ge(*self.norm.tile_done(4 * g + i))
                    last = nc.tensor.transpose(ps[:, self.banks[g], P * i:P * i + P], self.norm.out()[:, 4 * g + i, :], ident[:])
                last.then_inc(self.full, 1)

            def act(self, e, g):
                e.wait_ge(self.full, g + 1)
                for v, (scale, offset, out32, split) in enumerate(self.variants):
                    q = g * self.n + v
                    if split is not None:
                        nc.scalar.activation(split[:, 0, 512 * g:512 * g + 512], ps[:, self.banks[g], :], ACT.Identity,
                                             bias=offset, scale=scale).then_inc(self.hi, 1)
                    if out32 is None and q >= 4:
                        e.wait_ge(self.lo, q - 3)
                    nc.scalar.activation(self.out32(g, v), ps[:, self.banks[g], :], ACT.Identity,
                                         bias=offset, scale=scale).then_inc(self.f32, 1)

            def dve(self, e, g):
                for v, (_, _, _, split) in enumerate(self.variants):
                    q = g * self.n + v
                    hi, lo = (split[:, k, 512 * g:512 * g + 512] for k in range(2))
                    e.wait_ge(self.hi, q + 1)
                    e.wait_ge(self.f32, q + 1)
                    nc.vector.tensor_tensor(lo, self.out32(g, v), hi, ALU.subtract).then_inc(self.lo, 1)

        class Attention:

            def __init__(self, name, scale, masked, xq, xk, xv, y, turn, w_sem, wo_sem):
                self.scale, self.masked, self.x3, self.y, self.turn = scale, masked, (xq, xk, xv), y, turn
                self.beside = {}
                self.w_sem, self.wo_sem = w_sem, wo_sem

                def s(what):
                    return sem(f"{name}_{what}")

                self.wsplit_hi = s("w_high")
                self.wsplit_lo = s("w_low")
                self.y_init = s("y_init")
                self.ring_full = s("ring_full")
                self.f_ready = s("f_ready")
                self.hi_ready = s("hi_ready")
                self.lo_ready = s("lo_ready")
                self.v_ready = s("v_ready")
                self.max_ready = s("max_ready")
                self.mtmp_ready = s("mtmp_ready")
                self.mneg_ready = s("mneg_ready")
                self.mrow_ready = s("mrow_ready")
                self.assembled = s("assembled")
                self.max_rows = [s(f"max_rows{c}") for c in range(NC)]
                self.scores = s("scores")
                self.probs = s("probs")
                self.pv = s("pv")
                self.summed = s("summed")
                self.o_copied = s("o_copied")
                self.sums = s("sums")
                self.rec_ready = s("rec_ready")
                self.att_ready = s("att_ready")
                self.y_added = s("y_added")

            def freed(self, use, n):
                kind, i = use
                if kind == "Q" or kind == "K":
                    return self.f_ready, 2 * (n + 1) + (1 if kind == "Q" else 2)
                if kind == "V":
                    return self.v_ready, n + 2
                if kind == "M":
                    return self.max_ready, NM * (n + 1) + i + 1
                if kind == "N":
                    return self.max_ready, NM * n + i + 1
                if kind == "T":
                    return self.mrow_ready, (2 * (n + 1) + 1 if i == 0 else 2 * n + 2)
                if kind == "Y":
                    return self.y_added, (2 * n + 1 if i == 0 else 2 * n)
                raise ValueError(kind)

            def slot(self, number, parity):
                k = 2 * ((number + parity) % 2)
                return ps[:, k:k + 2, :]

            def pe(self, e):
                e.wait_ge(*self.turn.ready(1))
                e.wait_ge(self.wsplit_lo, 3)
                uses = PROLOGUE
                for k, use in enumerate(uses):
                    if k >= 2:
                        e.wait_ge(*self.freed(uses[k - 2], -1))
                    self.pe_use(e, use, -1, 0, 1, k)
                self.turn.pe(e, 2)
                self.turn.pe(e, 3)
                e.wait_ge(self.turn.f32, 3 * self.turn.n)
                self.pe_iteration(e, 0, 0, 0, True, False)
                with e.Fori(0, NIT // 2 - 1) as j:
                    self.pe_iteration(e, 2 * j + 1, j, 1, False, False)
                    self.pe_iteration(e, 2 * j + 2, j + 1, 0, False, False)
                self.pe_iteration(e, NIT - 1, PAIRS - 1, 1, False, True)
                self.pe_pv(e, NIT - 1, 1, U - 1)

            def pe_last_sums(self, e):
                self.pe_sums(e, NIT, 1)

            def pe_last_y(self, e):
                self.pe_y(e, NIT, 1, ps[:, 4:6, :], PAIRS - 1)

            def pe_iteration(self, e, n, p, b, first, last):
                uses = ring_of(first, last)
                before = PROLOGUE if first else ring_of(at(n, 1), False)
                chain = [(x, n - 1 if not first else -1) for x in before[-2:]] + [(x, n) for x in uses]
                k = 0
                for u in range(U):
                    c, kt = divmod(u, KT)
                    if u == 0:
                        e.wait_ge(self.assembled, 96 * (n + 1))
                        e.wait_ge(self.max_rows[0], 32 * (n + 1))
                    if kt == 0 and c == 1:
                        e.wait_ge(self.max_rows[1], 32 * (n + 1))
                    for h in range(2):
                        if not (first and u == 0):
                            e.wait_ge(self.probs, 2 * U * n + 2 * u + h - 1)
                        self.pe_scores(e, b, h, c, kt)
                    for use in extras(u, first, last):
                        if use[0] == "L":
                            self.pe_sums(e, n, use[1])
                        if use[0] in "LR":
                            continue
                        if first and use == ("Q", 0):
                            e.wait_ge(*self.turn.ready(3))
                        e.wait_ge(*self.freed(*chain[k]))
                        self.pe_use(e, use, n, p, b, k)
                        k += 1
                    if u > 0:
                        self.pe_pv(e, n, b, u - 1)
                    elif not first:
                        self.pe_pv(e, n - 1, 1 - b, U - 1)

            def pe_use(self, e, use, n, p, b, k):
                kind, i = use
                slot = self.ring_slot(n, b, k)
                p1, b1 = p + b if not at(n, -1) else 0, 1 - b
                if kind in "QK":
                    self.pe_qk(e, "QK".index(kind), p1, b1, slot)
                elif kind == "V":
                    self.pe_v(e, p1, b1, slot)
                elif kind in "MN":
                    e.wait_ge(self.hi_ready, 2 * n + (4 if kind == "M" else 2))
                    self.pe_m(i, slot)
                elif kind == "T":
                    e.wait_ge(self.mneg_ready, 2 * (n + 1) + 1 if i == 0 else 2 * n + 2)
                    nc.tensor.transpose(slot[0:8, 0, 0:64].bitcast(F16),
                                        mneg[:, i].rearrange("p h t -> p (h t)"), ident16[:]).then_inc(self.ring_full, 1)
                elif kind == "Y":
                    self.pe_y(e, n, i, slot, p if i == 0 else p + b - 1)

            def ring_slot(self, n, b, k):
                if at(n, -1):
                    return self.slot(k, 0)
                if at(n, 0):
                    return self.slot(PRO + k, 0)
                return self.slot(PRO + R0 - R1 + k, b * R1)

            def pe_qk(self, e, which, p, b, slot):
                hi, lo = (w[:, which, bass.ds(p * P, P)] for w in (wh, wl))
                xt = self.x3[which]
                for c in range(NC):
                    cols = slice(b * S + 512 * c, b * S + 512 * c + 512)
                    nc.tensor.matmul(slot[:, c, :], hi, xt[:, 0, cols], start=True, stop=False)
                    nc.tensor.matmul(slot[:, c, :], hi, xt[:, 1, cols], start=False, stop=False)
                    last = nc.tensor.matmul(slot[:, c, :], lo, xt[:, 0, cols], start=False, stop=True)
                last.then_inc(self.ring_full, 1)

            def pe_v(self, e, p, b, slot):
                hi, lo = (w[:, 2, bass.ds(p * P, P)] for w in (wh, wl))
                for i in range(KT):
                    cols = slice(b * S + P * i, b * S + P * i + P)
                    o = slot[:, i // 4, P * (i % 4):P * (i % 4) + P]
                    nc.tensor.matmul(o, self.x3[2][:, 0, cols], hi, start=True, stop=False)
                    nc.tensor.matmul(o, self.x3[2][:, 0, cols], lo, start=False, stop=False)
                    last = nc.tensor.matmul(o, self.x3[2][:, 1, cols], hi, start=False, stop=True)
                last.then_inc(self.ring_full, 1)

            def pe_m(self, item, slot):
                i, half = divmod(item, 2)
                masked = self.masked and i == 0 and half == 1
                for h in range(2):
                    r = slice(HD * h, HD * h + HD)
                    last = nc.tensor.matmul(slot[:, h, :], pair[r, QH, P * i:P * i + P], pair[r, KH, 512 * half:512 * half + 512],
                                            start=True, stop=True)
                if masked:
                    for h in range(2):
                        last = nc.tensor.matmul(slot[:, h, 511:512], mrows[0:1, 0, :], ones[0:1, 0:1], start=False, stop=True,
                                                skip_group_check=True)
                last.then_inc(self.ring_full, 1)

            def pe_scores(self, e, b, h, c, kt):
                hb = heads[b]
                keys, queries = slice(P * kt, P * kt + P), slice(512 * c, 512 * c + 512)
                o = ps[:, 4 + h, :]
                masked = self.masked and c == 0 and kt == KT - 1
                nc.tensor.matmul(o, hb[:, h, KA, keys], hb[:, h, QA, queries], start=True, stop=False)
                last = nc.tensor.matmul(o, hb[0:HD + 1, h, KB, keys], hb[0:HD + 1, h, QB, queries],
                                        start=False, stop=True)
                if masked:
                    last = nc.tensor.matmul(o[:, 0:1], mrows[0:1, 1, :], ones[0:1, 0:1], start=False, stop=True,
                                            skip_group_check=True)
                last.then_inc(self.scores, 1)

            def pe_pv(self, e, n, b, u):
                c, kt = divmod(u, KT)
                e.wait_ge(self.probs, 2 * U * n + 2 * u + 2)
                if u == 0:
                    e.wait_ge(self.v_ready, n + 1)
                if kt == 0 and not (at(n, 0) and c == 0):
                    e.wait_ge(self.o_copied, 2 * n + c)
                for h in range(2):
                    last = nc.tensor.matmul(ps[HD * h:HD * h + HD, 6, :], vb[b][:, kt, HD * h:HD * h + HD], pt[:, u % 4, h, :],
                                            start=(kt == 0), stop=(kt == KT - 1), skip_group_check=True)
                last.then_inc(self.pv, 1)

            def pe_sums(self, e, n, i):
                chunk = 2 * n if i == 0 else 2 * n - 1
                e.wait_ge(self.summed, 7 * chunk + 7)
                if not (at(n, 0) and i == 0):
                    e.wait_ge(self.rec_ready, 4 * chunk)
                for h in range(2):
                    last = nc.tensor.matmul(ps[HD * h:HD * h + HD, 7, :], ones[:, 0:HD], acc[:, i, h, :],
                                            start=True, stop=True, skip_group_check=True)
                last.then_inc(self.sums, 1)

            def pe_y(self, e, n, i, slot, p):
                e.wait_ge(self.att_ready, 2 * n + 1 if i == 0 else 2 * n)
                for k in range(4):
                    last = nc.tensor.matmul(slot[:, 0, P * k:P * k + P], att[:, i, P * k:P * k + P],
                                            wo[:, p, :] if isinstance(p, int) else wo[:, bass.ds(p, 1), :].rearrange("p a n -> p (a n)"),
                                            start=True, stop=True)
                last.then_inc(self.ring_full, 1)

            def act_prologue(self, e):
                for k, use in enumerate(PROLOGUE):
                    self.act_use(e, use, -1, 0, 1, k, k)

            def act(self, e):
                self.act_prologue(e)
                e.wait_ge(self.lo_ready, 2)
                self.turn.act(e, 2)
                self.turn.act(e, 3)
                self.act_iteration(e, 0, 0, 0, True, False)
                with e.Fori(0, NIT // 2 - 1) as j:
                    self.act_iteration(e, 2 * j + 1, j, 1, False, False)
                    self.act_iteration(e, 2 * j + 2, j + 1, 0, False, False)
                self.act_iteration(e, NIT - 1, PAIRS - 1, 1, False, True)
                self.act_copy_o(e, NIT - 1, 1)

            def act_weights(self, e):
                e.wait_ge(self.w_sem, 16 * 5)
                for i in range(3):
                    nc.scalar.activation(wh[:, i, :], self.raw_weights(i), ACT.Copy, scale=WS).then_inc(self.wsplit_hi, 1)

            def act_iteration(self, e, n, p, b, first, last):
                k, base = 0, ring_base(n, first)
                for u in range(U):
                    self.act_exp(e, n, u, first)
                    for use in extras(u, first, last):
                        if use[0] not in "LR":
                            self.act_use(e, use, n, p, b, k, base + k)
                            k += 1
                    if u == 0 and not first:
                        self.act_copy_o(e, n - 1, 1)
                    if u == KT:
                        self.act_copy_o(e, n, 0)
                    if last and ("act", u) in self.beside:
                        self.beside["act", u](e)

            def act_exp(self, e, n, u, first):
                if not (first and u < 4):
                    e.wait_ge(self.pv, U * n + u - 3)
                    if u >= 4:
                        c, kt = divmod(u - 4, KT)
                        e.wait_ge(self.summed, 14 * n + 7 * c + max(kt, 1))
                    else:
                        e.wait_ge(self.summed, 14 * n - 14 + 7 + U // 2 - 4 + u)
                for h in range(2):
                    e.wait_ge(self.scores, 2 * U * n + 2 * u + h + 1)
                    nc.scalar.activation(pt[:, u % 4, h, :], ps[:, 4 + h, :], ACT.Exp,
                                         scale=self.scale).then_inc(self.probs, 1)

            def act_use(self, e, use, n, p, b, k, number):
                kind, _ = use
                if kind not in "QK":
                    return
                slot = self.ring_slot(n, b, k)
                which = "QK".index(kind)
                p1 = p + b if not at(n, -1) else 0
                e.wait_ge(self.ring_full, number + 1)
                if not at(n, -1):
                    e.wait_ge(self.lo_ready, 2 * n + which + 1)
                offset = bqk[:, which, p1:p1 + 1] if isinstance(p1, int) else bqk[:, which, bass.ds(p1, 1)]
                if not at(n, -1):
                    e.wait_ge(self.assembled, 96 * (n + 1))
                if not isinstance(p1, int):
                    nc.scalar.copy(spare[:, 1 + which:2 + which], spare[:, 0:1])
                hi = pair[:, (QH, KH)[which], :]
                nc.scalar.activation(hi.rearrange("p (a n) -> p a n", a=2), slot, ACT.Identity,
                                     bias=offset, scale=1.0 / WS).then_inc(self.hi_ready, 1)
                nc.scalar.activation(f[:, which, :].rearrange("p (a n) -> p a n", a=2), slot, ACT.Identity,
                                     bias=offset, scale=1.0 / WS).then_inc(self.f_ready, 1)

            def act_copy_o(self, e, n, c):
                e.wait_ge(self.pv, U * n + KT * c + KT)
                if c == 1:
                    e.wait_ge(self.att_ready, 2 * n + 1)
                elif not at(n, 0):
                    e.wait_ge(self.att_ready, 2 * n - 1)
                nc.scalar.activation(ou[:, c, :], ps[:, 6, :], ACT.Copy).then_inc(self.o_copied, 1)

            def dve_weights(self, e):
                for i in range(3):
                    e.wait_ge(self.wsplit_hi, i + 1)
                    nc.vector.scalar_tensor_tensor(out=wl[:, i, :], in0=self.raw_weights(i), scalar=WS, in1=wh[:, i, :],
                                                   op0=ALU.mult, op1=ALU.subtract).then_inc(self.wsplit_lo, 1)

            def dve(self, e):
                for k, use in enumerate(PROLOGUE):
                    self.dve_use(e, use, -1, 0, 1, k, k)
                self.turn.dve(e, 2)
                self.turn.dve(e, 3)
                e.wait_ge(self.wo_sem, 32)
                y = self.y
                nc.vector.tensor_tensor(y[:], y[:], bo[:].rearrange("p (a n) -> p a n", a=1).broadcast_to([P, NT, D]),
                                        ALU.add).then_inc(self.y_init, 1)
                self.dve_iteration(e, 0, 0, 0, True, False)
                with e.Fori(0, NIT // 2 - 1) as j:
                    self.dve_iteration(e, 2 * j + 1, j, 1, False, False)
                    self.dve_iteration(e, 2 * j + 2, j + 1, 0, False, False)
                self.dve_iteration(e, NIT - 1, PAIRS - 1, 1, False, True)

            def dve_last_normalise(self, e):
                for piece in range(4):
                    self.dve_normalise(e, NIT, 1, piece)

            def dve_last_y(self, e):
                self.dve_add_y(e, NIT, 1, 1, ps[:, 4:6, :], NIT * R1 + (PRO + R0 - R1) - self.ahead + 1)

            ahead = R1 - len(ring_of(False, True))

            def raw_weights(self, i):
                return (acc[:, 0].rearrange("p h n -> p (h n)"), acc[:, 1].rearrange("p h n -> p (h n)"),
                        ou[:].rearrange("p c n -> p (c n)"))[i]

            def dve_iteration(self, e, n, p, b, first, last):
                k, base = 0, ring_base(n, first)
                for u in range(U):
                    for use in extras(u, first, last):
                        if use[0] == "L":
                            continue
                        if use[0] == "R":
                            self.dve_normalise(e, n, *divmod(use[1], 4))
                            continue
                        self.dve_use(e, use, n, p, b, k, base + k)
                        k += 1
                    if last and ("dve", u) in self.beside:
                        self.beside["dve", u](e)

            def dve_use(self, e, use, n, p, b, k, number):
                kind, i = use
                slot = self.ring_slot(n, b, k)
                if kind in "QK":
                    which = "QK".index(kind)
                    done = 2 * (n + 1) + which + 1
                    hi, lo = (pair[:, s, :] for s in ((QH, QL), (KH, KL))[which])
                    e.wait_ge(self.f_ready, done)
                    nc.vector.tensor_tensor(lo, f[:, which, :], hi, ALU.subtract).then_inc(self.lo_ready, 1)
                    return
                e.wait_ge(self.ring_full, number + 1)
                if kind == "V":
                    b1, p1 = 1 - b, (p + b if not at(n, -1) else 0)
                    if not at(n, -1) and not at(n, 0):
                        e.wait_ge(self.pv, U * n)
                    offset = bv[:, p1 * P:p1 * P + P] if isinstance(p1, int) else bv[:, bass.ds(p1 * P, P)]
                    nc.vector.scalar_tensor_tensor(
                        out=vb[b1][:], in0=slot.rearrange("p a (t n) -> p (a t) n", n=P), scalar=1.0 / WS,
                        in1=offset.rearrange("p (a n) -> p a n", a=1).broadcast_to([P, KT, P]),
                        op0=ALU.mult, op1=ALU.add).then_inc(self.v_ready, 1)
                elif kind in "MN":
                    m = n + 1 if kind == "M" else n
                    t_, half = divmod(i, 2)
                    nc.vector.tensor_reduce(mxp[:, t_, :, half], slot, AX.X, ALU.max).then_inc(self.max_ready, 1)
                    if t_ % 4 == 3 and half == 1:
                        c = t_ // 4
                        e.wait_ge(self.max_ready, NM * m + i + 1)
                        nc.vector.tensor_tensor(mtmp[:, c], mxp[:, 4 * c:4 * c + 4, :, 0], mxp[:, 4 * c:4 * c + 4, :, 1],
                                                ALU.max).then_inc(self.mtmp_ready, 1)
                        e.wait_ge(self.mtmp_ready, 2 * m + c + 1)
                        nc.vector.tensor_scalar(mneg[:, c].rearrange("p h t -> p t h"), mtmp[:, c], -1.0, None,
                                                ALU.mult).then_inc(self.mneg_ready, 1)
                elif kind == "T":
                    m = n + 1 if i == 0 else n
                    if not (at(m, 0)):
                        e.wait_ge(self.max_rows[i], 32 * m)
                    nc.vector.tensor_copy(mrow[:, i, :], slot[0:8, 0, 0:64].bitcast(F16)).then_inc(self.mrow_ready, 1)
                elif kind == "Y":
                    self.dve_add_y(e, n, i, b if i == 0 else 1 - b, slot, None)

            def dve_normalise(self, e, n, i, piece):
                chunk = 2 * n if i == 0 else 2 * n - 1
                if piece == 0:
                    e.wait_ge(self.sums, chunk + 1)
                cols = slice(P * piece, P * piece + P)
                nc.vector.reciprocal(att[:, i, cols], ps[:, 7, cols]).then_inc(self.rec_ready, 1)
                if piece == 3:
                    e.wait_ge(self.rec_ready, 4 * chunk + 4)
                    e.wait_ge(self.o_copied, chunk + 1)
                    nc.vector.tensor_tensor(att[:, i, :], ou[:, i, :], att[:, i, :], ALU.mult).then_inc(self.att_ready, 1)

            def dve_add_y(self, e, n, i, b, slot, full):
                if full is not None:
                    e.wait_ge(self.ring_full, full)
                done = 2 * n if i == 0 else 2 * n - 1
                if at(n, 0) and i == 0:
                    e.wait_ge(self.y_init, 1)
                else:
                    e.wait_ge(self.y_added, done)
                first = b * KT + 4 * i
                ys = self.y[:, first:first + 4, :]
                nc.vector.tensor_tensor(ys, ys, slot[:, 0, :].rearrange("p (t n) -> p t n", t=4), ALU.add)\
                    .then_inc(self.y_added, 1)

            Y_DONE = 2 * NIT

            def pool(self, e):
                e.wait_ge(self.wsplit_lo, 3)
                self.pool_iteration(e, 0)
                with e.Fori(1, NIT) as n:
                    self.pool_iteration(e, n)

            def pool_iteration(self, e, n):
                for c in range(NC):
                    if not at(n, 0):
                        e.wait_ge(self.sums, 2 * (n - 1) + c + 1)
                    for kt in range(1, KT):
                        u = KT * c + kt
                        e.wait_ge(self.probs, 2 * U * n + 2 * u + 2)
                        one = pt[:, (u - 1) % 4] if kt == 1 else acc[:, c]
                        if kt > 1:
                            e.wait_ge(self.summed, 14 * n + 7 * c + kt - 1)
                        nc.gpsimd.tensor_tensor(acc[:, c], one, pt[:, u % 4], ALU.add).then_inc(self.summed, 1)

            def sp(self, e):
                self.sp_assemble(e, 0, 0)
                self.sp_rows(e, 0, 0, 0)
                self.sp_rows(e, 0, 0, 1)
                self.sp_assemble(e, 1, 1)
                self.sp_rows(e, 1, 1, 0)
                self.sp_rows(e, 1, 1, 1)
                with e.Fori(1, NIT // 2) as j:
                    for b in range(B):
                        m = 2 * j + b
                        self.sp_assemble(e, m, b)
                        self.sp_rows(e, m, b, 0)
                        self.sp_rows(e, m, b, 1)

            def sp_assemble(self, e, m, b):
                e.wait_ge(self.lo_ready, 2 * m + 2)
                for h in range(2):
                    r = slice(HD * h, HD * h + HD)
                    for dst, src in ((heads[b][0:HD, h, QB:KA + 1, :], pair[r, QH:KH + 1, :]),
                                     (heads[b][HD:P, h, KA:QA + 1, :], pair[r, KH:QL + 1, :]),
                                     (heads[b][0:HD, h, QA, :], pair[r, QH, :])):
                        e.dma_start(dst, src).then_inc(self.assembled, 16)

            def sp_rows(self, e, m, b, c):
                e.wait_ge(self.mrow_ready, 2 * m + c + 1)
                for h in range(2):
                    e.dma_start(heads[b][HD:HD + 1, h, QB, 512 * c:512 * c + 512],
                                mrow[4 * h:4 * h + 4, c, :]).then_inc(self.max_rows[c], 16)

        class Mlp:

            def __init__(self, turn, attn):
                self.turn, self.attn = turn, attn
                self.up = sem("mlp_up")
                self.gelu = sem("mlp_gelu")
                self.down = sem("mlp_down")
                self.x_b2 = sem("mlp_x_b2")
                self.x_h = sem("mlp_x_h")
                self.x_ready = sem("mlp_x_ready")

            def pe_up(self, e, g):
                if g == 0:
                    e.wait_ge(loads["mlp"], 16 * 4)
                e.wait_ge(self.turn.f32, g + 1)
                for i in range(2):
                    k = 2 * g + i
                    if k == 0:
                        e.wait_ge(self.attn.probs, 2 * U * NIT)
                    elif k == 1:
                        e.wait_ge(self.attn.o_copied, 2 * NIT)
                    else:
                        e.wait_ge(self.gelu, k - 1)
                    nc.tensor.matmul(ps[:, 5 + k % 2, :], mw1[:, P * i:P * i + P], xT32[:, 512 * g:512 * g + 512],
                                     start=True, stop=True).then_inc(self.up, 1)

            def pe_down(self, e, g):
                e.wait_ge(self.gelu, 2 * g + 2)
                for k in range(4):
                    for i in range(2):
                        last = nc.tensor.matmul(ps[:, self.turn.banks[g], P * k:P * k + P],
                                                h1T[:, i, 512 * g + P * k:512 * g + P * k + P],
                                                mw2[:, i, :], start=(i == 0), stop=(i == 1))
                last.then_inc(self.down, 1)

            def act(self, e, g):
                for i in range(2):
                    k = 2 * g + i
                    e.wait_ge(self.up, k + 1)
                    nc.scalar.activation(h1T[:, i, 512 * g:512 * g + 512], ps[:, 5 + k % 2, :], ACT.Gelu_apprx_tanh,
                                         bias=mb1[:, i:i + 1]).then_inc(self.gelu, 1)

            def dve_b2(self, e):
                e.wait_ge(loads["mlp"], 16 * 4)
                nc.vector.tensor_tensor(x[:], x[:], mb2[:].rearrange("p (a n) -> p a n", a=1).broadcast_to([P, NT, D]),
                                        ALU.add).then_inc(self.x_b2, 1)

            def dve_h(self, e, g):
                e.wait_ge(self.x_b2, 1)
                e.wait_ge(self.attn.y_added, 2 * NIT - 3 + g)
                xg = x[:, 4 * g:4 * g + 4, :]
                nc.vector.tensor_tensor(xg, xg, xn[:, 4 * g:4 * g + 4, :], ALU.add).then_inc(self.x_h, 1)

            def dve_down(self, e, g):
                e.wait_ge(self.down, g + 1)
                e.wait_ge(self.x_h, g + 1)
                xg = x[:, 4 * g:4 * g + 4, :]
                nc.vector.tensor_tensor(xg, xg, ps[:, self.turn.banks[g], :].rearrange("p (t n) -> p t n", t=4), ALU.add)\
                    .then_inc(self.x_ready, 1)

        class Moe:

            def __init__(self, name, turn):
                self.turn = turn

                def s(what):
                    return sem(f"{name}_{what}")

                self.logits = s("logits")
                self.gate = s("gate_dve")
                self.gexp = s("gate_exp")
                self.b1_ready = s("b1_ready")
                self.up = s("up")
                self.gelu = s("gelu")
                self.hi = s("high")
                self.lo = s("low")
                self.down = s("down")
                self.combined = s("combined")

            NK = NE * NG
            G_LG, G_MAX = 1, 1 + NT
            G_IDX = 1 + 2 * NT
            G_D = G_IDX + 2
            G_END = G_D + 10

            def pe_gate(self, e):
                e.wait_ge(*self.turn.ready(NG - 1))
                e.wait_ge(small_lo, 2)
                for i in range(NT):
                    o = ps[:, 6, E * i:E * i + E]
                    hi, lo = (xs[0][:, k, P * i:P * i + P] for k in range(2))
                    nc.tensor.matmul(o, hi, gwh[:], start=True, stop=False)
                    nc.tensor.matmul(o, hi, gwl[:], start=False, stop=False)
                    last = nc.tensor.matmul(o, lo, gwh[:], start=False, stop=True)
                last.then_inc(self.logits, 1)

            def pe(self, e, after):
                self.pe_expert(e, 0)
                with e.Fori(1, NE - 1) as ex:
                    self.pe_expert(e, ex)
                for c in range(NG):
                    if c < 3:
                        self.pe_up(e, NE - 1, c + 1, False)
                    self.pe_down(e, NE - 1, c)
                    after(c)

            def pe_expert(self, e, ex):
                for c in range(NG):
                    self.pe_up(e, ex if c < NG - 1 else ex + 1, (c + 1) % NG, False)
                    self.pe_down(e, ex, c)

            def pe_up(self, e, ex, c, start):
                for i in range(HT):
                    if not start:
                        e.wait_ge(self.gelu, 16 * ex + 4 * c + i - 3)
                    if isinstance(ex, int):
                        hi, lo = (w[:, ex, P * i:P * i + P] for w in (w1h, w1l))
                    else:
                        hi, lo = (w[:].rearrange("p e n -> p (e n)")[:, bass.ds(ex * HID + P * i, P)] for w in (w1h, w1l))
                    cols = slice(512 * c, 512 * c + 512)
                    nc.tensor.matmul(ps[:, i, :], hi, xs[0][:, 0, cols], start=True, stop=False)
                    nc.tensor.matmul(ps[:, i, :], hi, xs[0][:, 1, cols], start=False, stop=False)
                    nc.tensor.matmul(ps[:, i, :], lo, xs[0][:, 0, cols], start=False, stop=True).then_inc(self.up, 1)

            def pe_down(self, e, ex, c):
                k = 4 * ex + c
                if not (at(ex, 0) and c < 2):
                    e.wait_ge(self.combined, 4 * k - 4)
                e.wait_ge(self.lo, 4 * k + 4)
                hs = hsplit[c % 2]
                for i in range(4):
                    o = ps[:, 4 + c % 2, P * i:P * i + P]
                    cols = slice(P * i, P * i + P)
                    for q in range(HT):
                        if isinstance(ex, int):
                            hi, lo = (w[:, ex, P * q:P * q + P] for w in (w2h, w2l))
                        else:
                            hi, lo = (w[:].rearrange("p e n -> p (e n)")[:, bass.ds(ex * HID + P * q, P)] for w in (w2h, w2l))
                        nc.tensor.matmul(o, hs[:, 0, q, cols], hi, start=(q == 0), stop=False)
                        nc.tensor.matmul(o, hs[:, 0, q, cols], lo, start=False, stop=False)
                        nc.tensor.matmul(o, hs[:, 1, q, cols], hi, start=False, stop=False)
                    offset = fb2s[:, ex * D:ex * D + D] if isinstance(ex, int) else fb2s[:, bass.ds(ex * D, D)]
                    last = nc.tensor.matmul(o, ones16[:], offset, start=False, stop=True)
                last.then_inc(self.down, 1)

            def act_gate(self, e):
                e.wait_ge(self.gate, self.G_D)
                nc.scalar.activation(ge[:], gd[:], ACT.Exp).then_inc(self.gexp, 1)

            def act(self, e, between, after):
                self.act_chunk(e, 0, 2)
                self.act_chunk(e, 0, 3)
                between()
                with e.Fori(1, NE - 1) as ex:
                    self.act_offsets(e, ex)
                    for c in range(NG):
                        self.act_chunk(e, ex, c)
                self.act_offsets(e, NE - 1)
                for c in range(NG):
                    self.act_chunk(e, NE - 1, c)
                    after(c)

            def act_offsets(self, e, ex):
                if at(ex, 0):
                    nc.scalar.copy(now_b1[:], fb1[:, 0, :]).then_inc(self.b1_ready, 1)
                else:
                    e.wait_ge(self.gelu, 16 * ex)
                    nc.scalar.copy(spare[:, 3:4], spare[:, 0:1])
                    src = fb1[:, ex, :] if isinstance(ex, int) else \
                        fb1[:].rearrange("p e n -> p (e n)")[:, bass.ds(ex * HT, HT)]
                    nc.scalar.copy(now_b1[:], src).then_inc(self.b1_ready, 1)
                e.wait_ge(self.b1_ready, ex + 1)

            def act_chunk(self, e, ex, c):
                for i in range(HT):
                    k = 4 * c + i
                    if not (at(ex, 0) and k < 8):
                        e.wait_ge(self.lo, 16 * ex + k - 7)
                    e.wait_ge(self.up, 16 * ex + k + 1)
                    nc.scalar.activation(h32[:, k % 8, :], ps[:, i, :], ACT.Gelu, bias=now_b1[:, i:i + 1], scale=1.0 / WS)\
                        .then_inc(self.gelu, 1)

            def dve(self, e, between, after):
                self.dve_expert(e, 0)
                between()
                with e.Fori(1, NE - 1) as ex:
                    self.dve_expert(e, ex)
                for c in range(NG):
                    if c < 3:
                        self.dve_split(e, NE - 1, c + 1, False)
                    self.dve_combine(e, NE - 1, c)
                    after(c)

            def x_ready(self, g):
                return self.combined, 4 * (self.NK - NG + g + 1)

            def dve_gate(self, e):
                g = self.gate
                e.wait_ge(self.logits, 1)
                nc.vector.scalar_tensor_tensor(out=lg[:], in0=ps[:, 6, 0:NT * E].rearrange("p (t e) -> p t e", t=NT),
                                               scalar=1.0 / WS,
                                               in1=gb[:].rearrange("p (a e) -> p a e", a=1).broadcast_to([P, NT, E]),
                                               op0=ALU.mult, op1=ALU.add).then_inc(g, 1)
                e.wait_ge(g, self.G_LG)
                for i in range(NT):
                    nc.vector.max(mx8[:, i, :], lg[:, i, :]).then_inc(g, 1)
                e.wait_ge(g, self.G_MAX)
                for i in range(NT):
                    nc.vector.max_index(ix8[:, i, :], mx8[:, i, :], lg[:, i, :]).then_inc(g, 1)
                e.wait_ge(g, self.G_IDX)
                nc.vector.tensor_copy(ixf[:], ix8[:, :, 0:2]).then_inc(g, 1)
                nc.vector.tensor_tensor(gd[:], mx8[:, :, 1], mx8[:, :, 0], ALU.subtract).then_inc(g, 1)
                e.wait_ge(self.gexp, 1)
                n = self.G_D
                nc.vector.tensor_scalar(gden[:], ge[:], 1.0, None, ALU.add).then_inc(g, 1)
                e.wait_ge(g, n + 1)
                nc.vector.reciprocal(g1[:], gden[:]).then_inc(g, 1)
                e.wait_ge(g, n + 2)
                nc.vector.tensor_tensor(g2[:], ge[:], g1[:], ALU.mult).then_inc(g, 1)
                e.wait_ge(g, n + 3)
                io = iota[:].rearrange("p (a e) -> p a e", a=1).broadcast_to([P, NT, E])
                for k in range(2):
                    nc.vector.tensor_tensor(eq[:, k], io, ixf[:, :, k:k + 1].broadcast_to([P, NT, E]), ALU.is_equal).then_inc(g, 1)
                e.wait_ge(g, n + 5)
                for k, w in enumerate((g1, g2)):
                    nc.vector.tensor_tensor(eq[:, k], eq[:, k], w[:].rearrange("p (t a) -> p t a", a=1).broadcast_to([P, NT, E]),
                                            ALU.mult).then_inc(g, 1)
                e.wait_ge(g, n + 7)
                nc.vector.tensor_tensor(comb[:, 0:E, :].rearrange("p e t -> p t e"), eq[:, 0], eq[:, 1], ALU.add).then_inc(g, 1)
                nc.vector.memset(comb[:, E, :], 1.0).then_inc(g, 1)
                e.wait_ge(g, n + 9)
                nc.vector.tensor_scalar(combs[:], comb[:], 1.0 / WS, None, ALU.mult).then_inc(g, 1)
                e.wait_ge(g, self.G_END)

            def dve_expert(self, e, ex):
                for c in range(NG):
                    self.dve_split(e, ex if c < NG - 1 else ex + 1, (c + 1) % NG, False)
                    self.dve_combine(e, ex, c)

            def dve_split(self, e, ex, c, start):
                hs = hsplit[c % 2]
                if not (start or (at(ex, 0) and c < 2)):
                    e.wait_ge(self.down, 4 * ex + c - 1)
                for i in range(HT):
                    n = 16 * ex + 4 * c + i + 1
                    src = h32[:, (4 * c + i) % 8, :]
                    e.wait_ge(self.gelu, n)
                    nc.vector.tensor_copy(hs[:, 0, i, :], src).then_inc(self.hi, 1)
                    e.wait_ge(self.hi, n)
                    nc.vector.tensor_tensor(hs[:, 1, i, :], src, hs[:, 0, i, :], ALU.subtract).then_inc(self.lo, 1)

            def dve_combine(self, e, ex, c):
                k = 4 * ex + c
                e.wait_ge(self.down, k + 1)
                if not (at(ex, 0)):
                    e.wait_ge(self.combined, 4 * (k - 3))
                for i in range(4):
                    tile = 4 * c + i
                    w = combs[:, ex, tile:tile + 1] if isinstance(ex, int) else \
                        combs[:].rearrange("p e t -> p (e t)")[:, bass.ds(ex * NT + tile, 1)]
                    nc.vector.scalar_tensor_tensor(out=x[:, tile, :], in0=ps[:, 4 + c % 2, P * i:P * i + P], scalar=w,
                                                   in1=x[:, tile, :], op0=ALU.mult, op1=ALU.add).then_inc(self.combined, 1)

        norm_a = Norm("a", x, xn, [(loads[f"x{g}"], 16) for g in range(NG)], twice=tmp_tok)
        turn_a = Turn("a", norm_a, [(ln_sb[:, v, 0:1], ln_sb[:, v, 1:2], None, xs[v]) for v in range(3)], [6, 7, 6, 7])
        attn_a = Attention("attn_a", SCALE_A, True, xs[0], xs[1], xs[2], xn, turn_a, loads["wa"], loads["woa"])
        norm_m = Norm("m", xn, tmp_m, [(attn_a.y_added, 2 * NIT - 3 + g) for g in range(NG)])
        turn_m = Turn("m", norm_m, [(ln_sb[:, 3, 0:1], ln_sb[:, 3, 1:2], xT32, None)], [2, 3, 0, 1])
        mlp = Mlp(turn_m, attn_a)
        norm_f1 = Norm("f1", x, xn, [(mlp.x_ready, g + 1) for g in range(NG)])
        turn_f1 = Turn("f1", norm_f1, [(1.0, 0.0, None, xs[0])], [7, 6, 7, 6], free={1: (mlp.gelu, 2 * NG)})
        moe1 = Moe("moe1", turn_f1)
        norm_b = Norm("b", x, xn, [moe1.x_ready(g) for g in range(NG)])
        turn_b = Turn("b", norm_b, [(1.0, 0.0, None, xs[0])], [6, 7, 6, 7])
        attn_b = Attention("attn_b", SCALE_B, False, xs[0], xs[0], xs[0], x, turn_b, loads["wb"], loads["wob"])
        norm_f2 = Norm("f2", x, xn, [(attn_b.y_added, 2 * NIT - 3 + g) for g in range(NG)])
        turn_f2 = Turn("f2", norm_f2, [(1.0, 0.0, None, xs[0])], [5, 6, 5, 6],
                       free={0: (attn_b.probs, 2 * U * NIT), 1: (attn_b.o_copied, 2 * NIT)})
        moe2 = Moe("moe2", turn_f2)

        def nothing(*_):
            pass

        def act_expert_weights(e, ex):
            e.wait_ge(staged[ex % 3], 32 * (ex // 3 + 1))
            nc.scalar.activation(w1h[:, ex, :], stage[:, ex % 3, 0:HID], ACT.Copy, scale=WS).then_inc(w_hi, 1)
            nc.scalar.activation(w2h[:, ex, :], stage[:, ex % 3, HID:2 * HID], ACT.Copy, scale=WS).then_inc(w_hi, 1)

        def dve_expert_weights(e, ex):
            for i, (hi, lo) in enumerate(((w1h, w1l), (w2h, w2l))):
                e.wait_ge(w_hi, 2 * ex + i + 1)
                nc.vector.scalar_tensor_tensor(out=lo[:, ex, :], in0=stage[:, ex % 3, HID * i:HID * i + HID], scalar=WS,
                                               in1=hi[:, ex, :], op0=ALU.mult, op1=ALU.subtract).then_inc(w_lo, 1)

        def act_small_weights(e):
            e.wait_ge(loads["gate"], 16 * 2)
            e.wait_ge(loads["ffn"], 16 * 3)
            nc.scalar.activation(gwh[:], gw[:], ACT.Copy, scale=WS).then_inc(small_hi, 1)
            nc.scalar.activation(fb2h, fb2, ACT.Copy, scale=WS).then_inc(small_hi, 1)

        def dve_small_weights(e):
            e.wait_ge(small_hi, 2)
            nc.vector.scalar_tensor_tensor(out=gwl[:], in0=gw[:], scalar=WS, in1=gwh[:], op0=ALU.mult, op1=ALU.subtract)\
                .then_inc(small_lo, 1)
            nc.vector.tensor_scalar(fb2h, fb2h, ident[0:2, 1:2], None, ALU.mult).then_inc(small_hi, 1)
            e.wait_ge(small_hi, 3)
            nc.vector.scalar_tensor_tensor(out=fb2s[:], in0=fb2, scalar=WS, in1=fb2h, op0=ALU.mult, op1=ALU.subtract)\
                .then_inc(small_lo, 1)

        WEIGHT_STEP = {0: 0, 1: 1, 2: 2, 5: 3, 6: 4, 7: 5, 10: 6, 11: 7, 12: 8}
        for u, ex in WEIGHT_STEP.items():
            attn_a.beside["act", u] = lambda e, ex=ex: act_expert_weights(e, ex)
            attn_a.beside["dve", u] = lambda e, ex=ex: dve_expert_weights(e, ex)
        attn_a.beside["act", 3] = act_small_weights
        attn_a.beside["dve", 3] = dve_small_weights
        attn_a.beside["dve", 14] = mlp.dve_b2
        for attn, norm in ((attn_a, norm_m), (attn_b, norm_f2)):
            attn.beside["dve", 8] = lambda e, norm=norm: [norm.dve_stats(e, g) for g in range(2)]
            attn.beside["act", 9] = lambda e, norm=norm: [norm.act_root(e, g) for g in range(2)]
            attn.beside["dve", 9] = lambda e, norm=norm: [norm.dve_norm(e, g) for g in range(2)]

        def load_attention(e, k, w_sem, wo_sem):
            for i in range(3):
                e.dma_start(attn_a.raw_weights(i), t[f"w{k}"][i]).then_inc(w_sem, 16)
            e.dma_start(bqk[:], t[f"bqk{k}"]).then_inc(w_sem, 16)
            e.dma_start(bv[:], t[f"bv{k}"].partition_broadcast(P)).then_inc(w_sem, 16)
            e.dma_start(wo[:], t[f"wo{k}"].rearrange("(a r) n -> r a n", r=P)).then_inc(wo_sem, 16)
            e.dma_start(bo[:], t[f"bo{k}"].partition_broadcast(P)).then_inc(wo_sem, 16)

        def load_expert(e, ex):
            w1, w2 = (t["fw1"][ex], t["fw2"][ex]) if ex < E else (t["fws1"], t["fws2"])
            e.dma_start(stage[:, ex % 3, 0:HID], w1).then_inc(staged[ex % 3], 16)
            e.dma_start(stage[:, ex % 3, HID:2 * HID].rearrange("p (i n) -> p i n", i=HT),
                        w2.rearrange("(i p) n -> p i n", p=P)).then_inc(staged[ex % 3], 16)

        block = ctx.enter_context(nc.Block())

        @block.sync
        def _(sp):
            for g in range(NG):
                sp.dma_start(x[:, 4 * g:4 * g + 4, :],
                             t["x"].rearrange("b (t p) d -> p (b t) d", p=P)[:, 4 * g:4 * g + 4, :]).then_inc(loads[f"x{g}"], 16)
                if g == 1:
                    for dst, name in ((ident, "ident"), (ident16, "ident16"), (mrows, "mrows"), (iota, "iota"), (ln_sb, "ln_sb")):
                        sp.dma_start(dst[:], t[name]).then_inc(loads["const"], 16)
            load_attention(sp, "a", loads["wa"], loads["woa"])
            for ex in range(3):
                load_expert(sp, ex)
            sp.dma_start(gw[:], t["gw"]).then_inc(loads["gate"], 16)
            sp.dma_start(gb[:], t["gb"].partition_broadcast(P)).then_inc(loads["gate"], 16)
            sp.dma_start(fb1[:], t["fb1"]).then_inc(loads["ffn"], 16)
            sp.dma_start(mw1[:], t["mw1"]).then_inc(loads["mlp"], 16)
            sp.dma_start(mw2[:], t["mw2"].rearrange("(i p) n -> p i n", p=P)).then_inc(loads["mlp"], 16)
            sp.dma_start(mb1[:], t["mb1"]).then_inc(loads["mlp"], 16)
            sp.dma_start(mb2[:], t["mb2"].partition_broadcast(P)).then_inc(loads["mlp"], 16)
            attn_a.sp(sp)
            for r in range(2):
                sp.dma_start(fb2[r:r + 1, :], t["fb2"]).then_inc(loads["ffn"], 16)
            for ex in range(3, NE):
                sp.wait_ge(w_lo, 2 * (ex - 2))
                load_expert(sp, ex)
            sp.wait_ge(attn_a.y_added, Attention.Y_DONE)
            load_attention(sp, "b", loads["wb"], loads["wob"])
            attn_b.sp(sp)
            for g in range(NG):
                sp.wait_ge(*moe2.x_ready(g))
                sp.dma_start(out.rearrange("b (t p) d -> p (b t) d", p=P)[:, 4 * g:4 * g + 4, :],
                             x[:, 4 * g:4 * g + 4, :]).then_inc(stored, 16)
            sp.wait_ge(stored, 16 * NG)

        @block.gpsimd
        def _(pool):
            nc.gpsimd.memset(ones[:], 1.0).then_inc(const_ready, 1)
            pool.wait_ge(const_ready, 1)
            nc.gpsimd.memset(spare[:], 0.0).then_inc(const_ready, 1)
            pool.wait_ge(const_ready, 2)
            nc.gpsimd.memset(ones16[:], 1.0).then_inc(const_ready, 1)
            pool.wait_ge(const_ready, 3)
            for b in range(B):
                nc.gpsimd.memset(heads[b][HD:HD + 1, :, KB, :], 1.0).then_inc(rows_ready, 1)
                pool.wait_ge(rows_ready, b + 1)
            attn_a.pool(pool)
            pool.wait_ge(moe1.down, Moe.NK)
            for b in range(B):
                nc.gpsimd.memset(heads[b][HD:HD + 1, :, KB, :], 1.0).then_inc(rows_ready, 1)
                pool.wait_ge(rows_ready, B + b + 1)
            attn_b.pool(pool)

        @block.scalar
        def _(act):
            for g in (0, 1):
                norm_a.act_root(act, g)
            for g in (0, 1):
                norm_a.act_root2(act, g)
            for g in (2, 3):
                norm_a.act_root(act, g)
            for g in (2, 3):
                norm_a.act_root2(act, g)
            act.wait_ge(loads["const"], 16 * 5)
            turn_a.act(act, 0)
            turn_a.act(act, 1)
            attn_a.act_weights(act)
            attn_a.act(act)
            norm_m.act_root(act, 2)
            turn_m.act(act, 0)
            turn_m.act(act, 1)
            mlp.act(act, 0)
            mlp.act(act, 1)
            turn_m.act(act, 2)
            mlp.act(act, 2)
            norm_m.act_root(act, 3)
            norm_f1.act_root(act, 0)
            norm_f1.act_root(act, 1)
            turn_m.act(act, 3)
            mlp.act(act, 3)
            norm_f1.act_root(act, 2)
            turn_f1.act(act, 0)
            turn_f1.act(act, 1)
            norm_f1.act_root(act, 3)
            act.wait_ge(loads["ffn"], 16 * 3)
            moe1.act_offsets(act, 0)
            moe1.act_chunk(act, 0, 0)
            turn_f1.act(act, 2)
            turn_f1.act(act, 3)
            moe1.act_chunk(act, 0, 1)
            moe1.act_gate(act)

            def after(c):
                if c >= 2:
                    norm_b.act_root(act, c - 2)

            moe1.act(act, lambda: attn_b.act_weights(act), after)
            turn_b.act(act, 0)
            turn_b.act(act, 1)
            norm_b.act_root(act, 2)
            norm_b.act_root(act, 3)
            attn_b.act(act)
            turn_f2.act(act, 0)
            turn_f2.act(act, 1)
            norm_f2.act_root(act, 2)
            act.wait_ge(attn_b.summed, 14 * NIT)
            moe2.act_offsets(act, 0)
            moe2.act_chunk(act, 0, 0)
            turn_f2.act(act, 2)
            norm_f2.act_root(act, 3)
            turn_f2.act(act, 3)
            moe2.act_chunk(act, 0, 1)
            moe2.act_gate(act)
            moe2.act(act, nothing, nothing)

        @block.vector
        def _(dve):
            for pair_of_groups in ((0, 1), (2, 3)):
                for g in pair_of_groups:
                    norm_a.dve_stats(dve, g)
                for g in pair_of_groups:
                    norm_a.dve_norm(dve, g)
                    norm_a.dve_stats2(dve, g)
                for g in pair_of_groups:
                    norm_a.dve_norm2(dve, g)
            turn_a.dve(dve, 0)
            turn_a.dve(dve, 1)
            attn_a.dve_weights(dve)
            attn_a.dve(dve)
            norm_m.dve_stats(dve, 2)
            mlp.dve_h(dve, 0)
            mlp.dve_h(dve, 1)
            attn_a.dve_last_normalise(dve)
            norm_m.dve_norm(dve, 2)
            mlp.dve_h(dve, 2)
            attn_a.dve_last_y(dve)
            norm_m.dve_stats(dve, 3)
            mlp.dve_h(dve, 3)
            for g in (0, 1):
                mlp.dve_down(dve, g)
                norm_f1.dve_stats(dve, g)
            norm_m.dve_norm(dve, 3)
            norm_f1.dve_norm(dve, 0)
            norm_f1.dve_norm(dve, 1)
            mlp.dve_down(dve, 2)
            norm_f1.dve_stats(dve, 2)
            mlp.dve_down(dve, 3)
            norm_f1.dve_stats(dve, 3)
            norm_f1.dve_norm(dve, 2)
            turn_f1.dve(dve, 0)
            turn_f1.dve(dve, 1)
            norm_f1.dve_norm(dve, 3)
            moe1.dve_split(dve, 0, 0, True)
            turn_f1.dve(dve, 2)
            turn_f1.dve(dve, 3)
            moe1.dve_gate(dve)

            def after(c):
                norm_b.dve_stats(dve, c)
                if c >= 1:
                    norm_b.dve_norm(dve, c - 1)

            moe1.dve(dve, lambda: attn_b.dve_weights(dve), after)
            turn_b.dve(dve, 0)
            turn_b.dve(dve, 1)
            norm_b.dve_norm(dve, 3)
            attn_b.dve(dve)
            norm_f2.dve_stats(dve, 2)
            turn_f2.dve(dve, 0)
            turn_f2.dve(dve, 1)
            attn_b.dve_last_normalise(dve)
            norm_f2.dve_norm(dve, 2)
            attn_b.dve_last_y(dve)
            norm_f2.dve_stats(dve, 3)
            moe2.dve_split(dve, 0, 0, True)
            norm_f2.dve_norm(dve, 3)
            turn_f2.dve(dve, 2)
            turn_f2.dve(dve, 3)
            moe2.dve_gate(dve)
            moe2.dve(dve, nothing, nothing)

        @block.tensor
        def _(pe):
            pe.wait_ge(loads["const"], 16 * 5)
            pe.wait_ge(const_ready, 3)
            turn_a.pe(pe, 0)
            turn_a.pe(pe, 1)
            pe.wait_ge(rows_ready, 2)
            attn_a.pe(pe)
            turn_m.pe(pe, 0)
            turn_m.pe(pe, 1)
            mlp.pe_up(pe, 0)
            mlp.pe_up(pe, 1)
            attn_a.pe_last_sums(pe)
            turn_m.pe(pe, 2)
            mlp.pe_up(pe, 2)
            mlp.pe_down(pe, 0)
            attn_a.pe_last_y(pe)
            mlp.pe_down(pe, 1)
            mlp.pe_down(pe, 2)
            turn_m.pe(pe, 3)
            mlp.pe_up(pe, 3)
            turn_f1.pe(pe, 0)
            mlp.pe_down(pe, 3)
            turn_f1.pe(pe, 1)
            pe.wait_ge(w_lo, 2 * NE)
            pe.wait_ge(turn_f1.lo, 1)
            moe1.pe_up(pe, 0, 0, True)
            turn_f1.pe(pe, 2)
            turn_f1.pe(pe, 3)
            moe1.pe_gate(pe)

            def after(c):
                if c >= 2:
                    turn_b.pe(pe, c - 2)

            moe1.pe(pe, after)
            pe.wait_ge(rows_ready, 4)
            attn_b.pe(pe)
            turn_f2.pe(pe, 0)
            turn_f2.pe(pe, 1)
            pe.wait_ge(turn_f2.lo, 1)
            pe.wait_ge(attn_b.y_added, 2 * NIT - 1)
            moe2.pe_up(pe, 0, 0, True)
            attn_b.pe_last_sums(pe)
            attn_b.pe_last_y(pe)
            turn_f2.pe(pe, 2)
            turn_f2.pe(pe, 3)
            moe2.pe_gate(pe)
            moe2.pe(pe, nothing)


def kernel(**inputs):
    import numpy as np
    import concourse.bacc as _bacc
    from concourse import mybir as _mybir
    from concourse.bass_utils import run_bass_kernel_spmd as _run

    a = {k.removeprefix("L0_"): np.asarray(v) for k, v in inputs.items()}

    def cols(v, *shape):
        return np.ascontiguousarray(np.moveaxis(v.reshape(*shape, 128), -1, 0))

    last, first = np.zeros(128, np.float32), np.zeros(128, np.float32)
    first[0] = last[127] = MASK * float(D) ** 0.5
    arrays = {
        "x": a["attn_a_x"],
        "ident": np.eye(128, dtype=np.float32), "ident16": np.eye(128, dtype=np.float16),
        "mrows": np.stack([first, last])[None], "iota": np.tile(np.arange(E, dtype=np.float32), (128, 1)),
        "ln_sb": np.stack([np.stack([a[f"attn_a_ln{k}_{p}"] for p in "sb"], -1) for k in "qkvm"], 1),
        "wa": np.stack([a[f"attn_a_W{k}"] for k in "qkv"]),
        "bqka": np.stack([cols(a[f"attn_a_b{k}"], 8) for k in "qk"], 1),
        "bva": a["attn_a_bv"], "woa": a["attn_a_Wo"], "boa": a["attn_a_bo"],
        "wb": np.stack([a[f"attn_b_W_{k}"].transpose(2, 0, 1).reshape(128, 1024) for k in "QKV"]),
        "bqkb": np.stack([cols(a[f"attn_b_b_{k}"], 8) for k in "QK"], 1),
        "bvb": a["attn_b_b_V"].reshape(-1), "wob": a["attn_b_W_O"].transpose(0, 2, 1).reshape(1024, 128),
        "bob": a["attn_b_b_O"],
        "mw1": a["attn_a_W1"], "mw2": a["attn_a_W2"], "mb1": cols(a["attn_a_b1"], 2), "mb2": a["attn_a_b2"],
        "gw": a["ffn_gate_w"], "gb": a["ffn_gate_b"],
        "fw1": a["ffn_w1"], "fws1": a["ffn_ws1"], "fw2": a["ffn_w2"], "fws2": a["ffn_ws2"],
        "fb1": np.concatenate([cols(a["ffn_b1"], 8, 4), cols(a["ffn_bs1"], 1, 4)], 1),
        "fb2": np.concatenate([a["ffn_b2"], a["ffn_bs2"][None]]).reshape(1, -1),
    }
    nc = _bacc.Bacc("TRN2", target_bir_lowering=False, num_devices=1)
    feeds, aps = {}, {}
    for name, v in arrays.items():
        v = np.ascontiguousarray(v)
        feeds[f"in_{name}"] = v
        aps[name] = nc.dram_tensor(f"in_{name}", v.shape, _mybir.dt.from_np(v.dtype), kind="ExternalInput").ap()
    out = nc.dram_tensor("out_0", (B, S, D), _mybir.dt.float32, kind="ExternalOutput").ap()
    build(nc, aps, out)
    r = _run(nc, [feeds], core_ids=[0])
    return r.results[0]["out_0"]
```

```python
from contextlib import ExitStack

import concourse.bass as bass
from concourse import mybir

F32 = mybir.dt.float32
F16 = mybir.dt.float16
U32 = mybir.dt.uint32
ALU = mybir.AluOpType
ACT = mybir.ActivationFunctionType
AX = mybir.AxisListType

P = 128
B, S, D = 2, 1024, 128
TOK = B * S
NT = TOK // P
NG = TOK // 512
H, HD = 16, 64
PAIRS = H // 2
NIT = PAIRS * B
KT = S // P
NC = S // 512
U = NC * KT
E, HID = 8, 512
NE = E + 1
HT = HID // P
WS = 64.0
EPS = 1e-5
MASK = -999.0
SCALE_A = float(D) ** -0.5
SCALE_B = float(HD) ** -0.5
QB, KB, KA, QA = range(4)
QH, KL, KH, QL = range(4)

NM = KT * 2

AHEAD = 11
M_STEPS = {3: 1, 4: 1, 5: 1, 6: 2, 7: 1, 8: 2, 9: 1, 10: 1, 11: 1, 12: 1, 13: 2, 14: 1, 15: 1}
M_STEPS_FIRST = {7: 1, 8: 2, 9: 2, 10: 2, 11: 2, 12: 2, 13: 2, 14: 2, 15: 1}


def extras(u, first, last):
    out = []
    lead = 4 if first else 0
    if first and u < 4:
        out += [("N", i) for i in ((AHEAD,), (AHEAD + 1,), (AHEAD + 2,), (AHEAD + 3, AHEAD + 4))[u]]
    if not last:
        if u == lead:
            out.append(("Q", 0))
        if u == lead + 1:
            out.append(("K", 0))
        if u == lead + 2:
            out.append(("V", 0))
    if not first:
        if u == 2:
            out.append(("L", 1))
        if u == 7:
            out.append(("Y", 1))
    if u == (5 if first else 3):
        out.append(("T", 1))
    if u == 10:
        out.append(("L", 0))
    if not last:
        steps = M_STEPS_FIRST if first else M_STEPS
        done = sum(n for v, n in steps.items() if v < u)
        out += [("M", done + i) for i in range(steps.get(u, 0))]
        if u == (13 if first else 10):
            out.append(("T", 0))
    if 2 <= u < 6 and not first:
        out.append(("R", 4 + u - 2))
    if 10 <= u < 14:
        out.append(("R", u - 10))
    if u == U - 1:
        out.append(("Y", 0))
    return out


PROLOGUE = [("Q", 0), ("K", 0)] + [("M", i) for i in range(NM // 2)] + [("T", 0), ("V", 0)] + \
    [("M", i) for i in range(NM // 2, AHEAD)]


def ring_of(first, last):
    return [x for u in range(U) for x in extras(u, first, last) if x[0] not in "LR"]


PRO = len(PROLOGUE)
R0 = len(ring_of(True, False))
R1 = len(ring_of(False, False))


def at(n, value):
    return isinstance(n, int) and n == value


def ring_base(n, first):
    return PRO if first else n * R1 + (PRO + R0 - R1)


def build(nc, t, out):
    with ExitStack() as ctx:
        def sb(name, shape, dt):
            return ctx.enter_context(nc.sbuf_tensor(name, shape, dt))

        def sem(name):
            return ctx.enter_context(nc.semaphore(name))

        ps = ctx.enter_context(nc.psum_tensor("ps", [P, 8, 512], F32))

        x = sb("x", [P, NT, D], F32)
        xn = sb("xn", [P, NT, D], F32)
        xs = [sb(f"xs{v}", [P, 2, TOK], F16) for v in range(3)]
        xT32 = xs[1][:].rearrange("p a n -> p (a n)").bitcast(F32)
        wh = sb("wh", [P, 3, H * HD], F16)
        wl = sb("wl", [P, 3, H * HD], F16)
        wo = sb("wo", [P, PAIRS, D], F32)
        bqk = sb("bqk", [P, 2, PAIRS], F32)
        bv = sb("bv", [P, H * HD], F32)
        bo = sb("bo", [P, D], F32)
        w1h = sb("w1h", [P, NE, HID], F16)
        w1l = sb("w1l", [P, NE, HID], F16)
        w2h = sb("w2h", [P, NE, HT * D], F16)
        w2l = sb("w2l", [P, NE, HT * D], F16)
        stage = sb("stage", [P, 3, 2 * HID], F32)
        fb2s = stage[0:2, 0, :].bitcast(F16)[:, 0:NE * D]
        fb1 = sb("fb1", [P, NE, HT], F32)
        gw = sb("gw", [P, E], F32)
        gwh = sb("gwh", [P, E], F16)
        gwl = sb("gwl", [P, E], F16)
        gb = sb("gb", [P, E], F32)
        ln_sb = sb("ln_sb", [P, 4, 2], F32)
        mw1 = sb("mw1", [P, 2 * D], F32)
        mw2 = sb("mw2", [P, 2, D], F32)
        mb1 = sb("mb1", [P, 2], F32)
        mb2 = sb("mb2", [P, D], F32)
        ident = sb("ident", [P, P], F32)
        ident16 = sb("ident16", [P, P], F16)
        ones = sb("ones", [P, P], F32)
        ones16 = sb("ones16", [P, P], F16)
        mfirst = sb("mfirst", [1, P], F16)
        iota = sb("iota", [P, E], F32)
        pair = sb("pair", [P, 4, S], F16)
        heads = [sb(f"heads{b}", [P, 2, 4, S], F16) for b in range(2)]
        vb = [sb(f"vb{b}", [P, KT, P], F32) for b in range(2)]
        pt = sb("pt", [P, 4, 2, 512], F32)
        acc = sb("acc", [P, NC, 2, 512], F32)
        f = sb("f", [P, 2, S], F32)
        ou = sb("ou", [P, NC, 512], F32)
        att = sb("att", [P, NC, 512], F32)
        mxp = sb("mxp", [P, KT, 2, 2], F32)
        mtmp = sb("mtmp", [P, NC, 4, 2], F32)
        mneg = sb("mneg", [P, NC, 2, 4], F16)
        mrow = sb("mrow", [8, NC, P], F16)
        spare = sb("spare", [P, 4], F32)
        now_b1 = sb("now_b1", [P, HT], F32)
        st = sb("st", [P, NT, 6], F32)
        mv = sb("mv", [P, NT, 2], F32)
        var = sb("var", [P, NT], F32)
        std = sb("std", [P, NT], F32)
        rstd = sb("rstd", [P, NT], F32)
        var2 = sb("var2", [P, NT], F32)
        std2 = sb("std2", [P, NT], F32)
        rstd2 = sb("rstd2", [P, NT], F32)
        ix8 = sb("ix8", [P, NT, 8], U32)
        ixf = sb("ixf", [P, NT, 2], F32)
        gd = sb("gd", [P, NT], F32)
        ge = sb("ge", [P, NT], F32)
        gden = sb("gden", [P, NT], F32)
        g1 = sb("g1", [P, NT], F32)
        g2 = sb("g2", [P, NT], F32)

        fb2 = f[0:2].rearrange("p a n -> p (a n)")[:, 0:NE * D]
        fb2h = pair[0:2].rearrange("p a n -> p (a n)")[:, 0:NE * D]
        att_flat = att[:].rearrange("p c n -> p (c n)")

        def gate_buffer(at, *shape):
            size = shape[0] * shape[1] * (shape[2] if len(shape) > 2 else 1)
            names = "abc"[:len(shape)]
            return att_flat[:, at:at + size].rearrange(f"p ({' '.join(names)}) -> p {' '.join(names)}",
                                                       **dict(zip(names, shape)))

        lg = gate_buffer(0, NT, E)
        mx8 = gate_buffer(NT * E, NT, 8)
        eq = gate_buffer(2 * NT * E, 2, NT, E)
        comb = gate_buffer(4 * NT * E, E, NT)
        combs = gate_buffer(5 * NT * E, E, NT)
        pt_flat = pt[:].rearrange("p a b n -> p (a b n)")
        tmp_tok = pt_flat[:, 0:NT * D].rearrange("p (t d) -> p t d", t=NT)
        tmp_m = xs[2][:].rearrange("p a n -> p (a n)").bitcast(F32).rearrange("p (t d) -> p t d", t=NT)
        h1T = heads[1][:].rearrange("p a b n -> p (a b n)").bitcast(F32).rearrange("p (i n) -> p i n", i=2)
        h32 = pt_flat.rearrange("p (r n) -> p r n", r=8)
        hsplit = [heads[b][:].rearrange("p a b n -> p (a b n)")[:, 0:2 * HT * 512]
                  .rearrange("p (s i n) -> p s i n", s=2, i=HT) for b in range(2)]

        loads = {}

        def load_sem(name):
            loads[name] = sem("ld_" + name)
            return loads[name]

        for name in ("mask", "x0", "x1", "x2", "x3", "const", "ln", "wa", "woa", "mlp", "ffn", "gate", "wb", "wob"):
            load_sem(name)
        staged = [sem(f"staged{i}") for i in range(3)]
        w_hi = sem("w_hi")
        w_lo = sem("w_lo")
        small_hi = sem("small_high")
        small_lo = sem("small_low")
        stored = sem("stored")
        const_ready = sem("const_ready")
        rows_ready = sem("rows_ready")

        class Norm:
            STEPS = 14

            def __init__(self, name, src, dst, before, twice=None):
                self.src, self.dst, self.before, self.twice = src, dst, before, twice
                self.stats = sem(name + "_norm_stats")
                self.root = sem(name + "_norm_root")
                self.done = sem(name + "_norm_done")
                if twice is not None:
                    self.var2 = sem(name + "_norm_var2")
                    self.root2 = sem(name + "_norm_root2")
                    self.done2 = sem(name + "_norm_done2")

            def out(self):
                return self.dst if self.twice is None else self.twice

            def tile_done(self, i):
                return (self.done if self.twice is None else self.done2), 5 * (i // 4) + i % 4 + 2

            def dve_stats(self, e, g):
                e.wait_ge(*self.before[g])
                for i in range(4 * g, 4 * g + 4):
                    nc.vector.bn_stats(st[:, i, :], self.src[:, i, :]).then_inc(self.stats, 1)
                e.wait_ge(self.stats, 9 * g + 4)
                for i in range(4 * g, 4 * g + 4):
                    nc.vector.bn_aggr(mv[:, i, :], st[:, i, :]).then_inc(self.stats, 1)
                e.wait_ge(self.stats, 9 * g + 8)
                r = slice(4 * g, 4 * g + 4)
                nc.vector.tensor_scalar(var[:, r], mv[:, r, 1], EPS, None, ALU.add).then_inc(self.stats, 1)

            def act_root(self, e, g):
                e.wait_ge(self.stats, 9 * g + 9)
                nc.scalar.activation(std[:, 4 * g:4 * g + 4], var[:, 4 * g:4 * g + 4], ACT.Sqrt).then_inc(self.root, 1)

            def dve_norm(self, e, g):
                e.wait_ge(self.root, g + 1)
                nc.vector.reciprocal(rstd[:, 4 * g:4 * g + 4], std[:, 4 * g:4 * g + 4]).then_inc(self.done, 1)
                e.wait_ge(self.done, 5 * g + 1)
                for i in range(4 * g, 4 * g + 4):
                    nc.vector.tensor_scalar(self.dst[:, i, :], self.src[:, i, :], mv[:, i, 0:1], rstd[:, i:i + 1],
                                            ALU.subtract, ALU.mult).then_inc(self.done, 1)

            def dve_stats2(self, e, g):
                r = slice(4 * g, 4 * g + 4)
                nc.vector.tensor_tensor(var2[:, r], mv[:, r, 1], rstd[:, r], ALU.mult).then_inc(self.var2, 1)
                e.wait_ge(self.var2, 3 * g + 1)
                nc.vector.tensor_tensor(var2[:, r], var2[:, r], rstd[:, r], ALU.mult).then_inc(self.var2, 1)
                e.wait_ge(self.var2, 3 * g + 2)
                nc.vector.tensor_scalar(var2[:, r], var2[:, r], EPS, None, ALU.add).then_inc(self.var2, 1)

            def act_root2(self, e, g):
                e.wait_ge(self.var2, 3 * g + 3)
                nc.scalar.activation(std2[:, 4 * g:4 * g + 4], var2[:, 4 * g:4 * g + 4], ACT.Sqrt).then_inc(self.root2, 1)

            def dve_norm2(self, e, g):
                e.wait_ge(self.root2, g + 1)
                nc.vector.reciprocal(rstd2[:, 4 * g:4 * g + 4], std2[:, 4 * g:4 * g + 4]).then_inc(self.done2, 1)
                e.wait_ge(self.done2, 5 * g + 1)
                e.wait_ge(self.done, 5 * g + 5)
                for i in range(4 * g, 4 * g + 4):
                    nc.vector.tensor_scalar(self.twice[:, i, :], self.dst[:, i, :], rstd2[:, i:i + 1], None,
                                            ALU.mult).then_inc(self.done2, 1)

        class Turn:

            def __init__(self, name, norm, variants, banks, free=None, scratch=(), uses=range(4)):
                self.norm, self.variants, self.banks = norm, variants, banks
                self.free = free or {}
                self.scratch = list(scratch) + [f[:, q // 2, 512 * (q % 2):512 * (q % 2) + 512] for q in range(4)]
                self.uses = list(uses)
                self.n = len(variants)
                self.full = sem(name + "_turned")
                self.hi = sem(name + "_high")
                self.f32 = sem(name + "_affine")
                self.lo = sem(name + "_low")
                self.split = any(v[3] is not None for v in variants)

            def number(self, g, v):
                return (g // 2) * 2 * self.n + 2 * v + g % 2

            def ready(self, g, v=-1):
                return (self.lo if self.split else self.f32), self.number(g, v % self.n) + 1

            def out32(self, g, v):
                if self.variants[v][2] is not None:
                    return self.variants[v][2][:, 512 * g:512 * g + 512]
                return self.scratch[self.uses[self.number(g, v)]]

            def pe(self, e, g):
                if g in self.free:
                    e.wait_ge(*self.free[g])
                before = [k for k in range(g) if self.banks[k] == self.banks[g]]
                if before:
                    e.wait_ge(self.f32, self.number(before[-1], self.n - 1) + 1)
                for i in range(4):
                    e.wait_ge(*self.norm.tile_done(4 * g + i))
                    last = nc.tensor.transpose(ps[:, self.banks[g], P * i:P * i + P], self.norm.out()[:, 4 * g + i, :], ident[:])
                last.then_inc(self.full, 1)

            def act(self, e, g, v=0):
                scale, offset, out32, split = self.variants[v]
                q = self.number(g, v)
                e.wait_ge(self.full, g + 1)
                if split is not None:
                    nc.scalar.activation(split[:, 0, 512 * g:512 * g + 512], ps[:, self.banks[g], :], ACT.Identity,
                                         bias=offset, scale=scale).then_inc(self.hi, 1)
                before = [k for k in range(q) if out32 is None and self.uses[k] == self.uses[q]]
                if before:
                    e.wait_ge(self.lo, before[-1] + 1)
                nc.scalar.activation(self.out32(g, v), ps[:, self.banks[g], :], ACT.Identity,
                                     bias=offset, scale=scale).then_inc(self.f32, 1)

            def dve(self, e, g, v=0):
                split = self.variants[v][3]
                q = self.number(g, v)
                hi, lo = (split[:, k, 512 * g:512 * g + 512] for k in range(2))
                e.wait_ge(self.hi, q + 1)
                e.wait_ge(self.f32, q + 1)
                nc.vector.tensor_tensor(lo, self.out32(g, v), hi, ALU.subtract).then_inc(self.lo, 1)

        class Attention:

            def __init__(self, name, scale, masked, xq, xk, xv, y, turn, w_sem, wo_sem, rows, last_bank):
                self.rows, self.last_y = rows, ps[:, last_bank:last_bank + 2, :]
                self.scale, self.masked, self.x3, self.y, self.turn = scale, masked, (xq, xk, xv), y, turn
                self.beside = {}
                self.between = {}
                self.w_sem, self.wo_sem = w_sem, wo_sem

                def s(what):
                    return sem(f"{name}_{what}")

                self.wsplit_hi = s("w_high")
                self.wsplit_lo = s("w_low")
                self.y_init = s("y_init")
                self.ring_full = s("ring_full")
                self.f_ready = s("f_ready")
                self.hi_ready = s("hi_ready")
                self.lo_ready = s("lo_ready")
                self.v_ready = s("v_ready")
                self.max_ready = s("max_ready")
                self.mtmp_ready = s("mtmp_ready")
                self.mneg_ready = s("mneg_ready")
                self.mrow_ready = s("mrow_ready")
                self.assembled = s("assembled")
                self.max_rows = [s(f"max_rows{c}") for c in range(NC)]
                self.scores = s("scores")
                self.probs = s("probs")
                self.pv = s("pv")
                self.summed = s("summed")
                self.o_copied = s("o_copied")
                self.sums = s("sums")
                self.rec_ready = s("rec_ready")
                self.att_ready = s("att_ready")
                self.y_added = s("y_added")

            def freed(self, use, n):
                kind, i = use
                if kind == "Q" or kind == "K":
                    return self.f_ready, 2 * (n + 1) + (1 if kind == "Q" else 2)
                if kind == "V":
                    return self.v_ready, n + 2
                if kind == "M":
                    return self.max_ready, NM * (n + 1) + i + 1
                if kind == "N":
                    return self.max_ready, NM * n + i + 1
                if kind == "T":
                    return self.mrow_ready, (2 * (n + 1) + 1 if i == 0 else 2 * n + 2)
                if kind == "Y":
                    return self.y_added, (2 * n + 1 if i == 0 else 2 * n)
                raise ValueError(kind)

            def slot(self, number, parity):
                k = 2 * ((number + parity) % 2)
                return ps[:, k:k + 2, :]

            def pe(self, e):
                uses = PROLOGUE
                for k, use in enumerate(uses):
                    if use[0] in "QKV":
                        v = "QKV".index(use[0])
                        e.wait_ge(*self.turn.ready(1, min(v, self.turn.n - 1)))
                        e.wait_ge(self.wsplit_lo, v + 1)
                    if k >= 2:
                        e.wait_ge(*self.freed(uses[k - 2], -1))
                    self.pe_use(e, use, -1, 0, 1, k)
                    if use == ("M", 1):
                        self.turn.pe(e, 2)
                        self.turn.pe(e, 3)
                e.wait_ge(rows_ready, self.rows)
                if self.masked:
                    e.wait_ge(loads["mask"], 16 * B)
                e.wait_ge(self.turn.f32, self.turn.number(2, self.turn.n - 1) + 1)
                self.pe_iteration(e, 0, 0, 0, True, False)
                with e.Fori(0, NIT // 2 - 1) as j:
                    self.pe_iteration(e, 2 * j + 1, j, 1, False, False)
                    self.pe_iteration(e, 2 * j + 2, j + 1, 0, False, False)
                self.pe_iteration(e, NIT - 1, PAIRS - 1, 1, False, True)
                self.pe_pv(e, NIT - 1, 1, U - 1)

            def pe_last_sums(self, e):
                self.pe_sums(e, NIT, 1)

            def pe_last_y(self, e):
                self.pe_y(e, NIT, 1, self.last_y, PAIRS - 1)

            def pe_iteration(self, e, n, p, b, first, last):
                uses = ring_of(first, last)
                before = PROLOGUE if first else ring_of(at(n, 1), False)
                chain = [(x, n - 1 if not first else -1) for x in before[-2:]] + [(x, n) for x in uses]
                k = 0
                for u in range(U):
                    c, kt = divmod(u, KT)
                    if u == 0:
                        e.wait_ge(self.assembled, 96 * (n + 1))
                        e.wait_ge(self.max_rows[0], 32 * (n + 1))
                    if kt == 0 and c == 1:
                        e.wait_ge(self.max_rows[1], 32 * (n + 1))
                    for h in range(2):
                        if not (first and u == 0):
                            e.wait_ge(self.probs, 2 * U * n + 2 * u + h - 1)
                        self.pe_scores(e, b, h, c, kt)
                    uses_now = extras(u, first, last)
                    for use in uses_now:
                        if use != ("Y", 0):
                            k = self.pe_extra(e, use, n, p, b, k, chain, first)
                    if u > 0:
                        self.pe_pv(e, n, b, u - 1)
                    elif not first:
                        self.pe_pv(e, n - 1, 1 - b, U - 1)
                    if ("Y", 0) in uses_now:
                        k = self.pe_extra(e, ("Y", 0), n, p, b, k, chain, first)

            def pe_extra(self, e, use, n, p, b, k, chain, first):
                if use[0] == "L":
                    self.pe_sums(e, n, use[1])
                if use[0] in "LR":
                    return k
                if first and use == ("Q", 0):
                    e.wait_ge(*self.turn.ready(3))
                e.wait_ge(*self.freed(*chain[k]))
                self.pe_use(e, use, n, p, b, k)
                return k + 1

            def pe_use(self, e, use, n, p, b, k):
                kind, i = use
                slot = self.ring_slot(n, b, k)
                p1, b1 = p + b if not at(n, -1) else 0, 1 - b
                if kind in "QK":
                    self.pe_qk(e, "QK".index(kind), p1, b1, slot)
                elif kind == "V":
                    self.pe_v(e, p1, b1, slot)
                elif kind in "MN":
                    e.wait_ge(self.hi_ready, 2 * n + (4 if kind == "M" else 2))
                    self.pe_m(i, slot)
                elif kind == "T":
                    e.wait_ge(self.mneg_ready, 2 * (n + 1) + 1 if i == 0 else 2 * n + 2)
                    nc.tensor.transpose(slot[0:8, 0, 0:64].bitcast(F16),
                                        mneg[:, i].rearrange("p h t -> p (h t)"), ident16[:]).then_inc(self.ring_full, 1)
                elif kind == "Y":
                    self.pe_y(e, n, i, slot, p if i == 0 else p + b - 1)

            def ring_slot(self, n, b, k):
                if at(n, -1):
                    return self.slot(k, 0)
                if at(n, 0):
                    return self.slot(PRO + k, 0)
                return self.slot(PRO + R0 - R1 + k, b * R1)

            def pe_qk(self, e, which, p, b, slot):
                hi, lo = (w[:, which, bass.ds(p * P, P)] for w in (wh, wl))
                xt = self.x3[which]
                for c in range(NC):
                    cols = slice(b * S + 512 * c, b * S + 512 * c + 512)
                    nc.tensor.matmul(slot[:, c, :], hi, xt[:, 0, cols], start=True, stop=False)
                    nc.tensor.matmul(slot[:, c, :], hi, xt[:, 1, cols], start=False, stop=False)
                    last = nc.tensor.matmul(slot[:, c, :], lo, xt[:, 0, cols], start=False, stop=True)
                last.then_inc(self.ring_full, 1)

            def pe_v(self, e, p, b, slot):
                hi, lo = (w[:, 2, bass.ds(p * P, P)] for w in (wh, wl))
                for i in range(KT):
                    cols = slice(b * S + P * i, b * S + P * i + P)
                    o = slot[:, i // 4, P * (i % 4):P * (i % 4) + P]
                    nc.tensor.matmul(o, self.x3[2][:, 0, cols], hi, start=True, stop=False)
                    nc.tensor.matmul(o, self.x3[2][:, 0, cols], lo, start=False, stop=False)
                    last = nc.tensor.matmul(o, self.x3[2][:, 1, cols], hi, start=False, stop=True)
                last.then_inc(self.ring_full, 1)

            def pe_m(self, item, slot):
                i, half = divmod(item, 2)
                masked = self.masked and i == 0 and half == 1
                for h in range(2):
                    r = slice(HD * h, HD * h + HD)
                    last = nc.tensor.matmul(slot[:, h, :], pair[r, QH, P * i:P * i + P], pair[r, KH, 512 * half:512 * half + 512],
                                            start=True, stop=True)
                if masked:
                    for h in range(2):
                        last = nc.tensor.matmul(slot[:, h, 511:512], mfirst[:], ones16[0:1, 0:1], start=False, stop=True,
                                                skip_group_check=True)
                last.then_inc(self.ring_full, 1)

            def pe_scores(self, e, b, h, c, kt):
                hb = heads[b]
                keys, queries = slice(P * kt, P * kt + P), slice(512 * c, 512 * c + 512)
                o = ps[:, 4 + h, :]
                rows = HD + 3 if self.masked else HD + 1
                nc.tensor.matmul(o, hb[:, h, KA, keys], hb[:, h, QA, queries], start=True, stop=False)
                last = nc.tensor.matmul(o, hb[0:rows, h, KB, keys], hb[0:rows, h, QB, queries],
                                        start=False, stop=True)
                last.then_inc(self.scores, 1)

            def pe_pv(self, e, n, b, u):
                c, kt = divmod(u, KT)
                e.wait_ge(self.probs, 2 * U * n + 2 * u + 2)
                if u == 0:
                    e.wait_ge(self.v_ready, n + 1)
                if kt == 0 and not (at(n, 0) and c == 0):
                    e.wait_ge(self.o_copied, 2 * n + c)
                for h in range(2):
                    last = nc.tensor.matmul(ps[HD * h:HD * h + HD, 6, :], vb[b][:, kt, HD * h:HD * h + HD], pt[:, u % 4, h, :],
                                            start=(kt == 0), stop=(kt == KT - 1), skip_group_check=True)
                last.then_inc(self.pv, 1)

            def pe_sums(self, e, n, i):
                chunk = 2 * n if i == 0 else 2 * n - 1
                e.wait_ge(self.summed, 7 * chunk + 7)
                if not (at(n, 0) and i == 0):
                    e.wait_ge(self.rec_ready, 4 * chunk)
                for h in range(2):
                    last = nc.tensor.matmul(ps[HD * h:HD * h + HD, 7, :], ones[:, 0:HD], acc[:, i, h, :],
                                            start=True, stop=True, skip_group_check=True)
                last.then_inc(self.sums, 1)

            def pe_y(self, e, n, i, slot, p):
                e.wait_ge(self.att_ready, 2 * n + 1 if i == 0 else 2 * n)
                for k in range(4):
                    last = nc.tensor.matmul(slot[:, 0, P * k:P * k + P], att[:, i, P * k:P * k + P],
                                            wo[:, p, :] if isinstance(p, int) else wo[:, bass.ds(p, 1), :].rearrange("p a n -> p (a n)"),
                                            start=True, stop=True)
                last.then_inc(self.ring_full, 1)

            def act_prologue(self, e):
                for k, use in enumerate(PROLOGUE):
                    self.act_use(e, use, -1, 0, 1, k, k)
                    if ("act", use) in self.between:
                        self.between["act", use](e)

            def act(self, e):
                self.act_prologue(e)
                e.wait_ge(self.lo_ready, 2)
                for v in range(self.turn.n):
                    for g in (2, 3):
                        self.turn.act(e, g, v)
                self.act_iteration(e, 0, 0, 0, True, False)
                with e.Fori(0, NIT // 2 - 1) as j:
                    self.act_iteration(e, 2 * j + 1, j, 1, False, False)
                    self.act_iteration(e, 2 * j + 2, j + 1, 0, False, False)
                self.act_iteration(e, NIT - 1, PAIRS - 1, 1, False, True)
                self.act_copy_o(e, NIT - 1, 1)

            def act_weights(self, e, which=range(3)):
                e.wait_ge(self.w_sem, 16 * 5)
                for i in which:
                    nc.scalar.activation(wh[:, i, :], self.raw_weights(i), ACT.Copy, scale=WS).then_inc(self.wsplit_hi, 1)

            def act_iteration(self, e, n, p, b, first, last):
                k, base = 0, ring_base(n, first)
                for u in range(U):
                    self.act_exp(e, n, u, first)
                    for use in extras(u, first, last):
                        if use[0] not in "LR":
                            self.act_use(e, use, n, p, b, k, base + k)
                            k += 1
                    if u == 0 and not first:
                        self.act_copy_o(e, n - 1, 1)
                    if u == KT:
                        self.act_copy_o(e, n, 0)
                    if last and ("act", u) in self.beside:
                        self.beside["act", u](e)

            def act_exp(self, e, n, u, first):
                if not (first and u < 4):
                    e.wait_ge(self.pv, U * n + u - 3)
                    if u >= 4:
                        c, kt = divmod(u - 4, KT)
                        e.wait_ge(self.summed, 14 * n + 7 * c + max(kt, 1))
                    else:
                        e.wait_ge(self.summed, 14 * n - 14 + 7 + U // 2 - 4 + u)
                for h in range(2):
                    e.wait_ge(self.scores, 2 * U * n + 2 * u + h + 1)
                    nc.scalar.activation(pt[:, u % 4, h, :], ps[:, 4 + h, :], ACT.Exp,
                                         scale=self.scale).then_inc(self.probs, 1)

            def act_use(self, e, use, n, p, b, k, number):
                kind, _ = use
                if kind not in "QK":
                    return
                slot = self.ring_slot(n, b, k)
                which = "QK".index(kind)
                p1 = p + b if not at(n, -1) else 0
                e.wait_ge(self.ring_full, number + 1)
                if not at(n, -1):
                    e.wait_ge(self.lo_ready, 2 * n + which + 1)
                offset = bqk[:, which, p1:p1 + 1] if isinstance(p1, int) else bqk[:, which, bass.ds(p1, 1)]
                if not at(n, -1):
                    e.wait_ge(self.assembled, 96 * (n + 1))
                if not isinstance(p1, int):
                    nc.scalar.copy(spare[:, 1 + which:2 + which], spare[:, 0:1])
                hi = pair[:, (QH, KH)[which], :]
                nc.scalar.activation(hi.rearrange("p (a n) -> p a n", a=2), slot, ACT.Identity,
                                     bias=offset, scale=1.0 / WS).then_inc(self.hi_ready, 1)
                nc.scalar.activation(f[:, which, :].rearrange("p (a n) -> p a n", a=2), slot, ACT.Identity,
                                     bias=offset, scale=1.0 / WS).then_inc(self.f_ready, 1)

            def act_copy_o(self, e, n, c):
                e.wait_ge(self.pv, U * n + KT * c + KT)
                if c == 1:
                    e.wait_ge(self.att_ready, 2 * n + 1)
                elif not at(n, 0):
                    e.wait_ge(self.att_ready, 2 * n - 1)
                nc.scalar.activation(ou[:, c, :], ps[:, 6, :], ACT.Copy).then_inc(self.o_copied, 1)

            def dve_weights(self, e, which=range(3)):
                for i in which:
                    e.wait_ge(self.wsplit_hi, i + 1)
                    nc.vector.scalar_tensor_tensor(out=wl[:, i, :], in0=self.raw_weights(i), scalar=WS, in1=wh[:, i, :],
                                                   op0=ALU.mult, op1=ALU.subtract).then_inc(self.wsplit_lo, 1)

            def dve(self, e):
                for k, use in enumerate(PROLOGUE):
                    self.dve_use(e, use, -1, 0, 1, k, k)
                    if ("dve", use) in self.between:
                        self.between["dve", use](e)
                for v in range(self.turn.n):
                    for g in (2, 3):
                        self.turn.dve(e, g, v)
                e.wait_ge(self.wo_sem, 32)
                y = self.y
                nc.vector.tensor_tensor(y[:], y[:], bo[:].rearrange("p (a n) -> p a n", a=1).broadcast_to([P, NT, D]),
                                        ALU.add).then_inc(self.y_init, 1)
                self.dve_iteration(e, 0, 0, 0, True, False)
                with e.Fori(0, NIT // 2 - 1) as j:
                    self.dve_iteration(e, 2 * j + 1, j, 1, False, False)
                    self.dve_iteration(e, 2 * j + 2, j + 1, 0, False, False)
                self.dve_iteration(e, NIT - 1, PAIRS - 1, 1, False, True)

            def dve_last_normalise(self, e):
                for piece in range(4):
                    self.dve_normalise(e, NIT, 1, piece)

            def dve_last_y(self, e):
                self.dve_add_y(e, NIT, 1, 1, self.last_y, NIT * R1 + (PRO + R0 - R1) - self.ahead + 1)

            ahead = R1 - len(ring_of(False, True))

            def raw_weights(self, i):
                return (acc[:, 0].rearrange("p h n -> p (h n)"), acc[:, 1].rearrange("p h n -> p (h n)"),
                        ou[:].rearrange("p c n -> p (c n)"))[i]

            def dve_iteration(self, e, n, p, b, first, last):
                k, base = 0, ring_base(n, first)
                for u in range(U):
                    for use in extras(u, first, last):
                        if use[0] == "L":
                            continue
                        if use[0] == "R":
                            self.dve_normalise(e, n, *divmod(use[1], 4))
                            continue
                        self.dve_use(e, use, n, p, b, k, base + k)
                        k += 1
                    if last and ("dve", u) in self.beside:
                        self.beside["dve", u](e)

            def dve_use(self, e, use, n, p, b, k, number):
                kind, i = use
                slot = self.ring_slot(n, b, k)
                if kind in "QK":
                    which = "QK".index(kind)
                    done = 2 * (n + 1) + which + 1
                    hi, lo = (pair[:, s, :] for s in ((QH, QL), (KH, KL))[which])
                    e.wait_ge(self.f_ready, done)
                    nc.vector.tensor_tensor(lo, f[:, which, :], hi, ALU.subtract).then_inc(self.lo_ready, 1)
                    return
                e.wait_ge(self.ring_full, number + 1)
                if kind == "V":
                    b1, p1 = 1 - b, (p + b if not at(n, -1) else 0)
                    if not at(n, -1) and not at(n, 0):
                        e.wait_ge(self.pv, U * n)
                    offset = bv[:, p1 * P:p1 * P + P] if isinstance(p1, int) else bv[:, bass.ds(p1 * P, P)]
                    nc.vector.scalar_tensor_tensor(
                        out=vb[b1][:], in0=slot.rearrange("p a (t n) -> p (a t) n", n=P), scalar=1.0 / WS,
                        in1=offset.rearrange("p (a n) -> p a n", a=1).broadcast_to([P, KT, P]),
                        op0=ALU.mult, op1=ALU.add).then_inc(self.v_ready, 1)
                elif kind in "MN":
                    m = n + 1 if kind == "M" else n
                    t_, half = divmod(i, 2)
                    nc.vector.tensor_reduce(mxp[:, t_, :, half], slot, AX.X, ALU.max).then_inc(self.max_ready, 1)
                    if t_ % 4 == 3 and half == 1:
                        c = t_ // 4
                        e.wait_ge(self.max_ready, NM * m + i + 1)
                        nc.vector.tensor_tensor(mtmp[:, c], mxp[:, 4 * c:4 * c + 4, :, 0], mxp[:, 4 * c:4 * c + 4, :, 1],
                                                ALU.max).then_inc(self.mtmp_ready, 1)
                        e.wait_ge(self.mtmp_ready, 2 * m + c + 1)
                        nc.vector.tensor_scalar(mneg[:, c].rearrange("p h t -> p t h"), mtmp[:, c], -1.0, None,
                                                ALU.mult).then_inc(self.mneg_ready, 1)
                elif kind == "T":
                    m = n + 1 if i == 0 else n
                    if not (at(m, 0)):
                        e.wait_ge(self.max_rows[i], 32 * m)
                    nc.vector.tensor_copy(mrow[:, i, :], slot[0:8, 0, 0:64].bitcast(F16)).then_inc(self.mrow_ready, 1)
                elif kind == "Y":
                    self.dve_add_y(e, n, i, b if i == 0 else 1 - b, slot, None)

            def dve_normalise(self, e, n, i, piece):
                chunk = 2 * n if i == 0 else 2 * n - 1
                if piece == 0:
                    e.wait_ge(self.sums, chunk + 1)
                cols = slice(P * piece, P * piece + P)
                nc.vector.reciprocal(att[:, i, cols], ps[:, 7, cols]).then_inc(self.rec_ready, 1)
                if piece == 3:
                    e.wait_ge(self.rec_ready, 4 * chunk + 4)
                    e.wait_ge(self.o_copied, chunk + 1)
                    nc.vector.tensor_tensor(att[:, i, :], ou[:, i, :], att[:, i, :], ALU.mult).then_inc(self.att_ready, 1)

            def dve_add_y(self, e, n, i, b, slot, full):
                if full is not None:
                    e.wait_ge(self.ring_full, full)
                done = 2 * n if i == 0 else 2 * n - 1
                if at(n, 0) and i == 0:
                    e.wait_ge(self.y_init, 1)
                else:
                    e.wait_ge(self.y_added, done)
                first = b * KT + 4 * i
                ys = self.y[:, first:first + 4, :]
                nc.vector.tensor_tensor(ys, ys, slot[:, 0, :].rearrange("p (t n) -> p t n", t=4), ALU.add)\
                    .then_inc(self.y_added, 1)

            Y_DONE = 2 * NIT

            def pool(self, e):
                e.wait_ge(self.wsplit_lo, 3)
                self.pool_iteration(e, 0)
                with e.Fori(1, NIT) as n:
                    self.pool_iteration(e, n)

            def pool_iteration(self, e, n):
                for c in range(NC):
                    if not at(n, 0):
                        e.wait_ge(self.sums, 2 * (n - 1) + c + 1)
                    for kt in range(1, KT):
                        u = KT * c + kt
                        e.wait_ge(self.probs, 2 * U * n + 2 * u + 2)
                        one = pt[:, (u - 1) % 4] if kt == 1 else acc[:, c]
                        if kt > 1:
                            e.wait_ge(self.summed, 14 * n + 7 * c + kt - 1)
                        nc.gpsimd.tensor_tensor(acc[:, c], one, pt[:, u % 4], ALU.add).then_inc(self.summed, 1)

            def sp(self, e):
                self.sp_assemble(e, 0, 0)
                self.sp_rows(e, 0, 0, 0)
                self.sp_rows(e, 0, 0, 1)
                self.sp_assemble(e, 1, 1)
                self.sp_rows(e, 1, 1, 0)
                self.sp_rows(e, 1, 1, 1)
                with e.Fori(1, NIT // 2) as j:
                    for b in range(B):
                        m = 2 * j + b
                        self.sp_assemble(e, m, b)
                        self.sp_rows(e, m, b, 0)
                        self.sp_rows(e, m, b, 1)

            def sp_assemble(self, e, m, b):
                e.wait_ge(self.lo_ready, 2 * m + 2)
                for h in range(2):
                    r = slice(HD * h, HD * h + HD)
                    for dst, src in ((heads[b][0:HD, h, QB:KA + 1, :], pair[r, QH:KH + 1, :]),
                                     (heads[b][HD:P, h, KA:QA + 1, :], pair[r, KH:QL + 1, :]),
                                     (heads[b][0:HD, h, QA, :], pair[r, QH, :])):
                        e.dma_start(dst, src).then_inc(self.assembled, 16)

            def sp_rows(self, e, m, b, c):
                e.wait_ge(self.mrow_ready, 2 * m + c + 1)
                for h in range(2):
                    e.dma_start(heads[b][HD:HD + 1, h, QB, 512 * c:512 * c + 512],
                                mrow[4 * h:4 * h + 4, c, :]).then_inc(self.max_rows[c], 16)

        class Mlp:

            def __init__(self, turn, attn):
                self.turn, self.attn = turn, attn
                self.up = sem("mlp_up")
                self.gelu = sem("mlp_gelu")
                self.down = sem("mlp_down")
                self.x_b2 = sem("mlp_x_b2")
                self.x_h = sem("mlp_x_h")
                self.x_ready = sem("mlp_x_ready")

            def pe_up(self, e, g):
                if g == 0:
                    e.wait_ge(loads["mlp"], 16 * 4)
                e.wait_ge(self.turn.f32, g + 1)
                for i in range(2):
                    k = 2 * g + i
                    if k == 0:
                        e.wait_ge(self.attn.probs, 2 * U * NIT)
                    elif k == 1:
                        e.wait_ge(self.attn.o_copied, 2 * NIT)
                    else:
                        e.wait_ge(self.gelu, k - 1)
                    nc.tensor.matmul(ps[:, 5 + k % 2, :], mw1[:, P * i:P * i + P], xT32[:, 512 * g:512 * g + 512],
                                     start=True, stop=True).then_inc(self.up, 1)

            def pe_down(self, e, g):
                e.wait_ge(self.gelu, 2 * g + 2)
                for k in range(4):
                    for i in range(2):
                        last = nc.tensor.matmul(ps[:, self.turn.banks[g], P * k:P * k + P],
                                                h1T[:, i, 512 * g + P * k:512 * g + P * k + P],
                                                mw2[:, i, :], start=(i == 0), stop=(i == 1))
                last.then_inc(self.down, 1)

            def act(self, e, g):
                for i in range(2):
                    k = 2 * g + i
                    e.wait_ge(self.up, k + 1)
                    nc.scalar.activation(h1T[:, i, 512 * g:512 * g + 512], ps[:, 5 + k % 2, :], ACT.Gelu_apprx_tanh,
                                         bias=mb1[:, i:i + 1]).then_inc(self.gelu, 1)

            def dve_b2(self, e):
                e.wait_ge(loads["mlp"], 16 * 4)
                nc.vector.tensor_tensor(x[:], x[:], mb2[:].rearrange("p (a n) -> p a n", a=1).broadcast_to([P, NT, D]),
                                        ALU.add).then_inc(self.x_b2, 1)

            def dve_h(self, e, g):
                e.wait_ge(self.x_b2, 1)
                e.wait_ge(self.attn.y_added, 2 * NIT - 3 + g)
                xg = x[:, 4 * g:4 * g + 4, :]
                nc.vector.tensor_tensor(xg, xg, xn[:, 4 * g:4 * g + 4, :], ALU.add).then_inc(self.x_h, 1)

            def dve_down(self, e, g):
                e.wait_ge(self.down, g + 1)
                e.wait_ge(self.x_h, g + 1)
                xg = x[:, 4 * g:4 * g + 4, :]
                nc.vector.tensor_tensor(xg, xg, ps[:, self.turn.banks[g], :].rearrange("p (t n) -> p t n", t=4), ALU.add)\
                    .then_inc(self.x_ready, 1)

        class Moe:

            def __init__(self, name, turn):
                self.turn = turn

                def s(what):
                    return sem(f"{name}_{what}")

                self.logits = s("logits")
                self.gate = s("gate_dve")
                self.gexp = s("gate_exp")
                self.b1_ready = s("b1_ready")
                self.up = s("up")
                self.gelu = s("gelu")
                self.hi = s("high")
                self.last_hi = s("last_high")
                self.lo = s("low")
                self.down = s("down")
                self.combined = s("combined")

            NK = NE * NG
            G_LG, G_MAX = 1, 1 + NT
            G_IDX = 1 + 2 * NT
            G_D = G_IDX + 2
            G_END = G_D + 9

            def pe_gate(self, e):
                e.wait_ge(small_lo, 2)
                for i in range(NT):
                    o = ps[:, 6, E * i:E * i + E]
                    hi, lo = (xs[0][:, k, P * i:P * i + P] for k in range(2))
                    nc.tensor.matmul(o, hi, gwh[:], start=True, stop=False)
                    nc.tensor.matmul(o, hi, gwl[:], start=False, stop=False)
                    last = nc.tensor.matmul(o, lo, gwh[:], start=False, stop=True)
                last.then_inc(self.logits, 1)

            def pe(self, e, after):
                self.pe_down(e, 0, 2)
                e.wait_ge(*self.turn.ready(NG - 1))
                self.pe_gate(e)
                self.pe_up(e, 0, 3, False)
                self.pe_up(e, 1, 0, False)
                self.pe_down(e, 0, 3)
                with e.Fori(1, NE - 1) as ex:
                    self.pe_expert(e, ex)
                for c in range(NG):
                    if c < 3:
                        self.pe_up(e, NE - 1, c + 1, False)
                    self.pe_down(e, NE - 1, c)
                    after(c)

            def pe_expert(self, e, ex):
                for c in range(NG):
                    self.pe_up(e, ex if c < NG - 1 else ex + 1, (c + 1) % NG, False)
                    self.pe_down(e, ex, c)

            def pe_up(self, e, ex, c, start):
                for i in range(HT):
                    if not start:
                        e.wait_ge(self.gelu, 16 * ex + 4 * c + i - 3)
                    if isinstance(ex, int):
                        hi, lo = (w[:, ex, P * i:P * i + P] for w in (w1h, w1l))
                    else:
                        hi, lo = (w[:].rearrange("p e n -> p (e n)")[:, bass.ds(ex * HID + P * i, P)] for w in (w1h, w1l))
                    cols = slice(512 * c, 512 * c + 512)
                    nc.tensor.matmul(ps[:, i, :], hi, xs[0][:, 0, cols], start=True, stop=False)
                    nc.tensor.matmul(ps[:, i, :], hi, xs[0][:, 1, cols], start=False, stop=False)
                    nc.tensor.matmul(ps[:, i, :], lo, xs[0][:, 0, cols], start=False, stop=True).then_inc(self.up, 1)

            def pe_down(self, e, ex, c):
                k = 4 * ex + c
                if not (at(ex, 0) and c < 2):
                    e.wait_ge(self.combined, 4 * k - 4)
                e.wait_ge(self.lo, 4 * k + 4)
                hs = hsplit[c % 2]
                for i in range(4):
                    o = ps[:, 4 + c % 2, P * i:P * i + P]
                    cols = slice(P * i, P * i + P)
                    for q in range(HT):
                        if isinstance(ex, int):
                            hi, lo = (w[:, ex, P * q:P * q + P] for w in (w2h, w2l))
                        else:
                            hi, lo = (w[:].rearrange("p e n -> p (e n)")[:, bass.ds(ex * HID + P * q, P)] for w in (w2h, w2l))
                        nc.tensor.matmul(o, hs[:, 0, q, cols], hi, start=(q == 0), stop=False)
                        nc.tensor.matmul(o, hs[:, 0, q, cols], lo, start=False, stop=False)
                        nc.tensor.matmul(o, hs[:, 1, q, cols], hi, start=False, stop=False)
                    offset = fb2s[:, ex * D:ex * D + D] if isinstance(ex, int) else fb2s[:, bass.ds(ex * D, D)]
                    last = nc.tensor.matmul(o, ones16[0:2, :], offset, start=False, stop=True)
                last.then_inc(self.down, 1)

            def act_gate(self, e):
                e.wait_ge(self.gate, self.G_D)
                nc.scalar.activation(ge[:], gd[:], ACT.Exp).then_inc(self.gexp, 1)

            def act(self, e, between, after):
                self.act_chunk(e, 0, 3)
                self.act_gate(e)
                self.act_offsets(e, 1)
                self.act_chunk(e, 1, 0)
                with e.Fori(1, NE - 2) as ex:
                    self.act_rest(e, ex)
                between()
                self.act_rest(e, NE - 2)
                after(0)
                for c in range(1, NG):
                    self.act_chunk(e, NE - 1, c, True)
                    after(c)

            def act_rest(self, e, ex):
                for c in range(1, NG):
                    self.act_chunk(e, ex, c)
                self.act_offsets(e, ex + 1)
                self.act_chunk(e, ex + 1, 0, at(ex, NE - 2))

            def act_offsets(self, e, ex):
                if at(ex, 0):
                    nc.scalar.copy(now_b1[:], fb1[:, 0, :]).then_inc(self.b1_ready, 1)
                else:
                    e.wait_ge(self.gelu, 16 * ex)
                    nc.scalar.copy(spare[:, 3:4], spare[:, 0:1])
                    src = fb1[:, ex, :] if isinstance(ex, int) else \
                        fb1[:].rearrange("p e n -> p (e n)")[:, bass.ds(ex * HT, HT)]
                    nc.scalar.copy(now_b1[:], src).then_inc(self.b1_ready, 1)
                e.wait_ge(self.b1_ready, ex + 1)

            def act_chunk(self, e, ex, c, high=False):
                for i in range(HT):
                    k = 4 * c + i
                    if not (at(ex, 0) and k < 8):
                        e.wait_ge(self.lo, 16 * ex + k - 7)
                    e.wait_ge(self.up, 16 * ex + k + 1)
                    if high:
                        if i == 0:
                            e.wait_ge(self.down, 4 * ex + c - 1)
                        nc.scalar.activation(hsplit[c % 2][:, 0, i, :], ps[:, i, :], ACT.Gelu, bias=now_b1[:, i:i + 1],
                                             scale=1.0 / WS).then_inc(self.last_hi, 1)
                    nc.scalar.activation(h32[:, k % 8, :], ps[:, i, :], ACT.Gelu, bias=now_b1[:, i:i + 1], scale=1.0 / WS)\
                        .then_inc(self.gelu, 1)

            def dve(self, e, between, after):
                self.dve_combine(e, 0, 1)
                self.dve_gate(e)
                self.dve_split(e, 0, 3, False)
                self.dve_combine(e, 0, 2)
                self.dve_split(e, 1, 0, False)
                self.dve_combine(e, 0, 3)
                self.dve_gate_weights(e)
                with e.Fori(1, NE - 2) as ex:
                    self.dve_expert(e, ex)
                between()
                self.dve_expert(e, NE - 2)
                for c in range(NG):
                    if c < 3:
                        self.dve_split(e, NE - 1, c + 1, False)
                    self.dve_combine(e, NE - 1, c)
                    after(c)

            def x_ready(self, g):
                return self.combined, 4 * (self.NK - NG + g + 1)

            def dve_gate(self, e):
                g = self.gate
                e.wait_ge(self.logits, 1)
                nc.vector.scalar_tensor_tensor(out=lg[:], in0=ps[:, 6, 0:NT * E].rearrange("p (t e) -> p t e", t=NT),
                                               scalar=1.0 / WS,
                                               in1=gb[:].rearrange("p (a e) -> p a e", a=1).broadcast_to([P, NT, E]),
                                               op0=ALU.mult, op1=ALU.add).then_inc(g, 1)
                e.wait_ge(g, self.G_LG)
                for i in range(NT):
                    nc.vector.max(mx8[:, i, :], lg[:, i, :]).then_inc(g, 1)
                e.wait_ge(g, self.G_MAX)
                for i in range(NT):
                    nc.vector.max_index(ix8[:, i, :], mx8[:, i, :], lg[:, i, :]).then_inc(g, 1)
                e.wait_ge(g, self.G_IDX)
                nc.vector.tensor_copy(ixf[:], ix8[:, :, 0:2]).then_inc(g, 1)
                nc.vector.tensor_tensor(gd[:], mx8[:, :, 1], mx8[:, :, 0], ALU.subtract).then_inc(g, 1)

            def dve_gate_weights(self, e):
                g = self.gate
                e.wait_ge(self.gexp, 1)
                n = self.G_D
                nc.vector.tensor_scalar(gden[:], ge[:], 1.0, None, ALU.add).then_inc(g, 1)
                e.wait_ge(g, n + 1)
                nc.vector.reciprocal(g1[:], gden[:]).then_inc(g, 1)
                e.wait_ge(g, n + 2)
                nc.vector.tensor_tensor(g2[:], ge[:], g1[:], ALU.mult).then_inc(g, 1)
                e.wait_ge(g, n + 3)
                io = iota[:].rearrange("p (a e) -> p a e", a=1).broadcast_to([P, NT, E])
                for k in range(2):
                    nc.vector.tensor_tensor(eq[:, k], io, ixf[:, :, k:k + 1].broadcast_to([P, NT, E]), ALU.is_equal).then_inc(g, 1)
                e.wait_ge(g, n + 5)
                for k, w in enumerate((g1, g2)):
                    nc.vector.tensor_tensor(eq[:, k], eq[:, k], w[:].rearrange("p (t a) -> p t a", a=1).broadcast_to([P, NT, E]),
                                            ALU.mult).then_inc(g, 1)
                e.wait_ge(g, n + 7)
                nc.vector.tensor_tensor(comb[:].rearrange("p e t -> p t e"), eq[:, 0], eq[:, 1], ALU.add).then_inc(g, 1)
                e.wait_ge(g, n + 8)
                nc.vector.tensor_scalar(combs[:], comb[:], 1.0 / WS, None, ALU.mult).then_inc(g, 1)
                e.wait_ge(g, self.G_END)

            def dve_expert(self, e, ex):
                for c in range(NG):
                    self.dve_split(e, ex if c < NG - 1 else ex + 1, (c + 1) % NG, False)
                    self.dve_combine(e, ex, c)

            def dve_split(self, e, ex, c, start):
                hs = hsplit[c % 2]
                if not (start or (at(ex, 0) and c < 2)):
                    e.wait_ge(self.down, 4 * ex + c - 1)
                for i in range(HT):
                    n = 16 * ex + 4 * c + i + 1
                    src = h32[:, (4 * c + i) % 8, :]
                    e.wait_ge(self.gelu, n)
                    if at(ex, NE - 1):
                        e.wait_ge(self.last_hi, 4 * c + i + 1)
                    else:
                        nc.vector.tensor_copy(hs[:, 0, i, :], src).then_inc(self.hi, 1)
                        e.wait_ge(self.hi, n)
                    nc.vector.tensor_tensor(hs[:, 1, i, :], src, hs[:, 0, i, :], ALU.subtract).then_inc(self.lo, 1)

            def dve_combine(self, e, ex, c):
                k = 4 * ex + c
                e.wait_ge(self.down, k + 1)
                if not (at(ex, 0)):
                    e.wait_ge(self.combined, 4 * (k - 3))
                for i in range(4):
                    tile = 4 * c + i
                    if at(ex, 0):
                        w = 1.0 / WS
                    elif isinstance(ex, int):
                        w = combs[:, ex - 1, tile:tile + 1]
                    else:
                        w = combs[:].rearrange("p e t -> p (e t)")[:, bass.ds((ex - 1) * NT + tile, 1)]
                    nc.vector.scalar_tensor_tensor(out=x[:, tile, :], in0=ps[:, 4 + c % 2, P * i:P * i + P], scalar=w,
                                                   in1=x[:, tile, :], op0=ALU.mult, op1=ALU.add).then_inc(self.combined, 1)

        norm_a = Norm("a", x, xn, [(loads[f"x{g}"], 16) for g in range(NG)], twice=tmp_tok)
        turn_a = Turn("a", norm_a, [(ln_sb[:, v, 0:1], ln_sb[:, v, 1:2], None, xs[v]) for v in range(3)], [6, 7, 6, 7],
                      scratch=[att[:, 0, :], att[:, 1, :]] +
                      [vb[1][:, 4 * i:4 * i + 4, :].rearrange("p t n -> p (t n)") for i in range(2)],
                      uses=(0, 1, 2, 3, 0, 1, 4, 5, 6, 7, 2, 3))
        attn_a = Attention("attn_a", SCALE_A, True, xs[0], xs[1], xs[2], xn, turn_a, loads["wa"], loads["woa"],
                           rows=B, last_bank=4)
        norm_m = Norm("m", xn, tmp_m, [(attn_a.y_added, 2 * NIT - 3 + g) for g in range(NG)])
        turn_m = Turn("m", norm_m, [(ln_sb[:, 3, 0:1], ln_sb[:, 3, 1:2], xT32, None)], [2, 3, 0, 1],
                      free={3: (attn_a.y_added, 2 * NIT)})
        mlp = Mlp(turn_m, attn_a)
        norm_f1 = Norm("f1", x, xn, [(mlp.x_ready, g + 1) for g in range(NG)])
        turn_f1 = Turn("f1", norm_f1, [(1.0, 0.0, None, xs[0])], [7, 6, 7, 6],
                       free={0: (attn_a.rec_ready, 8 * NIT), 1: (mlp.gelu, 2 * NG)})
        moe1 = Moe("moe1", turn_f1)
        norm_b = Norm("b", x, xn, [moe1.x_ready(g) for g in range(NG)])
        turn_b = Turn("b", norm_b, [(1.0, 0.0, None, xs[0])], [6, 7, 6, 7])
        attn_b = Attention("attn_b", SCALE_B, False, xs[0], xs[0], xs[0], x, turn_b, loads["wb"], loads["wob"],
                           rows=2 * B, last_bank=6)
        norm_f2 = Norm("f2", x, xn, [(attn_b.y_added, 2 * NIT - 3 + g) for g in range(NG)])
        turn_f2 = Turn("f2", norm_f2, [(1.0, 0.0, None, xs[0])], [5, 6, 5, 7],
                       free={0: (attn_b.probs, 2 * U * NIT), 1: (attn_b.o_copied, 2 * NIT)})
        moe2 = Moe("moe2", turn_f2)

        def nothing(*_):
            pass

        def act_for_v(e):
            attn_a.act_weights(e, (2,))
            turn_a.act(e, 0, 2)
            turn_a.act(e, 1, 2)

        def dve_for_v(e):
            turn_a.dve(e, 0, 2)
            turn_a.dve(e, 1, 2)
            attn_a.dve_weights(e, (2,))

        attn_a.between["act", ("K", 0)] = act_for_v
        attn_a.between["dve", ("T", 0)] = dve_for_v

        def act_expert_weights(e, ex):
            e.wait_ge(staged[ex % 3], 32 * (ex // 3 + 1))
            nc.scalar.activation(w1h[:, ex, :], stage[:, ex % 3, 0:HID], ACT.Copy, scale=WS).then_inc(w_hi, 1)
            nc.scalar.activation(w2h[:, ex, :], stage[:, ex % 3, HID:2 * HID], ACT.Copy, scale=WS).then_inc(w_hi, 1)

        def dve_expert_weights(e, ex):
            for i, (hi, lo) in enumerate(((w1h, w1l), (w2h, w2l))):
                e.wait_ge(w_hi, 2 * ex + i + 1)
                nc.vector.scalar_tensor_tensor(out=lo[:, ex, :], in0=stage[:, ex % 3, HID * i:HID * i + HID], scalar=WS,
                                               in1=hi[:, ex, :], op0=ALU.mult, op1=ALU.subtract).then_inc(w_lo, 1)

        def act_small_weights(e):
            e.wait_ge(loads["gate"], 16 * 2)
            e.wait_ge(loads["ffn"], 16 * 3)
            nc.scalar.activation(gwh[:], gw[:], ACT.Copy, scale=WS).then_inc(small_hi, 1)
            nc.scalar.activation(fb2h, fb2, ACT.Copy, scale=WS).then_inc(small_hi, 1)

        def dve_small_weights(e):
            e.wait_ge(small_hi, 2)
            nc.vector.scalar_tensor_tensor(out=gwl[:], in0=gw[:], scalar=WS, in1=gwh[:], op0=ALU.mult, op1=ALU.subtract)\
                .then_inc(small_lo, 1)
            nc.vector.tensor_scalar(fb2h, fb2h, ident[0:2, 1:2], None, ALU.mult).then_inc(small_hi, 1)
            e.wait_ge(small_hi, 3)
            nc.vector.scalar_tensor_tensor(out=fb2s, in0=fb2, scalar=WS, in1=fb2h, op0=ALU.mult, op1=ALU.subtract)\
                .then_inc(small_lo, 1)

        WEIGHT_STEP = {0: 0, 1: 1, 2: 2, 7: 3, 8: 4, 9: 5, 12: 6, 13: 7, 14: 8}
        for u, ex in WEIGHT_STEP.items():
            attn_a.beside["act", u] = lambda e, ex=ex: act_expert_weights(e, ex)
            attn_a.beside["dve", u] = lambda e, ex=ex: dve_expert_weights(e, ex)
        attn_a.beside["act", 15] = act_small_weights
        attn_a.beside["dve", 15] = dve_small_weights
        attn_a.beside["dve", 6] = mlp.dve_b2
        for attn, norm in ((attn_a, norm_m), (attn_b, norm_f2)):
            attn.beside["dve", 10] = lambda e, norm=norm: [norm.dve_stats(e, g) for g in range(2)]
            attn.beside["act", 11] = lambda e, norm=norm: [norm.act_root(e, g) for g in range(2)]
            attn.beside["dve", 11] = lambda e, norm=norm: [norm.dve_norm(e, g) for g in range(2)]

        def load_attention(e, k, w_sem, wo_sem):
            for i in range(3):
                e.dma_start(attn_a.raw_weights(i), t[f"w{k}"][i]).then_inc(w_sem, 16)
            e.dma_start(bqk[:], t[f"bqk{k}"]).then_inc(w_sem, 16)
            e.dma_start(bv[:], t[f"bv{k}"].partition_broadcast(P)).then_inc(w_sem, 16)
            e.dma_start(wo[:], t[f"wo{k}"].rearrange("(a r) n -> r a n", r=P)).then_inc(wo_sem, 16)
            e.dma_start(bo[:], t[f"bo{k}"].partition_broadcast(P)).then_inc(wo_sem, 16)

        def load_expert(e, ex):
            w1, w2 = (t["fw1"][ex - 1], t["fw2"][ex - 1]) if ex > 0 else (t["fws1"], t["fws2"])
            e.dma_start(stage[:, ex % 3, 0:HID], w1).then_inc(staged[ex % 3], 16)
            e.dma_start(stage[:, ex % 3, HID:2 * HID].rearrange("p (i n) -> p i n", i=HT),
                        w2.rearrange("(i p) n -> p i n", p=P)).then_inc(staged[ex % 3], 16)

        block = ctx.enter_context(nc.Block())

        @block.sync
        def _(sp):
            for g in range(NG):
                sp.dma_start(x[:, 4 * g:4 * g + 4, :],
                             t["x"].rearrange("b (t p) d -> p (b t) d", p=P)[:, 4 * g:4 * g + 4, :]).then_inc(loads[f"x{g}"], 16)
                if g == 1:
                    for dst, name in ((ident, "ident"), (ident16, "ident16"), (mfirst, "mfirst"), (iota, "iota"), (ln_sb, "ln_sb")):
                        sp.dma_start(dst[:], t[name]).then_inc(loads["const"], 16)
            load_attention(sp, "a", loads["wa"], loads["woa"])
            for b in range(B):
                sp.dma_start(heads[b][HD + 1:HD + 3, :, QB:KB + 1, :], t["mrows"]).then_inc(loads["mask"], 16)
            for ex in range(3):
                load_expert(sp, ex)
            sp.dma_start(gw[:], t["gw"]).then_inc(loads["gate"], 16)
            sp.dma_start(gb[:], t["gb"].partition_broadcast(P)).then_inc(loads["gate"], 16)
            sp.dma_start(fb1[:], t["fb1"]).then_inc(loads["ffn"], 16)
            sp.dma_start(mw1[:], t["mw1"]).then_inc(loads["mlp"], 16)
            sp.dma_start(mw2[:], t["mw2"].rearrange("(i p) n -> p i n", p=P)).then_inc(loads["mlp"], 16)
            sp.dma_start(mb1[:], t["mb1"]).then_inc(loads["mlp"], 16)
            sp.dma_start(mb2[:], t["mb2"].partition_broadcast(P)).then_inc(loads["mlp"], 16)
            attn_a.sp(sp)
            for r in range(2):
                sp.dma_start(fb2[r:r + 1, :], t["fb2"]).then_inc(loads["ffn"], 16)
            for ex in range(3, NE):
                sp.wait_ge(w_lo, 2 * (ex - 2))
                load_expert(sp, ex)
            sp.wait_ge(attn_a.y_added, Attention.Y_DONE)
            load_attention(sp, "b", loads["wb"], loads["wob"])
            attn_b.sp(sp)
            for g in range(NG):
                sp.wait_ge(*moe2.x_ready(g))
                sp.dma_start(out.rearrange("b (t p) d -> p (b t) d", p=P)[:, 4 * g:4 * g + 4, :],
                             x[:, 4 * g:4 * g + 4, :]).then_inc(stored, 16)
            sp.wait_ge(stored, 16 * NG)

        @block.gpsimd
        def _(pool):
            nc.gpsimd.memset(ones[:], 1.0).then_inc(const_ready, 1)
            pool.wait_ge(const_ready, 1)
            nc.gpsimd.memset(spare[:], 0.0).then_inc(const_ready, 1)
            pool.wait_ge(const_ready, 2)
            nc.gpsimd.memset(ones16[:], 1.0).then_inc(const_ready, 1)
            pool.wait_ge(const_ready, 3)
            for b in range(B):
                nc.gpsimd.memset(heads[b][HD:HD + 1, :, KB, :], 1.0).then_inc(rows_ready, 1)
                pool.wait_ge(rows_ready, b + 1)
            attn_a.pool(pool)
            pool.wait_ge(moe1.down, Moe.NK)
            for b in range(B):
                nc.gpsimd.memset(heads[b][HD:HD + 1, :, KB, :], 1.0).then_inc(rows_ready, 1)
                pool.wait_ge(rows_ready, B + b + 1)
            attn_b.pool(pool)

        @block.scalar
        def _(act):
            for g in (0, 1):
                norm_a.act_root(act, g)
            for g in (0, 1):
                norm_a.act_root2(act, g)
            act.wait_ge(loads["const"], 16 * 5)
            turn_a.act(act, 0, 0)
            turn_a.act(act, 1, 0)
            for g in (2, 3):
                norm_a.act_root(act, g)
            attn_a.act_weights(act, (0,))
            turn_a.act(act, 0, 1)
            turn_a.act(act, 1, 1)
            attn_a.act_weights(act, (1,))
            for g in (2, 3):
                norm_a.act_root2(act, g)
            attn_a.act(act)
            norm_m.act_root(act, 2)
            turn_m.act(act, 0)
            turn_m.act(act, 1)
            mlp.act(act, 0)
            mlp.act(act, 1)
            turn_m.act(act, 2)
            mlp.act(act, 2)
            norm_m.act_root(act, 3)
            norm_f1.act_root(act, 0)
            turn_m.act(act, 3)
            norm_f1.act_root(act, 1)
            turn_f1.act(act, 0)
            mlp.act(act, 3)
            turn_f1.act(act, 1)
            norm_f1.act_root(act, 2)
            norm_f1.act_root(act, 3)
            turn_f1.act(act, 2)
            act.wait_ge(loads["ffn"], 16 * 3)
            moe1.act_offsets(act, 0)
            moe1.act_chunk(act, 0, 0)
            turn_f1.act(act, 3)
            moe1.act_chunk(act, 0, 1)
            moe1.act_chunk(act, 0, 2)

            def after(c):
                if c >= 2:
                    norm_b.act_root(act, c - 2)

            moe1.act(act, lambda: attn_b.act_weights(act), after)
            turn_b.act(act, 0)
            turn_b.act(act, 1)
            norm_b.act_root(act, 2)
            norm_b.act_root(act, 3)
            attn_b.act(act)
            turn_f2.act(act, 0)
            turn_f2.act(act, 1)
            norm_f2.act_root(act, 2)
            act.wait_ge(attn_b.summed, 14 * NIT - 2)
            moe2.act_offsets(act, 0)
            moe2.act_chunk(act, 0, 0)
            turn_f2.act(act, 2)
            act.wait_ge(attn_b.summed, 14 * NIT)
            moe2.act_chunk(act, 0, 1)
            norm_f2.act_root(act, 3)
            moe2.act_chunk(act, 0, 2)
            turn_f2.act(act, 3)
            moe2.act(act, nothing, nothing)

        @block.vector
        def _(dve):
            for g in (0, 1):
                norm_a.dve_stats(dve, g)
            for g in (0, 1):
                norm_a.dve_norm(dve, g)
                norm_a.dve_stats2(dve, g)
            for g in (0, 1):
                norm_a.dve_norm2(dve, g)
            for g in (2, 3):
                norm_a.dve_stats(dve, g)
            turn_a.dve(dve, 0, 0)
            turn_a.dve(dve, 1, 0)
            attn_a.dve_weights(dve, (0,))
            for g in (2, 3):
                norm_a.dve_norm(dve, g)
                norm_a.dve_stats2(dve, g)
            turn_a.dve(dve, 0, 1)
            turn_a.dve(dve, 1, 1)
            attn_a.dve_weights(dve, (1,))
            for g in (2, 3):
                norm_a.dve_norm2(dve, g)
            attn_a.dve(dve)
            norm_m.dve_stats(dve, 2)
            norm_m.dve_norm(dve, 2)
            attn_a.dve_last_normalise(dve)
            for g in range(3):
                mlp.dve_h(dve, g)
            attn_a.dve_last_y(dve)
            norm_m.dve_stats(dve, 3)
            mlp.dve_h(dve, 3)
            mlp.dve_down(dve, 0)
            norm_f1.dve_stats(dve, 0)
            norm_m.dve_norm(dve, 3)
            norm_f1.dve_norm(dve, 0)
            mlp.dve_down(dve, 1)
            norm_f1.dve_stats(dve, 1)
            norm_f1.dve_norm(dve, 1)
            turn_f1.dve(dve, 0)
            for g in (2, 3):
                mlp.dve_down(dve, g)
                norm_f1.dve_stats(dve, g)
            turn_f1.dve(dve, 1)
            norm_f1.dve_norm(dve, 2)
            norm_f1.dve_norm(dve, 3)
            turn_f1.dve(dve, 2)
            moe1.dve_split(dve, 0, 0, True)
            turn_f1.dve(dve, 3)
            moe1.dve_split(dve, 0, 1, False)
            moe1.dve_combine(dve, 0, 0)
            moe1.dve_split(dve, 0, 2, False)

            def after(c):
                if c < 3:
                    norm_b.dve_stats(dve, c)
                    if c >= 1:
                        norm_b.dve_norm(dve, c - 1)

            moe1.dve(dve, lambda: attn_b.dve_weights(dve), after)
            turn_b.dve(dve, 0)
            turn_b.dve(dve, 1)
            norm_b.dve_stats(dve, 3)
            norm_b.dve_norm(dve, 2)
            norm_b.dve_norm(dve, 3)
            attn_b.dve(dve)
            norm_f2.dve_stats(dve, 2)
            turn_f2.dve(dve, 0)
            turn_f2.dve(dve, 1)
            norm_f2.dve_norm(dve, 2)
            attn_b.dve_last_normalise(dve)
            moe2.dve_split(dve, 0, 0, True)
            turn_f2.dve(dve, 2)
            attn_b.dve_last_y(dve)
            norm_f2.dve_stats(dve, 3)
            moe2.dve_split(dve, 0, 1, False)
            norm_f2.dve_norm(dve, 3)
            moe2.dve_combine(dve, 0, 0)
            moe2.dve_split(dve, 0, 2, False)
            turn_f2.dve(dve, 3)
            moe2.dve(dve, nothing, nothing)

        @block.tensor
        def _(pe):
            pe.wait_ge(loads["const"], 16 * 5)
            pe.wait_ge(const_ready, 3)
            turn_a.pe(pe, 0)
            turn_a.pe(pe, 1)
            attn_a.pe(pe)
            turn_m.pe(pe, 0)
            turn_m.pe(pe, 1)
            attn_a.pe_last_sums(pe)
            mlp.pe_up(pe, 0)
            mlp.pe_up(pe, 1)
            turn_m.pe(pe, 2)
            attn_a.pe_last_y(pe)
            mlp.pe_up(pe, 2)
            mlp.pe_down(pe, 0)
            mlp.pe_down(pe, 1)
            turn_m.pe(pe, 3)
            mlp.pe_down(pe, 2)
            turn_f1.pe(pe, 0)
            mlp.pe_up(pe, 3)
            mlp.pe_down(pe, 3)
            turn_f1.pe(pe, 1)
            pe.wait_ge(w_lo, 2 * NE)
            pe.wait_ge(turn_f1.lo, 1)
            pe.wait_ge(mlp.x_ready, NG)
            moe1.pe_up(pe, 0, 0, True)
            turn_f1.pe(pe, 2)
            turn_f1.pe(pe, 3)
            pe.wait_ge(turn_f1.lo, 2)
            moe1.pe_up(pe, 0, 1, False)
            moe1.pe_down(pe, 0, 0)
            pe.wait_ge(turn_f1.lo, 3)
            moe1.pe_up(pe, 0, 2, False)
            moe1.pe_down(pe, 0, 1)

            def after(c):
                if c >= 2:
                    turn_b.pe(pe, c - 2)

            moe1.pe(pe, after)
            attn_b.pe(pe)
            turn_f2.pe(pe, 0)
            turn_f2.pe(pe, 1)
            pe.wait_ge(turn_f2.lo, 1)
            pe.wait_ge(attn_b.y_added, 2 * NIT - 1)
            moe2.pe_up(pe, 0, 0, True)
            attn_b.pe_last_sums(pe)
            turn_f2.pe(pe, 2)
            pe.wait_ge(turn_f2.lo, 2)
            moe2.pe_up(pe, 0, 1, False)
            attn_b.pe_last_y(pe)
            moe2.pe_down(pe, 0, 0)
            pe.wait_ge(turn_f2.lo, 3)
            moe2.pe_up(pe, 0, 2, False)
            moe2.pe_down(pe, 0, 1)
            turn_f2.pe(pe, 3)
            moe2.pe(pe, nothing)


def kernel(**inputs):
    import numpy as np
    import concourse.bacc as _bacc
    from concourse import mybir as _mybir
    from concourse.bass_utils import run_bass_kernel_spmd as _run

    a = {k.removeprefix("L0_"): np.asarray(v) for k, v in inputs.items()}

    def cols(v, *shape):
        return np.ascontiguousarray(np.moveaxis(v.reshape(*shape, 128), -1, 0))

    mask = MASK * float(D) ** 0.5
    mrows = np.zeros((2, 2, 2, S), np.float16)
    mrows[:, :, 0, 0] = 1.0
    mrows[0, :, 1, S - 1] = mask
    mrows[1, :, 1, S - 1] = mask - float(np.float16(mask))
    first = np.zeros((1, 128), np.float16)
    first[0, 0] = mask
    arrays = {
        "x": a["attn_a_x"],
        "ident": np.eye(128, dtype=np.float32), "ident16": np.eye(128, dtype=np.float16),
        "mrows": mrows, "mfirst": first, "iota": np.tile(np.arange(E, dtype=np.float32), (128, 1)),
        "ln_sb": np.stack([np.stack([a[f"attn_a_ln{k}_{p}"] for p in "sb"], -1) for k in "qkvm"], 1),
        "wa": np.stack([a[f"attn_a_W{k}"] for k in "qkv"]),
        "bqka": np.stack([cols(a[f"attn_a_b{k}"], 8) for k in "qk"], 1),
        "bva": a["attn_a_bv"], "woa": a["attn_a_Wo"], "boa": a["attn_a_bo"],
        "wb": np.stack([a[f"attn_b_W_{k}"].transpose(2, 0, 1).reshape(128, 1024) for k in "QKV"]),
        "bqkb": np.stack([cols(a[f"attn_b_b_{k}"], 8) for k in "QK"], 1),
        "bvb": a["attn_b_b_V"].reshape(-1), "wob": a["attn_b_W_O"].transpose(0, 2, 1).reshape(1024, 128),
        "bob": a["attn_b_b_O"],
        "mw1": a["attn_a_W1"], "mw2": a["attn_a_W2"], "mb1": cols(a["attn_a_b1"], 2), "mb2": a["attn_a_b2"],
        "gw": a["ffn_gate_w"], "gb": a["ffn_gate_b"],
        "fw1": a["ffn_w1"], "fws1": a["ffn_ws1"], "fw2": a["ffn_w2"], "fws2": a["ffn_ws2"],
        "fb1": np.concatenate([cols(a["ffn_bs1"], 1, 4), cols(a["ffn_b1"], 8, 4)], 1),
        "fb2": np.concatenate([a["ffn_bs2"][None], a["ffn_b2"]]).reshape(1, -1),
    }
    nc = _bacc.Bacc("TRN2", target_bir_lowering=False, num_devices=1)
    feeds, aps = {}, {}
    for name, v in arrays.items():
        v = np.ascontiguousarray(v)
        feeds[f"in_{name}"] = v
        aps[name] = nc.dram_tensor(f"in_{name}", v.shape, _mybir.dt.from_np(v.dtype), kind="ExternalInput").ap()
    out = nc.dram_tensor("out_0", (B, S, D), _mybir.dt.float32, kind="ExternalOutput").ap()
    build(nc, aps, out)
    r = _run(nc, [feeds], core_ids=[0])
    return r.results[0]["out_0"]
```
